# Optimizing a Trainium2 kernel written in Bass

```python
import numpy as np
import jax
import jax.numpy as jnp

def _softmax(x, axis=-1):
    return jax.nn.softmax(x, axis=axis)

def _gelu(x):
    return jax.nn.gelu(x, approximate=True)

def _silu(x):
    return jax.nn.silu(x)

def _sigmoid(x):
    return jax.nn.sigmoid(x)

def _layernorm(x, axis=-1, eps=1e-05):
    m = jnp.mean(x, axis=axis, keepdims=True)
    v = jnp.var(x, axis=axis, keepdims=True)
    return (x - m) / jnp.sqrt(v + eps)

def _scatter_add(tgt, idx, src, axis=0):
    return tgt.at[idx].add(src)

def _segment_sum(src, seg, n):
    return jax.ops.segment_sum(src, seg, n)
kernel_name = 'mk_gps_d2_gnn_r8_f25633'

def setup_inputs(seed: int=0):
    np.random.seed(seed)
    _w = jnp.asarray

    def _rec_inputs():
        import jax
        import jax.numpy as jnp
        _gk = jax.random.key(seed)
        x = -0.0002117 + 1 * jax.random.normal(jax.random.fold_in(_gk, 1), (6250, 256), jnp.float32)
        _s = jax.random.randint(jax.random.fold_in(_gk, 2), (100000,), 0, 6250, jnp.int32)
        _d = jax.random.randint(jax.random.fold_in(_gk, 3), (100000,), 0, 6250, jnp.int32)
        _loop = jnp.arange(6250, dtype=jnp.int32)
        src = jnp.concatenate([_s, _d, _loop])
        dst = jnp.concatenate([_d, _s, _loop])
        _o = jnp.argsort(dst, stable=True)
        src = src[_o]
        dst = dst[_o]
        edge_weight = -0.00278149 + 0.998712 * jax.random.normal(jax.random.fold_in(_gk, 13), (206250,), jnp.float32)
        return (x, src, dst, edge_weight)
    x, src, dst, edge_weight = _rec_inputs()

    def _L0_gnn_setup():
        import jax, jax.numpy as jnp
        import numpy as np
        N = 12500
        E = 200000
        IN_FEATS = 256
        OUT_FEATS = 256
        MAXK = 32

        def _maxk(x, k):
            _, idx = jax.lax.top_k(x, k)
            rows = jnp.arange(x.shape[0])[:, None]
            mask = jnp.zeros_like(x).at[rows, idx].set(1.0)
            return x * mask
        key = jax.random.key(seed)
        k1, k2, k3, k4, k5 = jax.random.split(key, 5)
        feat = jax.random.normal(k1, (N, IN_FEATS), dtype=jnp.float32)
        W_self = jax.random.normal(k2, (IN_FEATS, OUT_FEATS), dtype=jnp.float32) * (1.0 / np.sqrt(IN_FEATS))
        W_neigh = jax.random.normal(k3, (IN_FEATS, OUT_FEATS), dtype=jnp.float32) * (1.0 / np.sqrt(IN_FEATS))
        src = jax.random.randint(k4, (E,), 0, N, dtype=jnp.int64)
        dst = jax.random.randint(k5, (E,), 0, N, dtype=jnp.int64)
        return {'feat': feat, 'W_self': W_self, 'W_neigh': W_neigh, 'src': src, 'dst': dst}
    _L0_gnn_all = _L0_gnn_setup()
    _L0_gnn_in = {k: v for k, v in _L0_gnn_all.items() if k in ('W_self', 'W_neigh')}
    del _L0_gnn_all

    def _L0_mix_setup():
        import jax, jax.numpy as jnp
        import numpy as np
        HEADS = 8
        DIM_HEAD = 64
        EPS = 1e-05

        def _inst_norm_lastdim(t):
            mu = jnp.mean(t, axis=-1, keepdims=True)
            var = jnp.mean(jnp.square(t - mu), axis=-1, keepdims=True)
            return (t - mu) * jax.lax.rsqrt(var + EPS)
        key = jax.random.key(seed)
        k1, k2, k3, k4 = jax.random.split(key, 4)
        b, n, dim = (4, 1024, 256)
        inner = HEADS * DIM_HEAD
        x = jax.random.normal(k1, (b, n, dim), dtype=jnp.float32)
        Wqkv = jax.random.normal(k2, (3 * inner, dim), dtype=jnp.float32) * (1.0 / np.sqrt(dim))
        Wout = jax.random.normal(k3, (dim, inner), dtype=jnp.float32) * (1.0 / np.sqrt(inner))
        bout = jax.random.normal(k4, (dim,), dtype=jnp.float32) * 0.01
        return {'x': x, 'Wqkv': Wqkv, 'Wout': Wout, 'bout': bout}
    _L0_mix_all = _L0_mix_setup()
    _L0_mix_in = {k: v for k, v in _L0_mix_all.items() if k in ('Wqkv', 'Wout', 'bout')}
    del _L0_mix_all

    def _L0_ffn_setup():
        import jax, jax.numpy as jnp
        import numpy as np
        B, S, D = (8, 512, 256)
        H = 4 * D
        CAPACITY = 0.5
        key = jax.random.key(seed)
        ks = jax.random.split(key, 6)
        x = jax.random.normal(ks[0], (B, S, D), dtype=jnp.float32)
        attention_mask = jnp.zeros((B, 1, 1, S), dtype=jnp.float32)
        wr = jax.random.normal(ks[1], (D, 1), dtype=jnp.float32) * 0.02
        br = jnp.zeros((1,), dtype=jnp.float32)
        w1 = jax.random.normal(ks[2], (D, H), dtype=jnp.float32) * 0.02
        b1 = jnp.zeros((H,), dtype=jnp.float32)
        w2 = jax.random.normal(ks[3], (H, D), dtype=jnp.float32) * 0.02
        b2 = jnp.zeros((D,), dtype=jnp.float32)
        return {'x': x, 'attention_mask': attention_mask, 'wr': wr, 'br': br, 'w1': w1, 'b1': b1, 'w2': w2, 'b2': b2}
    _L0_ffn_all = _L0_ffn_setup()
    _L0_ffn_in = {k: v for k, v in _L0_ffn_all.items() if k in ('attention_mask', 'wr', 'br', 'w1', 'b1', 'w2', 'b2')}
    del _L0_ffn_all

    def _L1_gnn_setup():
        import jax, jax.numpy as jnp
        import numpy as np
        N = 1250
        E = 40000
        D = 256
        EPS = 1e-05

        def layer_norm(x, g, b):
            mu = jnp.mean(x, axis=-1, keepdims=True)
            var = jnp.mean(jnp.square(x - mu), axis=-1, keepdims=True)
            return (x - mu) * jax.lax.rsqrt(var + EPS) * g + b

        def linear(x, w, b):
            return x @ w + b
        key = jax.random.key(seed)
        ks = jax.random.split(key, 20)
        s = 1.0 / np.sqrt(D)
        inp = {'x': jax.random.normal(ks[0], (N, D), jnp.float32), 'edge_index': jax.random.randint(ks[1], (2, E), 0, N, jnp.int64), 'edge_weight': jax.random.normal(ks[2], (E,), jnp.float32), 'wq': jax.random.normal(ks[3], (D, D), jnp.float32) * s, 'bq': jnp.zeros((D,), jnp.float32), 'wk': jax.random.normal(ks[4], (D, D), jnp.float32) * s, 'bk': jnp.zeros((D,), jnp.float32), 'wv': jax.random.normal(ks[5], (D, D), jnp.float32) * s, 'bv': jnp.zeros((D,), jnp.float32), 'ws': jax.random.normal(ks[6], (D, D), jnp.float32) * s, 'bs': jnp.zeros((D,), jnp.float32), 'we': jax.random.normal(ks[7], (1, 1), jnp.float32), 'be': jnp.zeros((1,), jnp.float32), 'g1': jnp.ones((D,), jnp.float32), 'b1': jnp.zeros((D,), jnp.float32), 'g2': jnp.ones((D,), jnp.float32), 'b2': jnp.zeros((D,), jnp.float32), 'w_ff1': jax.random.normal(ks[8], (D, 2 * D), jnp.float32) * s, 'b_ff1': jnp.zeros((2 * D,), jnp.float32), 'w_ff2': jax.random.normal(ks[9], (2 * D, D), jnp.float32) * (1.0 / np.sqrt(2 * D)), 'b_ff2': jnp.zeros((D,), jnp.float32)}
        return inp
    _L1_gnn_all = _L1_gnn_setup()
    _L1_gnn_in = {k: v for k, v in _L1_gnn_all.items() if k in ('wq', 'bq', 'wk', 'bk', 'wv', 'bv', 'ws', 'bs', 'we', 'be', 'g1', 'b1', 'g2', 'b2', 'w_ff1', 'b_ff1', 'w_ff2', 'b_ff2')}
    del _L1_gnn_all

    def _L1_mix_setup():
        import jax, jax.numpy as jnp
        import numpy as np
        DIM = 256
        HEADS = 4
        DIM_HEAD = 32
        NUM_MEM = 4
        HIDDEN = HEADS * DIM_HEAD
        SCALE = DIM_HEAD ** (-0.5)

        def rmsnorm(x, g):
            n = jnp.linalg.norm(x, axis=-1, keepdims=True)
            return x / jnp.maximum(n, 1e-12) * g * x.shape[-1] ** 0.5
        key = jax.random.key(seed)
        ks = jax.random.split(key, 8)
        B, N = (4, 2048)
        return {'x': jax.random.normal(ks[0], (B, N, DIM), jnp.float32), 't': jax.random.normal(ks[1], (B,), jnp.float32), 'w_qkv': jax.random.normal(ks[2], (DIM, 3 * HIDDEN), jnp.float32) * 0.02, 'mem_kv': jax.random.normal(ks[3], (2, HEADS, DIM_HEAD, NUM_MEM), jnp.float32), 'w_out': jax.random.normal(ks[4], (HIDDEN, DIM), jnp.float32) * 0.02, 'b_out': jnp.zeros((DIM,), jnp.float32), 'g_out': jnp.ones((DIM,), jnp.float32), 'g_pre': jnp.ones((DIM,), jnp.float32)}
    _L1_mix_all = _L1_mix_setup()
    _L1_mix_in = {k: v for k, v in _L1_mix_all.items() if k in ('t', 'w_qkv', 'mem_kv', 'w_out', 'b_out', 'g_out', 'g_pre')}
    del _L1_mix_all

    def _L1_ffn_setup():
        import jax, jax.numpy as jnp
        import numpy as np
        BN_EPS = 0.001

        def _bn(h, g, b, m, v):
            return g * (h - m) * jax.lax.rsqrt(v + BN_EPS) + b
        key = jax.random.key(seed)
        ks = jax.random.split(key, 8)
        B, F, Df = (256, 64, 256)
        E, H, D = (8, 256, 256)
        s1 = 1.0 / np.sqrt(Df)
        s2 = 1.0 / np.sqrt(H)
        return {'x': jax.random.normal(ks[0], (B, F, Df), jnp.float32), 'Wr': jax.random.normal(ks[1], (Df, E), jnp.float32) * s1, 'br': jnp.zeros((E,), jnp.float32), 'W1': jax.random.normal(ks[2], (E, Df, H), jnp.float32) * s1, 'b1': jnp.zeros((E, H), jnp.float32), 'g1': jnp.ones((E, H), jnp.float32), 'be1': jnp.zeros((E, H), jnp.float32), 'm1': jnp.zeros((E, H), jnp.float32), 'v1': jnp.ones((E, H), jnp.float32), 'W2': jax.random.normal(ks[3], (E, H, H), jnp.float32) * s2, 'b2': jnp.zeros((E, H), jnp.float32), 'g2': jnp.ones((E, H), jnp.float32), 'be2': jnp.zeros((E, H), jnp.float32), 'm2': jnp.zeros((E, H), jnp.float32), 'v2': jnp.ones((E, H), jnp.float32), 'Wo': jax.random.normal(ks[4], (E, H, D), jnp.float32) * s2, 'bo': jnp.zeros((E, D), jnp.float32)}
    _L1_ffn_all = _L1_ffn_setup()
    _L1_ffn_in = {k: v for k, v in _L1_ffn_all.items() if k in ('Wr', 'br', 'W1', 'b1', 'g1', 'be1', 'm1', 'v1', 'W2', 'b2', 'g2', 'be2', 'm2', 'v2', 'Wo', 'bo')}
    del _L1_ffn_all
    return {'x': x, 'src': src, 'dst': dst, 'edge_weight': edge_weight, 'L0_gnn_W_self': _L0_gnn_in['W_self'], 'L0_gnn_W_neigh': _L0_gnn_in['W_neigh'], 'L0_mix_Wqkv': _L0_mix_in['Wqkv'], 'L0_mix_Wout': _L0_mix_in['Wout'], 'L0_mix_bout': _L0_mix_in['bout'], 'L0_ffn_attention_mask': _L0_ffn_in['attention_mask'], 'L0_ffn_wr': _L0_ffn_in['wr'], 'L0_ffn_br': _L0_ffn_in['br'], 'L0_ffn_w1': _L0_ffn_in['w1'], 'L0_ffn_b1': _L0_ffn_in['b1'], 'L0_ffn_w2': _L0_ffn_in['w2'], 'L0_ffn_b2': _L0_ffn_in['b2'], 'L1_gnn_wq': _L1_gnn_in['wq'], 'L1_gnn_bq': _L1_gnn_in['bq'], 'L1_gnn_wk': _L1_gnn_in['wk'], 'L1_gnn_bk': _L1_gnn_in['bk'], 'L1_gnn_wv': _L1_gnn_in['wv'], 'L1_gnn_bv': _L1_gnn_in['bv'], 'L1_gnn_ws': _L1_gnn_in['ws'], 'L1_gnn_bs': _L1_gnn_in['bs'], 'L1_gnn_we': _L1_gnn_in['we'], 'L1_gnn_be': _L1_gnn_in['be'], 'L1_gnn_g1': _L1_gnn_in['g1'], 'L1_gnn_b1': _L1_gnn_in['b1'], 'L1_gnn_g2': _L1_gnn_in['g2'], 'L1_gnn_b2': _L1_gnn_in['b2'], 'L1_gnn_w_ff1': _L1_gnn_in['w_ff1'], 'L1_gnn_b_ff1': _L1_gnn_in['b_ff1'], 'L1_gnn_w_ff2': _L1_gnn_in['w_ff2'], 'L1_gnn_b_ff2': _L1_gnn_in['b_ff2'], 'L1_mix_t': _L1_mix_in['t'], 'L1_mix_w_qkv': _L1_mix_in['w_qkv'], 'L1_mix_mem_kv': _L1_mix_in['mem_kv'], 'L1_mix_w_out': _L1_mix_in['w_out'], 'L1_mix_b_out': _L1_mix_in['b_out'], 'L1_mix_g_out': _L1_mix_in['g_out'], 'L1_mix_g_pre': _L1_mix_in['g_pre'], 'L1_ffn_Wr': _L1_ffn_in['Wr'], 'L1_ffn_br': _L1_ffn_in['br'], 'L1_ffn_W1': _L1_ffn_in['W1'], 'L1_ffn_b1': _L1_ffn_in['b1'], 'L1_ffn_g1': _L1_ffn_in['g1'], 'L1_ffn_be1': _L1_ffn_in['be1'], 'L1_ffn_m1': _L1_ffn_in['m1'], 'L1_ffn_v1': _L1_ffn_in['v1'], 'L1_ffn_W2': _L1_ffn_in['W2'], 'L1_ffn_b2': _L1_ffn_in['b2'], 'L1_ffn_g2': _L1_ffn_in['g2'], 'L1_ffn_be2': _L1_ffn_in['be2'], 'L1_ffn_m2': _L1_ffn_in['m2'], 'L1_ffn_v2': _L1_ffn_in['v2'], 'L1_ffn_Wo': _L1_ffn_in['Wo'], 'L1_ffn_bo': _L1_ffn_in['bo']}

def reference(x, src, dst, edge_weight, L0_gnn_W_self, L0_gnn_W_neigh, L0_mix_Wqkv, L0_mix_Wout, L0_mix_bout, L0_ffn_attention_mask, L0_ffn_wr, L0_ffn_br, L0_ffn_w1, L0_ffn_b1, L0_ffn_w2, L0_ffn_b2, L1_gnn_wq, L1_gnn_bq, L1_gnn_wk, L1_gnn_bk, L1_gnn_wv, L1_gnn_bv, L1_gnn_ws, L1_gnn_bs, L1_gnn_we, L1_gnn_be, L1_gnn_g1, L1_gnn_b1, L1_gnn_g2, L1_gnn_b2, L1_gnn_w_ff1, L1_gnn_b_ff1, L1_gnn_w_ff2, L1_gnn_b_ff2, L1_mix_t, L1_mix_w_qkv, L1_mix_mem_kv, L1_mix_w_out, L1_mix_b_out, L1_mix_g_out, L1_mix_g_pre, L1_ffn_Wr, L1_ffn_br, L1_ffn_W1, L1_ffn_b1, L1_ffn_g1, L1_ffn_be1, L1_ffn_m1, L1_ffn_v1, L1_ffn_W2, L1_ffn_b2, L1_ffn_g2, L1_ffn_be2, L1_ffn_m2, L1_ffn_v2, L1_ffn_Wo, L1_ffn_bo):
    import jax
    import jax.numpy as jnp

    def _L0_gnn_ref(feat, W_self, W_neigh, src, dst):
        import jax, jax.numpy as jnp
        import numpy as np
        N = 12500
        E = 200000
        IN_FEATS = 256
        OUT_FEATS = 256
        MAXK = 32

        def _maxk(x, k):
            _, idx = jax.lax.top_k(x, k)
            rows = jnp.arange(x.shape[0])[:, None]
            mask = jnp.zeros_like(x).at[rows, idx].set(1.0)
            return x * mask
        n = feat.shape[0]
        h_self = feat @ W_self
        h_neigh = feat @ W_neigh
        h_sparse = _maxk(h_neigh, MAXK)
        msg = h_sparse[src]
        summed = jax.ops.segment_sum(msg, dst, num_segments=n)
        deg = jax.ops.segment_sum(jnp.ones((src.shape[0],), dtype=feat.dtype), dst, num_segments=n)
        neigh = summed / jnp.maximum(deg, 1.0)[:, None]
        return h_self + neigh

    def _L0_mix_ref(x, Wqkv, Wout, bout):
        import jax, jax.numpy as jnp
        import numpy as np
        HEADS = 8
        DIM_HEAD = 64
        EPS = 1e-05

        def _inst_norm_lastdim(t):
            mu = jnp.mean(t, axis=-1, keepdims=True)
            var = jnp.mean(jnp.square(t - mu), axis=-1, keepdims=True)
            return (t - mu) * jax.lax.rsqrt(var + EPS)
        b, n, dim = x.shape
        qkv = jnp.einsum('bnc,fc->bnf', x, Wqkv)
        q, k, v = jnp.split(qkv, 3, axis=-1)

        def to_heads(t):
            return t.reshape(b, n, HEADS, DIM_HEAD).transpose(0, 2, 1, 3)
        q, k, v = (to_heads(q), to_heads(k), to_heads(v))
        k = _inst_norm_lastdim(k)
        v = _inst_norm_lastdim(v)
        dots = jnp.einsum('bhnd,bhne->bhde', k, v)
        out = jnp.einsum('bhnd,bhde->bhne', q, dots) / n
        out = out.transpose(0, 2, 1, 3).reshape(b, n, HEADS * DIM_HEAD)
        return jnp.einsum('bnf,cf->bnc', out, Wout) + bout

    def _L0_ffn_ref(x, attention_mask, wr, br, w1, b1, w2, b2):
        import jax, jax.numpy as jnp
        import numpy as np
        B, S, D = (8, 512, 256)
        H = 4 * D
        CAPACITY = 0.5
        b, s, d = x.shape
        weights = (jnp.einsum('bsd,do->bso', x, wr) + br)[..., 0]
        k = max(1, int(CAPACITY * s))
        kk = k - 1 if k > 1 else 1
        _, idx = jax.lax.top_k(weights, k)
        sel_idx = idx[:, :kk]
        sel = jnp.take_along_axis(x, sel_idx[:, :, None], axis=1)
        h = jax.nn.gelu(jnp.einsum('bkd,dh->bkh', sel, w1) + b1)
        y = jnp.einsum('bkh,hd->bkd', h, w2) + b2
        w_sel = jnp.take_along_axis(weights, sel_idx, axis=1)
        y = y * w_sel[..., None]
        batch_idx = jnp.arange(b)[:, None]
        processed = jnp.zeros_like(x).at[batch_idx, sel_idx].set(y)
        return processed + x

    def _L1_gnn_ref(x, edge_index, edge_weight, wq, bq, wk, bk, wv, bv, ws, bs, we, be, g1, b1, g2, b2, w_ff1, b_ff1, w_ff2, b_ff2):
        import jax, jax.numpy as jnp
        import numpy as np
        N = 1250
        E = 40000
        D = 256
        EPS = 1e-05

        def layer_norm(x, g, b):
            mu = jnp.mean(x, axis=-1, keepdims=True)
            var = jnp.mean(jnp.square(x - mu), axis=-1, keepdims=True)
            return (x - mu) * jax.lax.rsqrt(var + EPS) * g + b

        def linear(x, w, b):
            return x @ w + b
        n = x.shape[0]
        scale = x.shape[-1] ** (-0.5)
        q = linear(x, wq, bq)
        k = linear(x, wk, bk)
        v = linear(x, wv, bv)
        src, dst = (edge_index[0], edge_index[1])
        scores = jnp.sum(q[dst] * k[src], axis=-1) * scale
        scores = scores + (edge_weight[:, None] @ we + be)[:, 0]
        seg_max = jax.ops.segment_max(scores, dst, num_segments=n)
        exp_s = jnp.exp(scores - seg_max[dst])
        denom = jax.ops.segment_sum(exp_s, dst, num_segments=n)
        attn = exp_s / jnp.maximum(denom[dst], 1e-12)
        message = v[src] * attn[:, None]
        out = jax.ops.segment_sum(message, dst, num_segments=n)
        x = layer_norm(x + out + linear(x, ws, bs), g1, b1)
        ffn = linear(jax.nn.gelu(linear(x, w_ff1, b_ff1)), w_ff2, b_ff2)
        x = layer_norm(x + ffn, g2, b2)
        return x

    def _L1_mix_ref(x, t, w_qkv, mem_kv, w_out, b_out, g_out, g_pre):
        import jax, jax.numpy as jnp
        import numpy as np
        DIM = 256
        HEADS = 4
        DIM_HEAD = 32
        NUM_MEM = 4
        HIDDEN = HEADS * DIM_HEAD
        SCALE = DIM_HEAD ** (-0.5)

        def rmsnorm(x, g):
            n = jnp.linalg.norm(x, axis=-1, keepdims=True)
            return x / jnp.maximum(n, 1e-12) * g * x.shape[-1] ** 0.5
        b, n, c = x.shape
        xn = rmsnorm(x, g_pre)
        qkv = xn @ w_qkv
        q, k, v = jnp.split(qkv, 3, axis=-1)

        def to_heads(z):
            return z.reshape(b, n, HEADS, DIM_HEAD).transpose(0, 2, 3, 1)
        q, k, v = map(to_heads, (q, k, v))
        mk = jnp.broadcast_to(mem_kv[0], (b, HEADS, DIM_HEAD, NUM_MEM))
        mv = jnp.broadcast_to(mem_kv[1], (b, HEADS, DIM_HEAD, NUM_MEM))
        k = jnp.concatenate([mk, k], axis=-1)
        v = jnp.concatenate([mv, v], axis=-1)
        q = jax.nn.softmax(q, axis=-2) * SCALE
        k = jax.nn.softmax(k, axis=-1)
        context = jnp.einsum('bhdn,bhen->bhde', k, v)
        out = jnp.einsum('bhde,bhdn->bhen', context, q)
        out = out.transpose(0, 3, 1, 2).reshape(b, n, HIDDEN)
        out = rmsnorm(out @ w_out + b_out, g_out)
        return out + x

    def _L1_ffn_ref(x, Wr, br, W1, b1, g1, be1, m1, v1, W2, b2, g2, be2, m2, v2, Wo, bo):
        import jax, jax.numpy as jnp
        import numpy as np
        BN_EPS = 0.001

        def _bn(h, g, b, m, v):
            return g * (h - m) * jax.lax.rsqrt(v + BN_EPS) + b
        feat = jnp.mean(x, axis=0)
        w = jax.nn.softmax(feat @ Wr + br, axis=-1)
        h = jnp.einsum('bfd,edh->bfeh', x, W1) + b1
        h = jax.nn.relu(_bn(h, g1, be1, m1, v1))
        h = jnp.einsum('bfeh,ehk->bfek', h, W2) + b2
        h = jax.nn.relu(_bn(h, g2, be2, m2, v2))
        y = jnp.einsum('bfeh,ehd->bfed', h, Wo) + bo
        return jnp.einsum('bfed,fe->bfd', y, w)
    edge_index = jnp.stack([src, dst])
    xn = _layernorm(x, axis=-1)
    x = x + _L0_gnn_ref(xn, L0_gnn_W_self, L0_gnn_W_neigh, src, dst) + _L0_mix_ref(xn[None], L0_mix_Wqkv, L0_mix_Wout, L0_mix_bout)[0]
    x = x + _L0_ffn_ref(_layernorm(x, axis=-1)[None], L0_ffn_attention_mask, L0_ffn_wr, L0_ffn_br, L0_ffn_w1, L0_ffn_b1, L0_ffn_w2, L0_ffn_b2)[0]
    xn = _layernorm(x, axis=-1)
    x = x + _L1_gnn_ref(xn, edge_index, edge_weight, L1_gnn_wq, L1_gnn_bq, L1_gnn_wk, L1_gnn_bk, L1_gnn_wv, L1_gnn_bv, L1_gnn_ws, L1_gnn_bs, L1_gnn_we, L1_gnn_be, L1_gnn_g1, L1_gnn_b1, L1_gnn_g2, L1_gnn_b2, L1_gnn_w_ff1, L1_gnn_b_ff1, L1_gnn_w_ff2, L1_gnn_b_ff2) + _L1_mix_ref(xn[None], L1_mix_t, L1_mix_w_qkv, L1_mix_mem_kv, L1_mix_w_out, L1_mix_b_out, L1_mix_g_out, L1_mix_g_pre)[0]
    x = x + _L1_ffn_ref(_layernorm(x, axis=-1)[None], L1_ffn_Wr, L1_ffn_br, L1_ffn_W1, L1_ffn_b1, L1_ffn_g1, L1_ffn_be1, L1_ffn_m1, L1_ffn_v1, L1_ffn_W2, L1_ffn_b2, L1_ffn_g2, L1_ffn_be2, L1_ffn_m2, L1_ffn_v2, L1_ffn_Wo, L1_ffn_bo)[0]
    return x

_drawn_inputs = setup_inputs


def setup_inputs(seed=0):
    import zlib

    import numpy as np

    out = dict(_drawn_inputs(seed))
    spreads = {'L0_ffn_b1': (0.0, 0.8),
     'L0_ffn_b2': (0.0, 0.799),
     'L1_gnn_bq': (0.0, 2.0),
     'L1_gnn_bk': (0.0, 2.0),
     'L1_gnn_bv': (0.0, 0.498),
     'L1_gnn_bs': (0.0, 0.497),
     'L1_gnn_g1': (1.0, 0.567),
     'L1_gnn_b1': (0.0, 0.351),
     'L1_gnn_g2': (1.0, 0.2),
     'L1_gnn_b2': (0.0, 0.321),
     'L1_gnn_b_ff1': (0.0, 0.572),
     'L1_gnn_b_ff2': (0.0, 0.406),
     'L1_mix_b_out': (0.0, 0.277),
     'L1_mix_g_out': (1.0, 0.2),
     'L1_mix_g_pre': (1.0, 0.6),
     'L1_ffn_br': (0.0, 0.8),
     'L1_ffn_b1': (0.0, 0.8),
     'L1_ffn_g1': (1.0, 0.6),
     'L1_ffn_be1': (0.0, 0.8),
     'L1_ffn_m1': (0.0, 0.8),
     'L1_ffn_v1': (1.0, 0.6),
     'L1_ffn_b2': (0.0, 0.8),
     'L1_ffn_g2': (1.0, 0.6),
     'L1_ffn_be2': (0.0, 0.8),
     'L1_ffn_m2': (0.0, 0.8),
     'L1_ffn_v2': (1.0, 0.6),
     'L1_ffn_bo': (0.0, 0.696)}
    factors = {'edge_weight': 43.206,
     'L0_mix_bout': 8.0,
     'L0_ffn_wr': 4.856,
     'L0_ffn_w1': 5.004,
     'L0_ffn_w2': 4.681,
     'L1_mix_w_qkv': 8.0,
     'L1_mix_mem_kv': 8.0,
     'L1_mix_w_out': 8.0,
     'L1_gnn_wq': 2.873}
    for name, (base, spread) in spreads.items():
        noise = np.random.default_rng([zlib.crc32(name.encode()), seed]).standard_normal(out[name].shape)
        drawn = base * np.exp(spread * noise) if base else spread * noise
        out[name] = jnp.asarray(drawn.astype(out[name].dtype))
    for name, factor in factors.items():
        out[name] = (out[name] * factor).astype(out[name].dtype)
    return out
```

```python
import numpy as np
import concourse.bass as bass
import concourse.mybir as mybir
from contextlib import ExitStack

F32 = mybir.dt.float32
I32 = mybir.dt.int32
BF16 = mybir.dt.bfloat16
ALU = mybir.AluOpType
ACT = mybir.ActivationFunctionType
AX = mybir.AxisListType

P = 128
N = 6250
E = 206250
D = 256
KD = D // P
D1 = D + 1
NT = 50
NG = NT // 2
NP = NT * P
TAIL = N - (NT - 2) * P
H = 8
B = 2 * H
NB = -(-E // (P * B))
C = B * NB
TOPK_ROUNDS = 32 // 8
L0_HEADS, L0_DH = 8, 64
INNER = L0_HEADS * L0_DH
PAIRS = INNER // P
FF = 4 * D
KF = FF // P
KEEP = max(1, int(0.5 * N)) - 1
HEADS, DH, MEM = 4, 32, 4
HID = HEADS * DH
FF1 = 2 * D
K1 = FF1 // P
EX = 8
LN_EPS = 1e-5
BN_EPS = 1e-3
BIG = 1e30
FAR = 65536.0
NEG = -3.0e38

ROWS = ["bout", "wr", "ffn_b2", "bs", "bv", "g1", "b1", "g2", "b2", "b_ff2", "b_out", "g_out"]
COLS = {"ffn_b1": KF, "b_ff1": K1, "g_pre": KD, "bq": KD, "ffn_br": 1, "we": 1, "be": 1, "moe_br": EX,
        "b1": 2 * EX, "g1": 2 * EX, "be1": 2 * EX, "m1": 2 * EX, "v1": 2 * EX,
        "b2": 2 * EX, "g2": 2 * EX, "be2": 2 * EX, "m2": 2 * EX, "v2": 2 * EX, "mem_k": MEM}
ROW = {n: i for i, n in enumerate(ROWS)}
COL, NCOL = {}, 0
for _n, _k in COLS.items():
    COL[_n] = NCOL
    NCOL += _k


def wait(eng, sem, value):
    if isinstance(value, int) and value <= 0:
        return
    eng.wait_ge(sem, value)


class Chain:

    def __init__(self, eng, sem):
        self.eng, self.sem, self.base, self.k, self.g, self.per = eng, sem, 0, 0, None, 0

    def link(self, ins, fence=False):
        self.k += 1
        ins.then_inc(self.sem, 1)
        v = self.base + self.k
        if self.g is not None:
            v = self.base + (self.g - 1) * self.per + self.k
        self.eng.wait_ge(self.sem, v)
        if fence and self.g is not None:
            self.eng.nop(nofuse=True)

    def groups(self, count, body):
        start = self.k
        body(0)
        self.per = self.k - start
        self.base, self.k = self.base + self.k, 0
        with self.eng.Fori(1, count) as g:
            self.g = g
            body(g)
            self.g = None
        assert self.k == self.per
        self.base, self.k = self.base + (count - 1) * self.per, 0


def plain_groups(eng, count, body):
    body(0)
    with eng.Fori(1, count) as g:
        body(g)


def build(nc, a, out):
    ctx = ExitStack()
    with ctx:
        def sb(name, shape, dt=F32):
            return ctx.enter_context(nc.sbuf_tensor(name, shape, dt))

        def sem(name):
            return ctx.enter_context(nc.semaphore(name))

        def table(name, width):
            return nc.dram_tensor(name, (NP, width), F32).ap()

        t_xn, t_hs, t_xn1, t_xs, t_y = (table(n, D) for n in ("t_xn", "t_hs", "t_xn1", "t_xs", "t_y"))
        t_x2, t_xn2, t_x3, t_xn3 = (table(n, D) for n in ("t_x2", "t_xn2", "t_x3", "t_xn3"))
        t_ag0, t_ag1, t_qk = (table(n, D1) for n in ("t_ag0", "t_ag1", "t_qk"))
        t_kv, t_q = table("t_kv", 2 * HID), table("t_q", HID)
        t_w = nc.dram_tensor("t_w", (1, NP), F32).ap()
        t_att = nc.dram_tensor("t_att", (1, C * P), F32).ap()

        src_c = sb("src_c", [P, C], I32)
        src_r = sb("src_r", [P, C], I32)
        dst_r = sb("dst_r", [P, C], I32)
        dstf = sb("dstf", [P, C + 1])
        endrow = sb("endrow", [P, C], I32)
        wt = sb("wt", [P, C])
        ewt = sb("ewt", [P, C])
        reg_s = sb("reg_s", [P, 6 * C])
        reg_g = sb("reg_g", [P, 2 * B * D1 + 2 * H * P])
        w_mix = sb("w_mix", [P, KD, D])
        w_qk = sb("w_qk", [P, KD, D1])
        w_qkv = sb("w_qkv", [P, KD, 3 * HID])
        w_out = sb("w_out", [P, D])
        w_m2 = sb("w_m2", [P, D])
        w_v = sb("w_v", [P, KD, D])
        w_s = sb("w_s", [P, KD, D])
        w_ff1 = sb("w_ff1", [P, KD, FF1])
        w_ff2 = sb("w_ff2", [P, K1, D])
        w_r = sb("w_r", [P, KD, EX])
        w_bo = sb("w_bo", [EX, D])
        mem_v = sb("mem_v", [MEM, HID + 1])
        rows = sb("rows", [P, len(ROWS), D])
        cols = sb("cols", [P, NCOL])
        qk_bias = sb("qk_bias", [P, D1])
        nb = sb("nb", [P, 2, 4200])
        ident = sb("ident", [P, P])
        lower = sb("lower", [P, P])
        ones = sb("ones", [P, P])
        e127 = sb("e127", [P, 1])
        half = sb("half", [P, 16])
        headmask = sb("headmask", [P, P])
        padneg = sb("padneg", [P, NT])
        dots = sb("dots", [P, PAIRS, P])
        fold = sb("fold", [P, PAIRS, D])
        w_all = sb("w_all", [P, NT])
        w_rank = sb("w_rank", [P, NT])
        above = sb("above", [P, NT])
        sel = sb("sel", [P, NT])
        pick = sb("pick", [P, 4, NT])
        kmax = sb("kmax", [P, HID])
        kneg = sb("kneg", [P, HID])
        ctxv = sb("ctxv", [P, HID + 1])
        ctxn = sb("ctxn", [P, 2, P])
        small = sb("small", [P, 64])
        srow = sb("srow", [1, 4, P])
        moe = sb("moe", [P, 6, 2 * EX])
        sidx = sb("sidx", [P, 2, H], I32)
        eidx = sb("eidx", [P, 2, H], I32)
        dcol = sb("dcol", [P, 2, H])
        scol = sb("scol", [P, 2, H])
        zrow = sb("zrow", [P, D1])

        def view(reg, off, *dims):
            n = 1
            for d in dims:
                n *= d
            v = reg[:, off:off + n]
            if len(dims) == 2:
                v = v.rearrange("p (a b) -> p a b", b=dims[1])
            if len(dims) == 3:
                v = v.rearrange("p (a b c) -> p a b c", b=dims[1], c=dims[2])
            return v

        s_wneigh = view(reg_s, 0, KD, D)
        s_wkv = view(reg_s, 512, KD, 2 * INNER)
        s_wq = view(reg_s, 2560, PAIRS, D)
        s_wout = view(reg_s, 3584, PAIRS, D)
        s_w1 = view(reg_s, 4608, KD, FF)
        s_w2 = view(reg_s, 6656, KF, D)
        s_wqT = view(reg_s, 8704, KD, D)
        s_wkT = fold[:, :, :].rearrange("p a b -> p (a b)")[:, 0:KD * D1].rearrange("p (a b) -> p a b", b=D1)
        score, s_prev, s_next, s_a, s_b, s_c = (view(reg_s, i * C, C) for i in range(6))
        s_wo = view(reg_s, 0, EX, KD, D)
        GR = view(reg_g, 0, B, D1)
        ZR = view(reg_g, B * D1, B, D1)
        PICKM = view(reg_g, 2 * B * D1, H, P)
        CARRYM = view(reg_g, 2 * B * D1 + H * P, H, P)
        w_bcast = view(reg_g, 0, NP)
        junk = reg_g[:, NP:NP + NP // 2].bitcast(BF16)
        g_w1 = view(reg_g, 0, EX, KD, D)
        g_w2 = view(reg_g, 4096, EX, KD, D)

        psT = [ctx.enter_context(nc.psum_tensor(f"psT{i}", [P, 512], F32)) for i in range(2)]
        psA = [ctx.enter_context(nc.psum_tensor(f"psA{i}", [P, 512], F32)) for i in range(2)]
        psB = [ctx.enter_context(nc.psum_tensor(f"psB{i}", [P, 1024], F32)) for i in range(2)]
        psZ = [psA[0], psA[1], psB[0], psB[1]]

        def nbuf(s, off, n):
            return nb[:, s, off:off + n]

        def row(name):
            return rows[:, ROW[name], :]

        def col(name, i=0, n=1):
            return cols[:, COL[name] + i:COL[name] + i + n]

        loaded = sem("loaded")
        consts = sem("consts")
        phase = sem("phase")
        dve_step, pool_step, act_step = sem("dve_step"), sem("pool_step"), sem("act_step")
        ld = [sem("ld0"), sem("ld1")]
        sta = [sem("sta0"), sem("sta1")]
        stb = [sem("stb0"), sem("stb1")]
        stc = [sem("stc0"), sem("stc1")]
        std = [sem("std0"), sem("std1")]
        zeroed = sem("zeroed")
        g_sem = [sem(f"gather{i}") for i in range(B)]
        z_sem = [sem(f"scatter{i}") for i in range(B)]
        misc = sem("misc")
        out_done = sem("out_done")

        class Base:
            pass

        names = ["xT_ps", "xT_sb", "var_ok", "rstd_ok", "xn_ok", "mm_a", "mm_b", "ev_a", "ev_b", "hs_ok",
                 "sq_red", "rstd_kv", "v_ok", "dots_ps", "dots_ok", "sum_ok", "res_ok", "tT_ps", "tT_sb",
                 "ff_ps", "ff_sb", "q_max", "q_exp", "var2_ok", "rstd2_ok", "rstd3_ok"]
        sg = {n: sem(n) for n in names}
        pe_one, dve_one, act_one = sem("pe_one"), sem("dve_one"), sem("act_one")
        idx_ok, dcol_ok, row_ps, pickm_ok, sum_ps, sum_sb, scored = (
            sem(n) for n in ("idx_ok", "dcol_ok", "row_ps", "pickm_ok", "sum_ps", "sum_sb", "scored"))
        scan_ok, shifted, attention_ok, moe_var, moe_root, moe_ok = (
            sem(n) for n in ("scan_ok", "shifted", "attention_ok", "moe_var", "moe_root", "moe_ok"))
        l1_ps, l1_sb, l2_ps, l2_sb, lo_ps, lo_ok = (
            sem(n) for n in ("l1_ps", "l1_sb", "l2_ps", "l2_sb", "lo_ps", "lo_ok"))

        used = {"P1": ["xT_ps", "xT_sb", "var_ok", "rstd_ok", "xn_ok", "mm_a", "mm_b", "ev_a", "ev_b", "hs_ok",
                       "sq_red", "rstd_kv", "v_ok", "dots_ps", "dots_ok"],
                "P3": ["xT_ps", "xT_sb", "var_ok", "rstd_ok", "xn_ok", "mm_a", "ev_a", "sum_ok"],
                "P3b": ["xT_ps", "xT_sb", "mm_b", "ev_b", "mm_a", "res_ok"],
                "P4": ["xT_ps", "xT_sb", "var_ok", "rstd_ok", "xn_ok", "mm_a", "ev_a", "mm_b", "ev_b",
                       "q_max", "q_exp", "res_ok", "var2_ok", "rstd2_ok", "sum_ok", "hs_ok"],
                "P4b": ["q_max", "q_exp", "mm_a", "ev_a"],
                "P6": ["xT_ps", "xT_sb", "mm_a", "ev_a", "var_ok", "rstd_ok", "xn_ok", "tT_ps", "tT_sb",
                       "ff_ps", "ff_sb", "mm_b", "var2_ok", "rstd2_ok", "sq_red", "rstd_kv", "res_ok",
                       "dots_ok", "v_ok", "rstd3_ok"],
                "P7": ["xT_ps", "xT_sb", "mm_a", "q_max", "q_exp", "tT_ps", "tT_sb", "res_ok", "ev_a", "mm_b",
                       "sum_ok"]}
        bases, count = {}, {n: 0 for n in names}
        for ph, ns in used.items():
            bases[ph] = dict(count)
            for n in ns:
                count[n] += NT
        ld_base, k = {}, 0
        for ph, n in (("P1", 1), ("P3", 3), ("P3b", 1), ("P4", 2), ("P4b", 1), ("P6", 4), ("P7", 2)):
            ld_base[ph] = (k, 16 * n)
            k += 16 * n * NG
        st_used = {"P1": "ab", "P3": "abc", "P3b": "a", "P4": "abcd", "P4b": "", "P6": "ab", "P7": "a"}
        st_base, cnt = {}, {c: 0 for c in "abcd"}
        st_extra = {"P4": {"d": 1}}
        for ph, cs in st_used.items():
            st_base[ph] = dict(cnt)
            for c in cs:
                cnt[c] += 16 * NG * (1 + st_extra.get(ph, {}).get(c, 0))
        stores = {"a": sta, "b": stb, "c": stc, "d": std}

        def sig(ph, n):
            assert n in used[ph], (ph, n)
            return sg[n], bases[ph][n]

        def need(eng, ph, n, value):
            if isinstance(value, int) and value <= 0:
                return
            s, b = sig(ph, n)
            eng.wait_ge(s, b + value)

        def stored(eng, ph, c, s, g, per=1):
            assert c in st_used[ph]
            if isinstance(g, int) and g <= 0:
                return
            eng.wait_ge(stores[c][s], st_base[ph][c] + 16 * per * g)

        def landed(eng, ph, s, g):
            b, per = ld_base[ph]
            eng.wait_ge(ld[s], b + per * (g + 1))

        def phase_end(eng, k):
            eng.drain().then_inc(phase, 1)
            eng.wait_ge(phase, 5 * k)

        def tile_rows(t):
            return bass.ds(t * P, P)

        loads = [
            (src_c[:, :], a["src_c"]), (src_r[:, :], a["src_r"]), (dst_r[:, :], a["dst_r"]),
            (ewt[:, :], a["ew_r"]), (rows[:, :, :].rearrange("p a b -> p (a b)"), a["rows"]),
            (cols[:, :], a["cols"]),
            (s_wneigh, a["W_neigh"]), (s_wkv, a["Wkv"]), (s_wq, a["Wq"]), (s_wout, a["WoutT"]),
            (s_w1, a["w1"]), (s_w2, a["w2"]), (s_wqT, a["wqT"]), (s_wkT, a["wkTb"]),
            (w_mix[:, :, :], a["W_self"]), (w_qkv[:, :, :], a["w_qkv"]), (w_out[:, :], a["w_out"]),
            (w_v[:, :, :], a["wv"]), (w_s[:, :, :], a["ws"]), (w_ff1[:, :, :], a["w_ff1"]),
            (w_ff2[:, :, :], a["w_ff2"]), (w_r[:, :, :], a["Wr"]), (w_bo[:, :], a["bo"]),
            (mem_v[:, 0:HID], a["mem_v"]),
            (dstf[:, :].bitcast(I32), a["dst_c"]),
            (endrow[:, :], a["dstn_c"]),
        ]
        NLOAD = 16 * len(loads)
        N_CONST = 12

        block = ctx.enter_context(nc.Block())

        @block.sync
        def _(sp):
            for dst_ap, src_ap in loads:
                if len(dst_ap.shape) == 3:
                    src_ap = src_ap.rearrange("p (a b) -> p a b", b=dst_ap.shape[2])
                sp.dma_start(dst_ap, src_ap).then_inc(loaded, 16)

            def hold(ph, n, value):
                need(sp, ph, n, value)
                sp.nop(nofuse=True)

            def pairs(prologue_load, load, store):
                for s in range(2):
                    load(s, s, 0, True)

                def body(g, last=False):
                    if not last:
                        for s in range(2):
                            load(2 * g + 2 + s, s, g + 1, False)
                    for s in range(2):
                        store(2 * g + s, s, g)
                body(0)
                with sp.Fori(1, NG - 1) as g:
                    body(g)
                body(NG - 1, True)

            def load(t, s, g, first):
                if not first:
                    hold("P1", "xn_ok", t - 1)
                sp.dma_start(nbuf(s, 0, D), a["x"][tile_rows(t), :]).then_inc(ld[s], 16)

            def store(t, s, g):
                hold("P1", "xn_ok", t + 1)
                sp.dma_start(t_xn[tile_rows(t), :], nbuf(s, 256, D)).then_inc(sta[s], 16)
                hold("P1", "hs_ok", t + 1)
                sp.dma_start(t_hs[tile_rows(t), :], nbuf(s, 1280, D)).then_inc(stb[s], 16)
            pairs(True, load, store)
            sp.wait_ge(consts, N_CONST)
            for tab in (t_ag0, t_ag1):
                with sp.Fori(0, NT) as t:
                    sp.dma_start(tab[tile_rows(t), :], zrow[:, :]).then_inc(zeroed, 16)
            sp.wait_ge(zeroed, 2 * NT * 16)
            for s in range(2):
                stored(sp, "P1", "a", s, NG)
                stored(sp, "P1", "b", s, NG)
            phase_end(sp, 1)
            phase_end(sp, 2)

            def load(t, s, g, first):
                if not first:
                    hold("P3", "var_ok", t - 1)
                sp.dma_start(nbuf(s, 0, D), a["x"][tile_rows(t), :]).then_inc(ld[s], 16)
                sp.dma_start(nbuf(s, 256, D), t_xn[tile_rows(t), :]).then_inc(ld[s], 16)
                sp.dma_start(nbuf(s, 512, D1), t_ag0[tile_rows(t), :]).then_inc(ld[s], 16)

            def store(t, s, g):
                hold("P3", "xn_ok", t + 1)
                sp.dma_start(t_xn1[tile_rows(t), :], nbuf(s, 1536, D)).then_inc(sta[s], 16)
                hold("P3", "sum_ok", t + 1)
                sp.dma_start(t_xs[tile_rows(t), :], nbuf(s, 1792, D)).then_inc(stb[s], 16)
                hold("P3", "ev_a", t + 1)
                sp.dma_start(t_w[0, bass.ds(t * P, P)].rearrange("(p a) -> p a", a=1),
                             nbuf(s, 2304, 1)).then_inc(stc[s], 16)
            pairs(True, load, store)
            for s in range(2):
                for c in "abc":
                    stored(sp, "P3", c, s, NG)
            sp.dma_start(w_bcast, t_w[0:1, :].to_broadcast([P, NP])).then_inc(misc, 16)
            sp.wait_ge(misc, 16)
            phase_end(sp, 3)

            def load(t, s, g, first):
                if not first:
                    hold("P3b", "xT_ps", t - 1)
                sp.dma_start(nbuf(s, 0, D), t_xn1[tile_rows(t), :]).then_inc(ld[s], 16)

            def store(t, s, g):
                hold("P3b", "res_ok", t + 1)
                sp.dma_start(t_y[tile_rows(t), :], nbuf(s, 2048, D)).then_inc(sta[s], 16)
            pairs(True, load, store)
            for s in range(2):
                stored(sp, "P3b", "a", s, NG)
            phase_end(sp, 4)

            def load(t, s, g, first):
                if not first:
                    hold("P4", "sum_ok", t - 1)
                sp.dma_start(nbuf(s, 0, D), t_xs[tile_rows(t), :]).then_inc(ld[s], 16)
                sp.dma_start(nbuf(s, 256, D), t_y[tile_rows(t), :]).then_inc(ld[s], 16)

            def store(t, s, g):
                hold("P4", "sum_ok", t + 1)
                sp.dma_start(t_x2[tile_rows(t), :], nbuf(s, 512, D)).then_inc(sta[s], 16)
                hold("P4", "xn_ok", t + 1)
                sp.dma_start(t_xn2[tile_rows(t), :], nbuf(s, 768, D)).then_inc(stb[s], 16)
                hold("P4", "ev_a", t + 1)
                sp.dma_start(t_qk[tile_rows(t), :], nbuf(s, 1280, D1)).then_inc(stc[s], 16)
                hold("P4", "ev_b", t + 1)
                sp.dma_start(t_kv[tile_rows(t), :], nbuf(s, 1792, 2 * HID)).then_inc(std[s], 16)
                hold("P4", "res_ok", t + 1)
                sp.dma_start(t_q[tile_rows(t), :], nbuf(s, 2560, HID)).then_inc(std[s], 16)
            pairs(True, load, store)
            for s in range(2):
                for c in "abc":
                    stored(sp, "P4", c, s, NG)
                stored(sp, "P4", "d", s, NG, 2)
            phase_end(sp, 5)

            def load(t, s, g, first):
                if not first:
                    hold("P4b", "mm_a", t - 1)
                sp.dma_start(nbuf(s, 0, 2 * HID), t_kv[tile_rows(t), :]).then_inc(ld[s], 16)
            pairs(True, load, lambda t, s, g: None)
            phase_end(sp, 6)

            sp.dma_start(s_a.bitcast(I32), a["dprev_r"]).then_inc(misc, 16)
            sp.dma_start(s_b.bitcast(I32), a["dnext_r"]).then_inc(misc, 16)
            sp.wait_ge(attention_ok, 1)
            sp.dma_start(t_att[0, :].rearrange("(p c) -> p c", c=C), s_c).then_inc(misc, 16)
            sp.wait_ge(misc, 64)
            for i in range(-(-C // P)):
                n = min(P, C - i * P)
                sp.dma_start(reg_g[0:n, i * P:(i + 1) * P], t_att[0, i * P * P:(i * P + n) * P].rearrange("(c q) -> c q", q=P)).then_inc(misc, 16)
            phase_end(sp, 7)
            phase_end(sp, 8)

            sp.dma_start(view(reg_g, 0, 4096), a["W1"]).then_inc(misc, 16)
            sp.dma_start(view(reg_g, 4096, 4096), a["W2"]).then_inc(misc, 16)
            sp.dma_start(view(reg_s, 0, 4096), a["Wo"]).then_inc(misc, 16)

            def load(t, s, g, first):
                if not first:
                    hold("P6", "res_ok", t - 1)
                sp.dma_start(nbuf(s, 0, D), t_x2[tile_rows(t), :]).then_inc(ld[s], 16)
                sp.dma_start(nbuf(s, 256, D), t_xn2[tile_rows(t), :]).then_inc(ld[s], 16)
                sp.dma_start(nbuf(s, 512, D1), t_ag1[tile_rows(t), :]).then_inc(ld[s], 16)
                sp.dma_start(nbuf(s, 769, HID), t_q[tile_rows(t), :]).then_inc(ld[s], 16)

            def store(t, s, g):
                hold("P6", "res_ok", t + 1)
                sp.dma_start(t_x3[tile_rows(t), :], nbuf(s, 3584, D)).then_inc(sta[s], 16)
                hold("P6", "dots_ok", t + 1)
                sp.dma_start(t_xn3[tile_rows(t), :], nbuf(s, 3840, D)).then_inc(stb[s], 16)
            pairs(True, load, store)
            for s in range(2):
                stored(sp, "P6", "a", s, NG)
                stored(sp, "P6", "b", s, NG)
            phase_end(sp, 9)

            def load(t, s, g, first):
                if not first:
                    hold("P7", "ev_a", t - 1)
                sp.dma_start(nbuf(s, 0, D), t_x3[tile_rows(t), :]).then_inc(ld[s], 16)
                sp.dma_start(nbuf(s, 256, D), t_xn3[tile_rows(t), :]).then_inc(ld[s], 16)

            def store(t, s, g):
                sp.wait_ge(lo_ok, g * 2 * EX + 2 * EX - 1 + s)
                sp.nop(nofuse=True)
                if isinstance(t, int) and t >= NT - 2:
                    n = TAIL if t == NT - 2 else 0
                    if n:
                        sp.dma_start(out[t * P:t * P + n, :], nbuf(s, 1792, D)[0:n, :]).then_inc(sta[s], 16)
                else:
                    sp.dma_start(out[tile_rows(t), :], nbuf(s, 1792, D)).then_inc(sta[s], 16)
            pairs(True, load, store)
            stored(sp, "P7", "a", 0, NG)
            stored(sp, "P7", "a", 1, NG - 1)

        @block.gpsimd
        def _(po):
            ch = Chain(po, pool_step)
            nc.gpsimd.memset(ident[:, :], 0.0).then_inc(consts, 1)
            nc.gpsimd.memset(lower[:, :], 1.0).then_inc(consts, 1)
            nc.gpsimd.memset(e127[:, :], 1.0).then_inc(consts, 1)
            nc.gpsimd.memset(padneg[:, :], 0.0).then_inc(consts, 1)
            po.wait_ge(consts, 4)
            nc.gpsimd.affine_select(out=ident[:, :], in_=ident[:, :], compare_op=ALU.not_equal, fill=1.0,
                                    base=0, pattern=[[-1, P]], channel_multiplier=1).then_inc(consts, 1)
            nc.gpsimd.affine_select(out=lower[:, :], in_=lower[:, :], compare_op=ALU.is_gt, fill=0.0,
                                    base=0, pattern=[[1, P]], channel_multiplier=-1).then_inc(consts, 1)
            nc.gpsimd.affine_select(out=e127[:, :], in_=e127[:, :], compare_op=ALU.is_ge, fill=0.0,
                                    base=1 - P, pattern=[[0, 1]], channel_multiplier=1).then_inc(consts, 1)
            nc.gpsimd.affine_select(out=padneg[:, :], in_=padneg[:, :], compare_op=ALU.is_ge, fill=NEG,
                                    base=N - 1, pattern=[[-P, NT]], channel_multiplier=-1).then_inc(consts, 1)
            nc.gpsimd.memset(half[:, :], -0.5).then_inc(consts, 1)
            nc.gpsimd.memset(ones[:, :], 1.0).then_inc(consts, 1)
            nc.gpsimd.memset(zrow[:, :], 0.0).then_inc(consts, 1)
            nc.gpsimd.memset(mem_v[:, HID:HID + 1], 1.0).then_inc(consts, 1)
            po.wait_ge(consts, N_CONST)

            def root(ph, var, rstd, t, s, src_off, dst_off):
                need(po, ph, var, t + 1)
                nc.gpsimd.tensor_tensor(nbuf(s, dst_off, 1), nbuf(s, src_off, 1), half[:, 0:1],
                                        ALU.pow).then_inc(sg[rstd], 1)

            po.wait_ge(moe_var, 2)
            for i in (4, 5):
                nc.gpsimd.tensor_tensor(moe[:, i, :], moe[:, i, :], half[:, 0:2 * EX],
                                        ALU.pow).then_inc(moe_root, 1)

            def body(g):
                for s in range(2):
                    root("P1", "var_ok", "rstd_ok", 2 * g + s, s, 4108, 4110)
                for s in range(2):
                    need(po, "P1", "sq_red", 2 * g + s + 1)
                    nc.gpsimd.tensor_tensor(nbuf(s, 4160, 8), nbuf(s, 4144, 8), half[:, 0:8],
                                            ALU.pow).then_inc(sg["rstd_kv"], 1)
            plain_groups(po, NG, body)
            phase_end(po, 1)

            def gather(rnd, h, idx, table_, dst, sems):
                for k in range(H):
                    s = h * H + k
                    nc.gpsimd.indirect_dma_start(
                        out=dst[:, s, 0:table_.shape[1]], out_offset=None, in_=table_[:, :],
                        in_offset=bass.IndirectOffsetOnAxis(ap=idx[:, h, k:k + 1], axis=0)).then_inc(sems[s], 16)

            def sum_pass(table_, sums, rnd0, chunk0):
                g0, z0, i0 = rnd0

                def fetch(it, h):
                    wait(po, sum_ps, chunk0 + it * B + h * H - H if not isinstance(it, int) or it > 0 else 0)
                    if not isinstance(it, int):
                        for k in range(H):
                            po.wait_ge(z_sem[h * H + k], z0 + it * 16)
                        po.nop(nofuse=True)
                    nc.gpsimd.tensor_copy(sidx[:, h, :], src_c[:, bass.ds(it * B + h * H, H)]).then_inc(idx_ok, 1)
                    nc.gpsimd.tensor_copy(eidx[:, h, :], endrow[:, bass.ds(it * B + h * H, H)]).then_inc(idx_ok, 1)
                    po.wait_ge(idx_ok, i0 + (it * 2 + h) * 2 + 2)
                    po.nop(nofuse=True)
                    gather(it, h, sidx, table_, GR, g_sem)

                def emit(it, h):
                    for k in range(H):
                        s = h * H + k
                        po.wait_ge(sum_sb, chunk0 + it * B + s + 1)
                        po.nop(nofuse=True)
                        nc.gpsimd.indirect_dma_start(
                            out=sums[:, :], out_offset=bass.IndirectOffsetOnAxis(ap=eidx[:, h, k:k + 1], axis=0),
                            in_=ZR[:, s, :], in_offset=None, bounds_check=NP - 1,
                            oob_is_err=False).then_inc(z_sem[s], 16)

                def body(it):
                    fetch(it, 0)
                    fetch(it, 1)
                    emit(it, 0)
                    emit(it, 1)
                plain_groups(po, NB, body)
                for s in range(B):
                    po.wait_ge(z_sem[s], z0 + 16 * NB)

            sum_pass(t_hs, t_ag0, (0, 0, 0), 0)
            phase_end(po, 2)

            def body(g):
                for s in range(2):
                    root("P3", "var_ok", "rstd_ok", 2 * g + s, s, 4108, 4110)
                for s in range(2):
                    need(po, "P3", "xn_ok", 2 * g + s + 1)
                    stored(po, "P3", "b", s, g)
                    nc.gpsimd.tensor_tensor(nbuf(s, 1792, D), nbuf(s, 1280, D), nbuf(s, 1536, D),
                                            ALU.add).then_inc(sg["sum_ok"], 1)
            plain_groups(po, NG, body)
            phase_end(po, 3)
            phase_end(po, 4)

            def body(g):
                for s in range(2):
                    root("P4", "var_ok", "rstd_ok", 2 * g + s, s, 4108, 4110)
                for s in range(2):
                    root("P4", "var2_ok", "rstd2_ok", 2 * g + s, s, 4112, 4114)
            plain_groups(po, NG, body)
            phase_end(po, 5)
            phase_end(po, 6)

            def body(it):
                for h in range(2):
                    wait(po, scored, it * B + h * H - H if not isinstance(it, int) or it > 0 else 0)
                    if not isinstance(it, int):
                        po.nop(nofuse=True)
                    nc.gpsimd.tensor_copy(sidx[:, h, :], src_r[:, bass.ds(it * B + h * H, H)]).then_inc(idx_ok, 1)
                    nc.gpsimd.tensor_copy(eidx[:, h, :], dst_r[:, bass.ds(it * B + h * H, H)]).then_inc(idx_ok, 1)
                    po.wait_ge(idx_ok, 4 * NB + (it * 2 + h) * 2 + 2)
                    po.nop(nofuse=True)
                    gather(it, h, sidx, t_xn2, GR, g_sem)
                    gather(it, h, eidx, t_qk, ZR, z_sem)
            plain_groups(po, NB, body)
            phase_end(po, 7)
            sum_pass(t_xn2, t_ag1, (32 * NB, 32 * NB, 8 * NB), C)
            phase_end(po, 8)

            def body(g):
                for s in range(2):
                    root("P6", "var_ok", "rstd_ok", 2 * g + s, s, 4108, 4110)
                for s in range(2):
                    root("P6", "sq_red", "rstd_kv", 2 * g + s, s, 4112, 4114)
                for s in range(2):
                    root("P6", "var2_ok", "rstd2_ok", 2 * g + s, s, 4108, 4110)
                for s in range(2):
                    need(po, "P6", "v_ok", 2 * g + s + 1)
                    nc.gpsimd.tensor_tensor(nbuf(s, 4110, 1), nbuf(s, 4108, 1), half[:, 0:1],
                                            ALU.pow).then_inc(sg["rstd3_ok"], 1)
            plain_groups(po, NG, body)
            phase_end(po, 9)

        @block.tensor
        def _(pe):
            mm, tr = nc.tensor.matmul, nc.tensor.transpose

            def flip(ph, s, src_off, ps, ps_off=0, n=KD, name="xT_ps"):
                for k in range(n):
                    last = tr(ps[:, ps_off + k * P:ps_off + (k + 1) * P], nbuf(s, src_off + k * P, P), ident[:, :])
                if name:
                    last.then_inc(sg[name], 1)
                return last

            pe.wait_ge(consts, N_CONST)
            pe.wait_ge(loaded, NLOAD)
            pe.wait_ge(dve_one, 1)
            for c in range(KD):
                for k in range(KD):
                    last = mm(psA[c][:, 0:D1], s_wqT[:, k, c * P:(c + 1) * P], s_wkT[:, k, :],
                              start=(k == 0), stop=(k == KD - 1))
            for k in range(KD):
                last = mm(psB[0][:, 0:D1], col("bq", k).to_broadcast([P, P]), s_wkT[:, k, :],
                          start=(k == 0), stop=(k == KD - 1))
            last.then_inc(pe_one, 1)
            pe.wait_ge(dve_one, 2)

            def body(g):
                for s in range(2):
                    need(pe, "P1", "xn_ok", 2 * g + s + 1)
                    flip("P1", s, 256, psT[s])
                for s in range(2):
                    t = 2 * g + s
                    need(pe, "P1", "xT_sb", t + 1)
                    need(pe, "P1", "ev_a", t - 1)
                    for k in range(KD):
                        last = mm(psA[s][:, 0:D], nbuf(s, 512 + k * P, P), s_wneigh[:, k, :],
                                  start=(k == 0), stop=(k == KD - 1))
                    last.then_inc(sg["mm_a"], 1)
                    need(pe, "P1", "ev_b", t)
                    for n in range(2):
                        for k in range(KD):
                            last = mm(psB[0][:, n * 512:(n + 1) * 512], nbuf(s, 512 + k * P, P),
                                      s_wkv[:, k, n * 512:(n + 1) * 512], start=(k == 0), stop=(k == KD - 1))
                    last.then_inc(sg["mm_b"], 1)
                for s in range(2):
                    t = 2 * g + s
                    need(pe, "P1", "v_ok", t + 1)
                    need(pe, "P1", "dots_ok", t)
                    for j in range(PAIRS):
                        last = mm(psB[1][:, j * P:(j + 1) * P], nbuf(s, 3584 + j * P, P),
                                  nbuf(s, 1536 + j * P, P), start=True, stop=True)
                    last.then_inc(sg["dots_ps"], 1)
            plain_groups(pe, NG, body)
            phase_end(pe, 1)

            def sum_pass(g0, chunk0, d0):
                def body(it):
                    for h in range(2):
                        pe.wait_ge(dcol_ok, d0 + it * 2 + h + 1)
                        for k in range(H):
                            tr(psT[k // 4][:, (k % 4) * P:(k % 4 + 1) * P],
                               dcol[:, h, k:k + 1].to_broadcast([P, P]), ident[:, :]).then_inc(row_ps, 1)
                        for k in range(H):
                            s = h * H + k
                            pe.wait_ge(pickm_ok, chunk0 + it * B + s + 1)
                            pe.wait_ge(g_sem[s], g0 + it * 16 + 16)
                            if not (isinstance(it, int) and s < 4):
                                pe.wait_ge(sum_sb, chunk0 + it * B + s - 3)
                            mm(psZ[s % 4][:, 0:D1], PICKM[:, k, :], GR[:, s, :], start=True, stop=False)
                            if not (isinstance(it, int) and s == 0):
                                pe.wait_ge(sum_sb, chunk0 + it * B + s)
                            mm(psZ[s % 4][:, 0:D1], CARRYM[96:P, k, :], ZR[96:P, (s - 1) % B, :],
                               start=False, stop=True).then_inc(sum_ps, 1)
                plain_groups(pe, NB, body)

            pe.wait_ge(dve_one, 3)
            for j in range(PAIRS):
                last = mm(psB[j // 2][:, (j % 2) * 512:(j % 2) * 512 + D], dots[:, j, :], s_wout[:, j, :],
                          start=True, stop=True)
            last.then_inc(pe_one, 1)
            pe.wait_ge(act_one, 1)
            for c in range(KD):
                for j in range(PAIRS):
                    last = mm(psA[c][:, 0:D], s_wq[:, j, c * P:(c + 1) * P], fold[:, j, :],
                              start=(j == 0), stop=(j == PAIRS - 1))
            last.then_inc(pe_one, 1)
            pe.wait_ge(dve_one, 5)
            sum_pass(0, 0, 0)
            phase_end(pe, 2)

            def body(g):
                for s in range(2):
                    landed(pe, "P3", s, g)
                    flip("P3", s, 256, psT[s])
                for s in range(2):
                    t = 2 * g + s
                    need(pe, "P3", "xT_sb", t + 1)
                    need(pe, "P3", "var_ok", t - 1)
                    for k in range(KD):
                        last = mm(psA[s][:, 0:D], nbuf(s, 769 + k * P, P), w_mix[:, k, :],
                                  start=(k == 0), stop=(k == KD - 1))
                    last.then_inc(sg["mm_a"], 1)
            plain_groups(pe, NG, body)
            phase_end(pe, 3)

            def body(g):
                for s in range(2):
                    landed(pe, "P3b", s, g)
                    flip("P3b", s, 0, psT[s])
                for s in range(2):
                    t = 2 * g + s
                    need(pe, "P3b", "xT_sb", t + 1)
                    for m in range(KF):
                        for k in range(KD):
                            last = mm(psB[s][:, m * P:(m + 1) * P], s_w1[:, k, m * P:(m + 1) * P],
                                      nbuf(s, 256 + k * P, P), start=(k == 0), stop=(k == KD - 1))
                    last.then_inc(sg["mm_b"], 1)
                for s in range(2):
                    t = 2 * g + s
                    need(pe, "P3b", "ev_b", t + 1)
                    need(pe, "P3b", "res_ok", t - 1)
                    for m in range(KF):
                        last = mm(psA[s][:, 0:D], nbuf(s, 512 + m * P, P), s_w2[:, m, :],
                                  start=(m == 0), stop=(m == KF - 1))
                    last.then_inc(sg["mm_a"], 1)
            plain_groups(pe, NG, body)
            phase_end(pe, 4)

            pe.wait_ge(dve_one, 6)
            tr(psT[0][0:1, 0:P], small[:, 0:1], ident[:, :]).then_inc(pe_one, 1)
            pe.wait_ge(dve_one, 7)
            tr(psT[0][:, P:P + 1], small[0:1, 1:2].to_broadcast([1, P]), ident[0:1, 0:1]).then_inc(pe_one, 1)
            pe.wait_ge(dve_one, 8)
            mm(psT[1][:, 0:NT], lower[:, :], pick[:, 0, :], start=True, stop=True)
            mm(psT[1][:, 64:64 + NT], ones[:, :], pick[:, 0, :], start=True, stop=True).then_inc(pe_one, 1)
            pe.wait_ge(dve_one, 9)

            def body(g):
                for s in range(2):
                    t = 2 * g + s
                    need(pe, "P4", "xn_ok", t + 1)
                    flip("P4", s, 768, psT[s])
                for s in range(2):
                    t = 2 * g + s
                    need(pe, "P4", "xT_sb", t + 1)
                    need(pe, "P4", "ev_a", t - 1)
                    for k in range(KD):
                        last = mm(psA[s][:, 0:D1], nbuf(s, 1024 + k * P, P), w_qk[:, k, :],
                                  start=(k == 0), stop=(k == KD - 1))
                    last.then_inc(sg["mm_a"], 1)
                    need(pe, "P4", "q_max", t - 1)
                    for k in range(KD):
                        last = mm(psB[s][:, 0:3 * HID], nbuf(s, 1024 + k * P, P), w_qkv[:, k, :],
                                  start=(k == 0), stop=(k == KD - 1))
                    last.then_inc(sg["mm_b"], 1)
            plain_groups(pe, NG, body)
            phase_end(pe, 5)

            tr(psT[0][:, 0:P], kmax[:, :], ident[:, :]).then_inc(pe_one, 1)
            pe.wait_ge(dve_one, 11)
            tr(psT[0][:, P:2 * P], small[:, 2:3].to_broadcast([P, P]), ident[:, :]).then_inc(pe_one, 1)
            pe.wait_ge(act_one, 2)
            tr(psT[1][0:MEM, 0:P], small[:, 8:8 + MEM], ident[:, :]).then_inc(pe_one, 1)
            pe.wait_ge(dve_one, 13)
            mm(psT[1][:, P:P + HID + 1], nbuf(0, 1024, P)[0:MEM, :], mem_v[:, :],
               start=True, stop=True).then_inc(pe_one, 1)

            def body(g):
                for s in range(2):
                    t = 2 * g + s
                    need(pe, "P4b", "q_exp", t + 1)
                    need(pe, "P4b", "ev_a", t - 1)
                    mm(psA[s][:, 0:HID + 1], nbuf(s, 512, P), nbuf(s, 640, HID + 1),
                       start=True, stop=True).then_inc(sg["mm_a"], 1)
            plain_groups(pe, NG, body)
            pe.wait_ge(dve_one, 16)
            tr(psT[0][:, 0:P], ctxn[:, 0, :], ident[:, :]).then_inc(pe_one, 1)
            pe.wait_ge(act_one, 3)
            mm(psA[0][:, 0:D], ctxn[:, 1, :], w_out[:, :], start=True, stop=True).then_inc(pe_one, 1)
            phase_end(pe, 6)

            for i in range(4):
                pe.wait_ge(scan_ok, 2 * i + 1)
                tr(psT[0][0:1, 0:P], small[:, 16:17], ident[:, :])
                tr(psT[0][0:1, P:2 * P], small[:, 17:18], ident[:, :]).then_inc(pe_one, 1)
                pe.wait_ge(scan_ok, 2 * i + 2)
                tr(psT[1][:, 0:1], srow[0:1, 3, :], ident[0:1, 0:1]).then_inc(pe_one, 1)
            nload = -(-C // P)
            pe.wait_ge(misc, 64 + 16 * nload)
            for i in range(nload):
                n = min(P, C - i * P)
                if i >= 2:
                    pe.wait_ge(act_one, 5 + i - 2)
                tr(psT[i % 2][:, 0:n], reg_g[0:n, i * P:(i + 1) * P], ident[0:n, 0:n]).then_inc(pe_one, 1)
            phase_end(pe, 7)
            sum_pass(32 * NB, C, 2 * NB)
            phase_end(pe, 8)

            def body(g):
                for s in range(2):
                    landed(pe, "P6", s, g)
                    flip("P6", s, 256, psB[s], 0, name=None)
                    flip("P6", s, 512, psB[s], 2 * P, name=None)
                    flip("P6", s, 769, psB[s], 4 * P, n=1)
                for s in range(2):
                    t = 2 * g + s
                    need(pe, "P6", "xT_sb", t + 1)
                    need(pe, "P6", "ev_a", t - 1)
                    for k in range(KD):
                        mm(psA[s][:, 0:D], nbuf(s, 1024 + k * P, P), w_s[:, k, :], start=(k == 0), stop=False)
                    for k in range(KD):
                        mm(psA[s][:, 0:D], nbuf(s, 1280 + k * P, P), w_v[:, k, :],
                           start=False, stop=(k == KD - 1))
                    mm(psA[s][:, D:2 * D], nbuf(s, 1536, P), w_m2[:, :],
                       start=True, stop=True).then_inc(sg["mm_a"], 1)
                for s in range(2):
                    need(pe, "P6", "xn_ok", 2 * g + s + 1)
                    flip("P6", s, 1920, psT[s], name="tT_ps")
                for s in range(2):
                    need(pe, "P6", "tT_sb", 2 * g + s + 1)
                    for m in range(K1):
                        for k in range(KD):
                            last = mm(psB[s][:, m * P:(m + 1) * P], w_ff1[:, k, m * P:(m + 1) * P],
                                      nbuf(s, 2176 + k * P, P), start=(k == 0), stop=(k == KD - 1))
                    last.then_inc(sg["ff_ps"], 1)
                for s in range(2):
                    need(pe, "P6", "ff_sb", 2 * g + s + 1)
                    for m in range(K1):
                        last = mm(psT[s][:, D:2 * D], nbuf(s, 2432 + m * P, P), w_ff2[:, m, :],
                                  start=(m == 0), stop=(m == K1 - 1))
                    last.then_inc(sg["mm_b"], 1)
            plain_groups(pe, NG, body)
            phase_end(pe, 9)

            pe.wait_ge(misc, 64 + 16 * nload + 48)

            def body(g):
                for s in range(2):
                    landed(pe, "P7", s, g)
                    flip("P7", s, 256, psT[s])
                for s in range(2):
                    t = 2 * g + s
                    need(pe, "P7", "xT_sb", t + 1)
                    for k in range(KD):
                        last = mm(psT[s][:, D:D + EX], nbuf(s, 512 + k * P, P), w_r[:, k, :],
                                  start=(k == 0), stop=(k == KD - 1))
                    last.then_inc(sg["mm_a"], 1)
                for s in range(2):
                    need(pe, "P7", "sum_ok", 2 * g + s + 1)
                    tr(psT[s][0:EX, 384:512], nbuf(s, 4120, EX), ident[:, :]).then_inc(sg["tT_ps"], 1)
                for s in range(2):
                    need(pe, "P7", "tT_sb", 2 * g + s + 1)
                    wait(pe, lo_ok, g * 2 * EX - 1 + s)
                    mm(psA[s][:, 0:D], nbuf(s, 2304, P)[0:EX, :], w_bo[:, :],
                       start=True, stop=True).then_inc(sg["mm_b"], 1)
                for e in range(EX):
                    for s in range(2):
                        n = g * 2 * EX + e * 2 + s
                        wait(pe, l1_sb, n - 1)
                        for m in range(KD):
                            for k in range(KD):
                                last = mm(psB[s][:, m * P:(m + 1) * P], g_w1[:, e, k, m * P:(m + 1) * P],
                                          nbuf(s, 512 + k * P, P), start=(k == 0), stop=(k == KD - 1))
                        last.then_inc(l1_ps, 1)
                    for s in range(2):
                        n = g * 2 * EX + e * 2 + s
                        wait(pe, l1_sb, n + 1)
                        for m in range(KD):
                            for k in range(KD):
                                last = mm(psB[s][:, 512 + m * P:512 + (m + 1) * P],
                                          g_w2[:, e, k, m * P:(m + 1) * P],
                                          nbuf(s, 768 + k * P, P), start=(k == 0), stop=(k == KD - 1))
                        last.then_inc(l2_ps, 1)
                    for s in range(2):
                        n = g * 2 * EX + e * 2 + s
                        wait(pe, l2_sb, n + 1)
                        if e == 0:
                            need(pe, "P7", "ev_a", 2 * g + s + 1)
                        else:
                            wait(pe, lo_ok, n - 1)
                        for k in range(KD):
                            last = mm(psA[s][:, 0:D], nbuf(s, 1024 + k * P, P), s_wo[:, e, k, :],
                                      start=(k == 0), stop=(k == KD - 1))
                        last.then_inc(lo_ps, 1)
            plain_groups(pe, NG, body)

        @block.scalar
        def _(act):
            cp, fn = nc.scalar.copy, nc.scalar.activation
            ch = Chain(act, act_step)

            def body(g):
                for s in range(2):
                    t = 2 * g + s
                    need(act, "P1", "xT_ps", t + 1)
                    need(act, "P1", "mm_b", t - 1)
                    cp(nbuf(s, 512, D), psT[s][:, 0:D]).then_inc(sg["xT_sb"], 1)
                for s in range(2):
                    t = 2 * g + s
                    need(act, "P1", "mm_a", t + 1)
                    need(act, "P1", "hs_ok", t - 1)
                    cp(nbuf(s, 768, D), psA[s][:, 0:D]).then_inc(sg["ev_a"], 1)
                    need(act, "P1", "mm_b", t + 1)
                    need(act, "P1", "dots_ps", t - 1)
                    cp(nbuf(s, 1536, 1024), psB[0][:, :])
                    need(act, "P1", "sq_red", t - 1)
                    fn(nbuf(s, 2560, 1024), psB[0][:, :], ACT.Square).then_inc(sg["ev_b"], 1)
            plain_groups(act, NG, body)
            phase_end(act, 1)

            act.wait_ge(pe_one, 2)
            for j in range(PAIRS):
                last = nc.scalar.mul(fold[:, j, :], psB[j // 2][:, (j % 2) * 512:(j % 2) * 512 + D], 1.0 / N)
            last.then_inc(act_one, 1)

            def sum_pass(chunk0, z0):
                def body(it):
                    for s in range(B):
                        act.wait_ge(sum_ps, chunk0 + it * B + s + 1)
                        if not isinstance(it, int):
                            act.wait_ge(z_sem[s], z0 + it * 16)
                        elif z0 > 0:
                            act.wait_ge(z_sem[s], z0)
                        cp(ZR[:, s, :], psZ[s % 4][:, 0:D1]).then_inc(sum_sb, 1)
                plain_groups(act, NB, body)
            sum_pass(0, 0)
            phase_end(act, 2)

            def body(g):
                for s in range(2):
                    t = 2 * g + s
                    need(act, "P3", "xT_ps", t + 1)
                    need(act, "P3", "mm_a", t - 1)
                    cp(nbuf(s, 769, D), psT[s][:, 0:D]).then_inc(sg["xT_sb"], 1)
            plain_groups(act, NG, body)
            phase_end(act, 3)

            def body(g):
                for s in range(2):
                    t = 2 * g + s
                    need(act, "P3b", "xT_ps", t + 1)
                    need(act, "P3b", "mm_b", t - 1)
                    cp(nbuf(s, 256, D), psT[s][:, 0:D]).then_inc(sg["xT_sb"], 1)
                for s in range(2):
                    t = 2 * g + s
                    need(act, "P3b", "mm_b", t + 1)
                    need(act, "P3b", "mm_a", t - 1)
                    for m in range(KF):
                        last = fn(nbuf(s, 512 + m * P, P), psB[s][:, m * P:(m + 1) * P], ACT.Gelu_apprx_tanh,
                                  bias=col("ffn_b1", m))
                    last.then_inc(sg["ev_b"], 1)
            plain_groups(act, NG, body)
            phase_end(act, 4)

            def body(g):
                for s in range(2):
                    t = 2 * g + s
                    need(act, "P4", "xT_ps", t + 1)
                    need(act, "P4", "mm_b", t - 1)
                    cp(nbuf(s, 1024, D), psT[s][:, 0:D]).then_inc(sg["xT_sb"], 1)
                for s in range(2):
                    t = 2 * g + s
                    need(act, "P4", "q_max", t + 1)
                    fn(nbuf(s, 2176, HID), nbuf(s, 2048, HID), ACT.Exp).then_inc(sg["q_exp"], 1)
            plain_groups(act, NG, body)
            phase_end(act, 5)

            act.wait_ge(dve_one, 12)
            fn(small[:, 8:8 + MEM], col("mem_k", 0, MEM), ACT.Exp, bias=small[:, 3:4]).then_inc(act_one, 1)

            def body(g):
                for s in range(2):
                    t = 2 * g + s
                    need(act, "P4b", "q_max", t + 1)
                    fn(nbuf(s, 512, P), nbuf(s, 256, P), ACT.Exp).then_inc(sg["q_exp"], 1)
            plain_groups(act, NG, body)
            act.wait_ge(pe_one, 11)
            cp(ctxn[:, 1, :], psT[0][:, 0:P]).then_inc(act_one, 1)
            phase_end(act, 6)

            act.wait_ge(shifted, 1)
            fn(s_c, s_c, ACT.Exp).then_inc(act_one, 1)
            nload = -(-C // P)
            for i in range(nload):
                n = min(P, C - i * P)
                act.wait_ge(pe_one, 21 + i)
                cp(wt[:, i * P:i * P + n], psT[i % 2][:, 0:n]).then_inc(act_one, 1)
            phase_end(act, 7)
            sum_pass(C, 32 * NB)
            phase_end(act, 8)

            def body(g):
                for s in range(2):
                    t = 2 * g + s
                    need(act, "P6", "xT_ps", t + 1)
                    need(act, "P6", "mm_a", t - 1)
                    cp(nbuf(s, 1024, 5 * P), psB[s][:, 0:5 * P]).then_inc(sg["xT_sb"], 1)
                for s in range(2):
                    t = 2 * g + s
                    need(act, "P6", "tT_ps", t + 1)
                    need(act, "P6", "ff_ps", t - 1)
                    cp(nbuf(s, 2176, D), psT[s][:, 0:D]).then_inc(sg["tT_sb"], 1)
                for s in range(2):
                    t = 2 * g + s
                    need(act, "P6", "ff_ps", t + 1)
                    need(act, "P6", "mm_b", t - 1)
                    for m in range(K1):
                        last = fn(nbuf(s, 2432 + m * P, P), psB[s][:, m * P:(m + 1) * P], ACT.Gelu_apprx_tanh,
                                  bias=col("b_ff1", m))
                    last.then_inc(sg["ff_sb"], 1)
            plain_groups(act, NG, body)
            phase_end(act, 9)

            act.wait_ge(moe_ok, 1)

            def body(g):
                for s in range(2):
                    t = 2 * g + s
                    need(act, "P7", "xT_ps", t + 1)
                    wait(act, l1_ps, g * 2 * EX - 1 + s)
                    cp(nbuf(s, 512, D), psT[s][:, 0:D]).then_inc(sg["xT_sb"], 1)
                for s in range(2):
                    need(act, "P7", "q_max", 2 * g + s + 1)
                    fn(nbuf(s, 4128, EX), nbuf(s, 4120, EX), ACT.Exp,
                       accum_out=nbuf(s, 4140, 1)).then_inc(sg["q_exp"], 1)
                for s in range(2):
                    need(act, "P7", "tT_ps", 2 * g + s + 1)
                    cp(nbuf(s, 2304, P)[0:EX, :], psT[s][0:EX, 384:512]).then_inc(sg["tT_sb"], 1)
                for e in range(EX):
                    for s in range(2):
                        n = g * 2 * EX + e * 2 + s
                        wait(act, l1_ps, n + 1)
                        wait(act, l2_ps, n - 1)
                        for m in range(KD):
                            i = e * KD + m
                            last = fn(nbuf(s, 768 + m * P, P), psB[s][:, m * P:(m + 1) * P], ACT.Relu,
                                      bias=moe[:, 1, i:i + 1], scale=moe[:, 0, i:i + 1])
                        last.then_inc(l1_sb, 1)
                    for s in range(2):
                        n = g * 2 * EX + e * 2 + s
                        wait(act, l2_ps, n + 1)
                        wait(act, lo_ps, n - 1)
                        for m in range(KD):
                            i = e * KD + m
                            last = fn(nbuf(s, 1024 + m * P, P), psB[s][:, 512 + m * P:512 + (m + 1) * P],
                                      ACT.Relu, bias=moe[:, 3, i:i + 1], scale=moe[:, 2, i:i + 1])
                        last.then_inc(l2_sb, 1)
            plain_groups(act, NG, body)

        @block.vector
        def _(v):
            ch = Chain(v, dve_step)
            link = ch.link
            tt, ts, stt = nc.vector.tensor_tensor, nc.vector.tensor_scalar, nc.vector.scalar_tensor_tensor
            red = nc.vector.tensor_reduce
            one = [0]

            def signal(ins):
                one[0] += 1
                ins.then_inc(dve_one, 1)
                v.wait_ge(dve_one, one[0])

            def stats(s, src, ph, var="var_ok", out_off=4108):
                link(nc.vector.bn_stats(nbuf(s, 4100, 6), nbuf(s, src, D)), True)
                link(nc.vector.bn_aggr(nbuf(s, 4106, 2), nbuf(s, 4100, 6)))
                ts(nbuf(s, out_off, 1), nbuf(s, 4107, 1), LN_EPS, None, ALU.add).then_inc(sg[var], 1)

            def normal(s, src, dst, name):
                ins = ts(nbuf(s, dst, D), nbuf(s, src, D), nbuf(s, 4106, 1), nbuf(s, 4110, 1),
                         ALU.subtract, ALU.mult)
                if name:
                    ins.then_inc(sg[name], 1)
                return ins

            nc.vector.memset(wt[:, :], 1.0)
            nc.vector.memset(dots[:, :, :], 0.0)
            link(nc.vector.memset(headmask[:, :], 0.0))
            for h in range(HEADS):
                link(nc.vector.memset(headmask[h * DH:(h + 1) * DH, h * DH:(h + 1) * DH], 1.0))
            v.wait_ge(loaded, NLOAD)
            link(nc.vector.tensor_copy(dstf[:, :], dstf[:, :].bitcast(I32)))
            link(tt(endrow[:, :], dstf[:, 1:C + 1], endrow[:, :], ALU.is_equal))
            link(stt(endrow[:, :], endrow[:, :], FAR, dstf[:, 1:C + 1], ALU.mult, ALU.add))
            kvw = s_wkv.rearrange("p a (h d) -> p (a h) d", d=L0_DH)
            link(red(small[:, 0:2 * KD * L0_HEADS], kvw, AX.X, ALU.add))
            link(ts(small[:, 0:2 * KD * L0_HEADS], small[:, 0:2 * KD * L0_HEADS], 1.0 / L0_DH, None, ALU.mult))
            signal(tt(kvw, kvw, small[:, 0:2 * KD * L0_HEADS].unsqueeze(2).to_broadcast(
                [P, 2 * KD * L0_HEADS, L0_DH]), ALU.subtract))
            for k in range(KD):
                link(ts(w_qkv[:, k, :], w_qkv[:, k, :], col("g_pre", k), None, ALU.mult))
            v.wait_ge(pe_one, 1)
            for c in range(KD):
                link(ts(w_qk[:, c, :], psA[c][:, 0:D1], D ** -0.5, None, ALU.mult))
            signal(ts(qk_bias[:, :], psB[0][:, 0:D1], D ** -0.5, None, ALU.mult))

            v.wait_ge(consts, N_CONST)
            for i, l in ((0, "1"), (1, "2")):
                ts(moe[:, 4 + i, :], col("v" + l, 0, 2 * EX), BN_EPS, None, ALU.add).then_inc(moe_var, 1)
            v.wait_ge(moe_root, 2)
            for i, l in ((0, "1"), (1, "2")):
                scale, bias = moe[:, 2 * i, :], moe[:, 2 * i + 1, :]
                link(tt(scale, col("g" + l, 0, 2 * EX), moe[:, 4 + i, :], ALU.mult))
                link(tt(bias, col("b" + l, 0, 2 * EX), col("m" + l, 0, 2 * EX), ALU.subtract))
                link(tt(bias, bias, scale, ALU.mult))
                last = tt(bias, bias, col("be" + l, 0, 2 * EX), ALU.add)
                if i == 0:
                    link(last)
            last.then_inc(moe_ok, 1)

            def body(g):
                for s in range(2):
                    landed(v, "P1", s, g)
                    if not isinstance(g, int):
                        v.nop(nofuse=True)
                    stats(s, 0, "P1")
                for s in range(2):
                    need(v, "P1", "rstd_ok", 2 * g + s + 1)
                    stored(v, "P1", "a", s, g)
                    normal(s, 0, 256, "xn_ok")
                for s in range(2):
                    t = 2 * g + s
                    need(v, "P1", "ev_a", t + 1)
                    if not isinstance(g, int):
                        v.nop(nofuse=True)
                    h, wk, m8 = nbuf(s, 768, D), nbuf(s, 1024, D), nbuf(s, 4120, 8)
                    for r in range(TOPK_ROUNDS):
                        link(nc.vector.max(m8, h if r == 0 else wk), True)
                        link(nc.vector.match_replace(wk, m8, h if r == 0 else wk, NEG), r < TOPK_ROUNDS - 1)
                    stored(v, "P1", "b", s, g)
                    stt(nbuf(s, 1280, D), wk, NEG, h, ALU.is_equal, ALU.mult).then_inc(sg["hs_ok"], 1)
                    need(v, "P1", "ev_b", t + 1)
                    link(red(nbuf(s, 4128, 16), nbuf(s, 2560, 1024).rearrange("p (h d) -> p h d", d=L0_DH),
                             AX.X, ALU.add))
                    link(ts(nbuf(s, 4128, 16), nbuf(s, 4128, 16), 1.0 / L0_DH, LN_EPS, ALU.mult, ALU.add))
                    tt(nbuf(s, 4144, 8), nbuf(s, 4128, 8), nbuf(s, 4136, 8), ALU.mult).then_inc(sg["sq_red"], 1)
                for s in range(2):
                    t = 2 * g + s
                    need(v, "P1", "rstd_kv", t + 1)
                    need(v, "P1", "dots_ps", t - 1)
                    tt(nbuf(s, 3584, INNER).rearrange("p (h d) -> p h d", d=L0_DH),
                       nbuf(s, 1536 + INNER, INNER).rearrange("p (h d) -> p h d", d=L0_DH),
                       nbuf(s, 4160, 8).unsqueeze(2).to_broadcast([P, L0_HEADS, L0_DH]),
                       ALU.mult).then_inc(sg["v_ok"], 1)
                for s in range(2):
                    t = 2 * g + s
                    need(v, "P1", "dots_ps", t + 1)
                    need(v, "P1", "dots_ok", t)
                    dd = dots[:, :, :].rearrange("p a b -> p (a b)")
                    tt(dd, psB[1][:, 0:INNER], dd, ALU.add).then_inc(sg["dots_ok"], 1)
            ch.groups(NG, body)
            need(v, "P1", "dots_ok", NT)
            phase_end(v, 1)

            link(nc.vector.memset(dots[0:64, :, 64:128], 0.0))
            signal(nc.vector.memset(dots[64:128, :, 0:64], 0.0))
            v.wait_ge(pe_one, 3)
            for c in range(KD):
                signal(tt(w_mix[:, c, :], psA[c][:, 0:D], w_mix[:, c, :], ALU.add))

            def sum_pass(chunk0, r0):
                def body(it):
                    for h in range(2):
                        wait(v, sum_ps, chunk0 + it * B + h * H)
                        nc.vector.tensor_copy(dcol[:, h, :],
                                              dstf[:, bass.ds(it * B + h * H + 1, H)]).then_inc(dcol_ok, 1)
                        for k in range(H):
                            c = it * B + h * H + k
                            if k % 4 == 0:
                                v.wait_ge(row_ps, chunk0 + it * B + h * H + k + 4)
                            Rk = psT[k // 4][:, (k % 4) * P:(k % 4 + 1) * P]
                            ts(PICKM[:, k, :], Rk, dstf[:, bass.ds(c + 1, 1)], wt[:, bass.ds(c, 1)],
                               ALU.is_equal, ALU.mult)
                            ts(CARRYM[96:P, k, :], Rk[96:P, :], dstf[96:P, bass.ds(c, 1)], e127[96:P, :],
                               ALU.is_equal, ALU.mult).then_inc(pickm_ok, 1)
                ch.groups(NB, body)
            nc.vector.memset(GR[:, :, D:D1], 1.0)
            link(nc.vector.memset(ZR[96:P, B - 1, :], 0.0))
            v.wait_ge(consts, N_CONST)
            sum_pass(0, 0)
            phase_end(v, 2)

            def body(g):
                for s in range(2):
                    t = 2 * g + s
                    landed(v, "P3", s, g)
                    ag, c = nbuf(s, 512, D), nbuf(s, 4120, 1)
                    link(ts(c, nbuf(s, 512 + D, 1), 1.0, None, ALU.max))
                    link(nc.vector.reciprocal(c, c))
                    link(stt(ag, ag, c, nbuf(s, 0, D), ALU.mult, ALU.add))
                    link(tt(ag, ag, row("bout"), ALU.add))
                    need(v, "P3", "mm_a", t + 1)
                    need(v, "P3", "sum_ok", t - 1)
                    link(tt(nbuf(s, 1280, D), psA[s][:, 0:D], ag, ALU.add), True)
                    stats(s, 1280, "P3")
                for s in range(2):
                    t = 2 * g + s
                    need(v, "P3", "rstd_ok", t + 1)
                    stored(v, "P3", "a", s, g)
                    ins = normal(s, 1280, 1536, "xn_ok")
                    need(v, "P3", "xn_ok", t + 1)
                    link(stt(nbuf(s, 2048, D), nbuf(s, 1536, D), 1.0, row("wr"), ALU.mult, ALU.mult,
                             accum_out=nbuf(s, 4121, 1)))
                    link(ts(nbuf(s, 4122, 1), nbuf(s, 4121, 1), col("ffn_br"), None, ALU.add))
                    link(nc.vector.tensor_copy(w_all[:, bass.ds(t, 1)], nbuf(s, 4122, 1)))
                    stored(v, "P3", "c", s, g)
                    ts(nbuf(s, 2304, 1), nbuf(s, 4122, 1), padneg[:, bass.ds(t, 1)], None,
                       ALU.add).then_inc(sg["ev_a"], 1)
                    need(v, "P3", "ev_a", t + 1)
                    link(nc.vector.tensor_copy(w_rank[:, bass.ds(t, 1)], nbuf(s, 2304, 1)))
            ch.groups(NG, body)
            phase_end(v, 3)

            def body(g):
                for s in range(2):
                    t = 2 * g + s
                    link(ts(junk, w_bcast, w_rank[:, bass.ds(t, 1)], None, ALU.is_gt, ALU.add,
                            accum_out=nbuf(s, 4130, 1)))
                    link(nc.vector.tensor_copy(above[:, bass.ds(t, 1)], nbuf(s, 4130, 1)))
                    need(v, "P3b", "mm_a", t + 1)
                    stored(v, "P3b", "a", s, g)
                    link(tt(nbuf(s, 2048, D), psA[s][:, 0:D], row("ffn_b2"), ALU.add))
                    ts(nbuf(s, 2048, D), nbuf(s, 2048, D), w_all[:, bass.ds(t, 1)], None,
                       ALU.mult).then_inc(sg["res_ok"], 1)
            ch.groups(NG, body)
            phase_end(v, 4)

            link(ts(pick[:, 1, :], above[:, :], float(KEEP), NEG, ALU.is_ge, ALU.mult))
            link(stt(pick[:, 1, :], w_rank[:, :], -1.0, pick[:, 1, :], ALU.mult, ALU.add))
            assert one[0] == 5
            signal(red(small[:, 0:1], pick[:, 1, :], AX.X, ALU.max))
            v.wait_ge(pe_one, 4)
            signal(red(small[0:1, 1:2], psT[0][0:1, 0:P], AX.X, ALU.max))
            v.wait_ge(pe_one, 5)
            link(ts(small[:, 4:5], psT[0][:, P:P + 1], -1.0, None, ALU.mult))
            signal(ts(pick[:, 0, :], w_rank[:, :], small[:, 4:5], None, ALU.is_equal))
            v.wait_ge(pe_one, 6)
            link(nc.vector.tensor_copy(pick[:, 3, :], psT[1][:, 64:64 + NT]))
            link(nc.vector.memset(pick[:, 2, :], 0.0))
            link(nc.vector.tensor_tensor_scan(pick[:, 1, :], pick[:, 3, :], pick[:, 2, :], 0.0, ALU.add, ALU.add))
            link(tt(pick[:, 1, :], pick[:, 1, :], pick[:, 3, :], ALU.subtract))
            link(tt(pick[:, 1, :], psT[1][:, 0:NT], pick[:, 1, :], ALU.add))
            link(tt(pick[:, 1, :], pick[:, 1, :], pick[:, 0, :], ALU.mult))
            link(tt(pick[:, 1, :], pick[:, 1, :], above[:, :], ALU.add))
            signal(ts(sel[:, :], pick[:, 1, :], float(KEEP), None, ALU.is_lt))
            signal(nc.vector.memset(kmax[:, :], NEG))

            def body(g):
                for s in range(2):
                    t = 2 * g + s
                    landed(v, "P4", s, g)
                    stored(v, "P4", "a", s, g)
                    stt(nbuf(s, 512, D), nbuf(s, 256, D), sel[:, bass.ds(t, 1)], nbuf(s, 0, D),
                        ALU.mult, ALU.add).then_inc(sg["sum_ok"], 1)
                    need(v, "P4", "sum_ok", t + 1)
                    if not isinstance(g, int):
                        v.nop(nofuse=True)
                    stats(s, 512, "P4")
                for s in range(2):
                    t = 2 * g + s
                    need(v, "P4", "rstd_ok", t + 1)
                    stored(v, "P4", "b", s, g)
                    normal(s, 512, 768, "xn_ok")
                    need(v, "P4", "xn_ok", t + 1)
                    link(stt(nbuf(s, 2816, D), nbuf(s, 768, D), 1.0, nbuf(s, 768, D), ALU.mult, ALU.mult,
                             accum_out=nbuf(s, 4111, 1)))
                    ts(nbuf(s, 4112, 1), nbuf(s, 4111, 1), 1e-24, None, ALU.max).then_inc(sg["var2_ok"], 1)
                for s in range(2):
                    t = 2 * g + s
                    need(v, "P4", "mm_a", t + 1)
                    stored(v, "P4", "c", s, g)
                    tt(nbuf(s, 1280, D1), psA[s][:, 0:D1], qk_bias[:, :], ALU.add).then_inc(sg["ev_a"], 1)
                    need(v, "P4", "rstd2_ok", t + 1)
                    link(ts(nbuf(s, 4115, 1), nbuf(s, 4114, 1), float(D) ** 0.5, None, ALU.mult))
                    need(v, "P4", "mm_b", t + 1)
                    stored(v, "P4", "d", s, g, 2)
                    qkv = psB[s]
                    ts(nbuf(s, 1792 + HID, HID), qkv[:, 2 * HID:3 * HID], nbuf(s, 4115, 1), None, ALU.mult)
                    ts(nbuf(s, 1792, HID), qkv[:, HID:2 * HID], nbuf(s, 4115, 1), padneg[:, bass.ds(t, 1)],
                       ALU.mult, ALU.add).then_inc(sg["ev_b"], 1)
                    need(v, "P4", "ev_b", t + 1)
                    need(v, "P4", "hs_ok", t)
                    tt(kmax[:, :], kmax[:, :], nbuf(s, 1792, HID), ALU.max).then_inc(sg["hs_ok"], 1)
                    q3 = nbuf(s, 2048, HID).rearrange("p (h d) -> p h d", d=DH)
                    link(ts(nbuf(s, 2048, HID), qkv[:, 0:HID], nbuf(s, 4115, 1), None, ALU.mult))
                    link(red(nbuf(s, 4120, HEADS), q3, AX.X, ALU.max))
                    tt(q3, q3, nbuf(s, 4120, HEADS).unsqueeze(2).to_broadcast([P, HEADS, DH]),
                       ALU.subtract).then_inc(sg["q_max"], 1)
                for s in range(2):
                    t = 2 * g + s
                    need(v, "P4", "q_exp", t + 1)
                    e3 = nbuf(s, 2176, HID).rearrange("p (h d) -> p h d", d=DH)
                    link(red(nbuf(s, 4124, HEADS), e3, AX.X, ALU.add))
                    link(nc.vector.reciprocal(nbuf(s, 4124, HEADS), nbuf(s, 4124, HEADS)))
                    link(ts(nbuf(s, 4124, HEADS), nbuf(s, 4124, HEADS), DH ** -0.5, None, ALU.mult))
                    tt(nbuf(s, 2560, HID).rearrange("p (h d) -> p h d", d=DH), e3,
                       nbuf(s, 4124, HEADS).unsqueeze(2).to_broadcast([P, HEADS, DH]),
                       ALU.mult).then_inc(sg["res_ok"], 1)
            ch.groups(NG, body)
            need(v, "P4", "hs_ok", NT)
            phase_end(v, 5)

            v.wait_ge(pe_one, 7)
            link(red(small[:, 2:3], psT[0][:, 0:P], AX.X, ALU.max))
            link(red(small[:, 5:6], col("mem_k", 0, MEM), AX.X, ALU.max))
            signal(tt(small[:, 2:3], small[:, 2:3], small[:, 5:6], ALU.max))
            signal(ts(small[:, 3:4], small[:, 2:3], -1.0, None, ALU.mult))
            v.wait_ge(pe_one, 8)
            link(nc.vector.tensor_copy(kneg[:, :], psT[0][:, P:2 * P]))
            v.wait_ge(pe_one, 9)
            signal(nc.vector.tensor_copy(nbuf(0, 1024, P)[0:MEM, :], psT[1][0:MEM, 0:P]))
            v.wait_ge(pe_one, 10)
            link(nc.vector.tensor_copy(ctxv[:, :], psT[1][:, P:P + HID + 1]))
            for s in range(2):
                link(nc.vector.memset(nbuf(s, 640 + HID, 1), 1.0))

            def body(g):
                for s in range(2):
                    t = 2 * g + s
                    landed(v, "P4b", s, g)
                    need(v, "P4b", "mm_a", t - 1)
                    nc.vector.tensor_copy(nbuf(s, 640, HID), nbuf(s, HID, HID))
                    need(v, "P4b", "q_exp", t - 1)
                    tt(nbuf(s, 256, P), nbuf(s, 0, P), kneg[:, :], ALU.subtract).then_inc(sg["q_max"], 1)
                for s in range(2):
                    t = 2 * g + s
                    need(v, "P4b", "mm_a", t + 1)
                    need(v, "P4b", "ev_a", t)
                    tt(ctxv[:, :], psA[s][:, 0:HID + 1], ctxv[:, :], ALU.add).then_inc(sg["ev_a"], 1)
            ch.groups(NG, body)
            need(v, "P4b", "ev_a", NT)
            signal(nc.vector.reciprocal(small[:, 6:7], ctxv[:, HID:HID + 1]))
            signal(ts(ctxn[:, 0, :], ctxv[:, 0:HID], small[:, 6:7], None, ALU.mult))
            signal(tt(ctxn[:, 0, :], ctxn[:, 0, :], headmask[:, :], ALU.mult))
            v.wait_ge(pe_one, 12)
            link(nc.vector.tensor_copy(w_m2[:, :], psA[0][:, 0:D]))
            phase_end(v, 6)

            v.wait_ge(misc, 48)
            link(nc.vector.memset(GR[:, :, D:D1], 1.0))
            link(nc.vector.tensor_copy(s_c, dst_r[:, :]))
            link(tt(s_prev, s_c, s_a.bitcast(I32), ALU.is_equal))
            link(tt(s_next, s_c, s_b.bitcast(I32), ALU.is_equal))

            def body(it):
                for h in range(2):
                    for k in range(H):
                        s = h * H + k
                        v.wait_ge(g_sem[s], 16 * NB + it * 16 + 16)
                        v.wait_ge(z_sem[s], 16 * NB + it * 16 + 16)
                        stt(nbuf(s % 2, 0, D1), GR[:, s, :], 1.0, ZR[:, s, :], ALU.mult, ALU.mult,
                            accum_out=scol[:, h, k:k + 1]).then_inc(scored, 1)
                        v.wait_ge(scored, it * B + s + 1)
                    link(nc.vector.tensor_copy(score[:, bass.ds(it * B + h * H, H)], scol[:, h, :]))
            ch.groups(NB, body)
            link(stt(s_a, ewt[:, :], col("we"), score, ALU.mult, ALU.add))
            link(ts(score, s_a, col("be"), None, ALU.add))

            def scan(dst, keep, x, op0, op1, neutral, back, i):
                def d(ap):
                    return ap[:, ::-1] if back else ap
                link(nc.vector.tensor_tensor_scan(d(dst), d(keep), d(x), neutral, op0, op1))
                link(nc.vector.tensor_copy(small[:, 16:17], dst[:, 0:1] if back else dst[:, C - 1:C]))
                red(small[:, 17:18], keep, AX.X, ALU.min).then_inc(scan_ok, 1)
                v.wait_ge(pe_one, 13 + 2 * i)
                link(nc.vector.tensor_copy(srow[0:1, 0, :], psT[0][0:1, 0:P]))
                link(nc.vector.tensor_copy(srow[0:1, 1, :], psT[0][0:1, P:2 * P]))
                r = (lambda k: srow[0:1, k, ::-1]) if back else (lambda k: srow[0:1, k, :])
                link(nc.vector.tensor_tensor_scan(r(2), r(1), r(0), neutral, op0, op1))
                link(nc.vector.memset(srow[0:1, 3, :], neutral))
                into, of = (slice(0, P - 1), slice(1, P)) if back else (slice(1, P), slice(0, P - 1))
                nc.vector.tensor_copy(srow[0:1, 3, into], srow[0:1, 2, of]).then_inc(scan_ok, 1)
                v.wait_ge(pe_one, 14 + 2 * i)
                link(nc.vector.tensor_copy(small[:, 18:19], psT[1][:, 0:1]))
                link(nc.vector.tensor_tensor_scan(d(dst), d(keep), d(x), small[:, 18:19], op0, op1))

            link(ts(s_a, s_prev, 1.0, BIG, ALU.subtract, ALU.mult))
            scan(s_b, s_a, score, ALU.add, ALU.max, -BIG, False, 0)
            link(ts(s_a, s_next, 1.0, BIG, ALU.subtract, ALU.mult))
            scan(s_c, s_a, s_b, ALU.add, ALU.max, -BIG, True, 1)
            tt(s_c, score, s_c, ALU.subtract).then_inc(shifted, 1)
            v.wait_ge(act_one, 4)
            scan(s_b, s_prev, s_c, ALU.mult, ALU.add, 0.0, False, 2)
            link(ts(s_a, s_next, -1.0, 1.0, ALU.mult, ALU.add))
            link(tt(s_b, s_b, s_a, ALU.mult))
            scan(s_a, s_next, s_b, ALU.mult, ALU.add, 0.0, True, 3)
            link(ts(s_a, s_a, 1e-12, None, ALU.max))
            link(nc.vector.reciprocal(s_a, s_a))
            tt(s_c, s_c, s_a, ALU.mult).then_inc(attention_ok, 1)
            phase_end(v, 7)
            link(nc.vector.memset(GR[:, :, D:D1], 1.0))
            link(nc.vector.memset(ZR[96:P, B - 1, :], 0.0))
            sum_pass(C, 0)
            phase_end(v, 8)

            def body(g):
                for s in range(2):
                    t = 2 * g + s
                    landed(v, "P6", s, g)
                    need(v, "P6", "mm_a", t + 1)
                    r, m, xn2 = nbuf(s, 2944, D), nbuf(s, 1664, D), nbuf(s, 256, D)
                    link(tt(r, psA[s][:, 0:D], row("bs"), ALU.add))
                    tt(m, psA[s][:, D:2 * D], row("b_out"), ALU.add).then_inc(sg["ev_a"], 1)
                    need(v, "P6", "ev_a", t + 1)
                    link(stt(r, row("bv"), nbuf(s, 512 + D, 1), r, ALU.mult, ALU.add))
                    link(tt(r, r, xn2, ALU.add), True)
                    link(stt(nbuf(s, 3200, D), m, 1.0, m, ALU.mult, ALU.mult, accum_out=nbuf(s, 4111, 1)))
                    ts(nbuf(s, 4112, 1), nbuf(s, 4111, 1), 1e-24, None, ALU.max).then_inc(sg["sq_red"], 1)
                    stats(s, 2944, "P6")
                for s in range(2):
                    t = 2 * g + s
                    z, m = nbuf(s, 1920, D), nbuf(s, 1664, D)
                    need(v, "P6", "rstd_ok", t + 1)
                    link(normal(s, 2944, 1920, None))
                    link(tt(z, z, row("g1"), ALU.mult))
                    tt(z, z, row("b1"), ALU.add).then_inc(sg["xn_ok"], 1)
                    need(v, "P6", "rstd_kv", t + 1)
                    link(ts(nbuf(s, 4115, 1), nbuf(s, 4114, 1), float(D) ** 0.5, None, ALU.mult))
                    link(stt(m, m, nbuf(s, 4115, 1), row("g_out"), ALU.mult, ALU.mult))
                    link(tt(m, m, nbuf(s, 256, D), ALU.add))
                for s in range(2):
                    t = 2 * g + s
                    u = nbuf(s, 3200, D)
                    need(v, "P6", "mm_b", t + 1)
                    need(v, "P6", "xn_ok", t + 1)
                    link(tt(u, psT[s][:, D:2 * D], row("b_ff2"), ALU.add))
                    link(tt(u, u, nbuf(s, 1920, D), ALU.add), True)
                    stats(s, 3200, "P6", "var2_ok")
                for s in range(2):
                    t = 2 * g + s
                    u, x3 = nbuf(s, 3200, D), nbuf(s, 3584, D)
                    need(v, "P6", "rstd2_ok", t + 1)
                    link(normal(s, 3200, 3200, None))
                    link(tt(u, u, row("g2"), ALU.mult))
                    link(tt(u, u, row("b2"), ALU.add))
                    link(tt(u, u, nbuf(s, 1664, D), ALU.add))
                    stored(v, "P6", "a", s, g)
                    tt(x3, u, nbuf(s, 0, D), ALU.add).then_inc(sg["res_ok"], 1)
                    need(v, "P6", "res_ok", t + 1)
                    if not isinstance(g, int):
                        v.nop(nofuse=True)
                    stats(s, 3584, "P6", "v_ok")
                for s in range(2):
                    t = 2 * g + s
                    need(v, "P6", "rstd3_ok", t + 1)
                    stored(v, "P6", "b", s, g)
                    normal(s, 3584, 3840, "dots_ok")
            ch.groups(NG, body)
            phase_end(v, 9)

            def body(g):
                for s in range(2):
                    wait(v, lo_ok, g * 2 * EX - 1 + s)
                    need(v, "P7", "mm_a", 2 * g + s + 1)
                    lg = nbuf(s, 4120, EX)
                    link(tt(lg, psT[s][:, D:D + EX], col("moe_br", 0, EX), ALU.add))
                    link(red(nbuf(s, 4137, 1), lg, AX.X, ALU.max))
                    ts(lg, lg, nbuf(s, 4137, 1), None, ALU.subtract).then_inc(sg["q_max"], 1)
                for s in range(2):
                    need(v, "P7", "q_exp", 2 * g + s + 1)
                    link(nc.vector.reciprocal(nbuf(s, 4141, 1), nbuf(s, 4140, 1)))
                    ts(nbuf(s, 4120, EX), nbuf(s, 4128, EX), nbuf(s, 4141, 1), None,
                       ALU.mult).then_inc(sg["sum_ok"], 1)
                for s in range(2):
                    t = 2 * g + s
                    landed(v, "P7", s, g)
                    need(v, "P7", "mm_b", t + 1)
                    tt(nbuf(s, 1536, D), psA[s][:, 0:D], nbuf(s, 0, D), ALU.add).then_inc(sg["ev_a"], 1)
                for e in range(EX):
                    for s in range(2):
                        n = g * 2 * EX + e * 2 + s
                        wait(v, lo_ps, n + 1)
                        if e == 0:
                            need(v, "P7", "ev_a", 2 * g + s + 1)
                        else:
                            v.wait_ge(lo_ok, n - 1)
                        dst = 1536
                        if e == EX - 1:
                            stored(v, "P7", "a", s, g)
                            dst = 1792
                        stt(nbuf(s, dst, D), psA[s][:, 0:D], nbuf(s, 4120 + e, 1), nbuf(s, 1536, D),
                            ALU.mult, ALU.add).then_inc(lo_ok, 1)
            ch.groups(NG, body)


def kernel(**inputs):
    import concourse.bacc as bacc
    from concourse.bass_utils import run_bass_kernel_spmd

    x = {k: np.asarray(v) for k, v in inputs.items()}

    def fold_rows(w):
        k = w.shape[0] // P
        return w.reshape(k, P, w.shape[1]).transpose(1, 0, 2).reshape(P, k * w.shape[1])

    def columns(v):
        return v.reshape(-1, P).T

    def every(v):
        return np.broadcast_to(v.reshape(1, -1), (P, v.size))

    def experts(w):
        return w.reshape(EX, KD, P, D).transpose(2, 0, 1, 3).reshape(P, EX * KD * D)

    pad = C * P - E
    src = np.concatenate([x["src"], np.zeros(pad, np.int32)])
    dst = np.concatenate([x["dst"], np.full(pad, N, np.int32)])
    none = np.full(1, -1, np.int32)
    prev, nxt = np.concatenate([none, dst[:-1]]), np.concatenate([dst[1:], none])
    ew = np.concatenate([x["edge_weight"], np.zeros(pad, np.float32)])
    f = "L1_ffn_"
    parts = {"ffn_b1": columns(x["L0_ffn_b1"]), "b_ff1": columns(x["L1_gnn_b_ff1"]),
             "g_pre": columns(x["L1_mix_g_pre"]), "bq": columns(x["L1_gnn_bq"]),
             "ffn_br": every(x["L0_ffn_br"]), "we": every(x["L1_gnn_we"]), "be": every(x["L1_gnn_be"]),
             "moe_br": every(x[f + "br"]), "mem_k": x["L1_mix_mem_kv"][0].reshape(HID, MEM)}
    for n in ("b1", "g1", "be1", "m1", "v1", "b2", "g2", "be2", "m2", "v2"):
        parts[n] = columns(x[f + n].reshape(-1))
    rowv = {"bout": "L0_mix_bout", "wr": "L0_ffn_wr", "ffn_b2": "L0_ffn_b2", "bs": "L1_gnn_bs", "bv": "L1_gnn_bv",
            "g1": "L1_gnn_g1", "b1": "L1_gnn_b1", "g2": "L1_gnn_g2", "b2": "L1_gnn_b2",
            "b_ff2": "L1_gnn_b_ff2", "b_out": "L1_mix_b_out", "g_out": "L1_mix_g_out"}
    arrays = {
        "x": np.concatenate([x["x"], np.zeros((NP - N, D), np.float32)]),
        "src_c": src.reshape(C, P).T, "src_r": src.reshape(P, C), "dst_r": dst.reshape(P, C),
        "dprev_r": prev.reshape(P, C), "dnext_r": nxt.reshape(P, C),
        "dst_c": np.concatenate([np.full((P, 1), -1, np.int32), dst.reshape(C, P).T], 1),
        "dstn_c": nxt.reshape(C, P).T, "ew_r": ew.reshape(P, C),
        "rows": np.concatenate([every(x[rowv[n]]) for n in ROWS], 1),
        "cols": np.concatenate([parts[n] for n in COLS], 1),
        "W_neigh": fold_rows(x["L0_gnn_W_neigh"]), "W_self": fold_rows(x["L0_gnn_W_self"]),
        "Wkv": fold_rows(x["L0_mix_Wqkv"][INNER:].T), "Wq": fold_rows(x["L0_mix_Wqkv"][:INNER]),
        "WoutT": fold_rows(x["L0_mix_Wout"].T), "w1": fold_rows(x["L0_ffn_w1"]), "w2": fold_rows(x["L0_ffn_w2"]),
        "wqT": fold_rows(x["L1_gnn_wq"].T),
        "wkTb": fold_rows(np.concatenate([x["L1_gnn_wk"].T, x["L1_gnn_bk"].reshape(D, 1)], 1)),
        "w_qkv": fold_rows(x["L1_mix_w_qkv"]), "w_out": x["L1_mix_w_out"],
        "wv": fold_rows(x["L1_gnn_wv"]), "ws": fold_rows(x["L1_gnn_ws"]),
        "w_ff1": fold_rows(x["L1_gnn_w_ff1"]), "w_ff2": fold_rows(x["L1_gnn_w_ff2"]),
        "Wr": fold_rows(x[f + "Wr"]), "bo": x[f + "bo"],
        "mem_v": x["L1_mix_mem_kv"][1].reshape(HID, MEM).T,
        "W1": experts(x[f + "W1"]), "W2": experts(x[f + "W2"]), "Wo": experts(x[f + "Wo"]),
    }
    arrays = {"in_" + k: np.ascontiguousarray(v) for k, v in arrays.items()}
    nc = bacc.Bacc("TRN2", target_bir_lowering=False, num_devices=1)
    aps = {k[3:]: nc.dram_tensor(k, v.shape, mybir.dt.from_np(v.dtype), kind="ExternalInput").ap()
           for k, v in arrays.items()}
    out = nc.dram_tensor("out_0", (N, D), F32, kind="ExternalOutput").ap()
    build(nc, aps, out)
    r = run_bass_kernel_spmd(nc, [arrays], core_ids=[0])
    return r.results[0]["out_0"]
```

```python
import numpy as np
import concourse.bass as bass
import concourse.mybir as mybir
from contextlib import ExitStack

F32 = mybir.dt.float32
I32 = mybir.dt.int32
BF16 = mybir.dt.bfloat16
ALU = mybir.AluOpType
ACT = mybir.ActivationFunctionType
AX = mybir.AxisListType

P = 128
N = 6250
E = 206250
D = 256
KD = D // P
D1 = D + 1
NT = 50
NG = NT // 2
NP = NT * P
TAIL = N - (NT - 2) * P
EC = P - 1
H = 8
B = 2 * H
NB = -(-E // (EC * B))
C = B * NB
CT = -(-C // P)
CR = -(-C * EC // P)
CARRY_LAG = 5
LAG = 4
FEW = 16
ZPER = 11
SUMROWS = NT * ZPER * P
ZROW = SUMROWS - P
assert C * FEW + (N + 1) // FEW * (P - FEW) <= ZROW
FULL = 1 << 17
assert FULL > SUMROWS and FULL > NT * P
LK = 5
TOPK_ROUNDS = 32 // 8
L0_HEADS, L0_DH = 8, 64
INNER = L0_HEADS * L0_DH
PAIRS = INNER // P
FF = 4 * D
KF = FF // P
KEEP = max(1, int(0.5 * N)) - 1
HEADS, DH, MEM = 4, 32, 4
HID = HEADS * DH
FF1 = 2 * D
K1 = FF1 // P
EX = 8
LN_EPS = 1e-5
BN_EPS = 1e-3
BIG = 1e30
FAR = 65536.0
NEG = -3.0e38

ROWS = ["bout", "wr", "ffn_b2", "bs", "bv", "g1", "b1", "g2", "b2", "b_ff2", "b_out", "g_out"]
COLS = {"ffn_b1": KF, "b_ff1": K1, "g_pre": KD, "bq": KD, "ffn_br": 1, "we": 1, "be": 1, "moe_br": EX,
        "b1": 2 * EX, "g1": 2 * EX, "be1": 2 * EX, "m1": 2 * EX, "v1": 2 * EX,
        "b2": 2 * EX, "g2": 2 * EX, "be2": 2 * EX, "m2": 2 * EX, "v2": 2 * EX, "mem_k": MEM}
ROW = {n: i for i, n in enumerate(ROWS)}
COL, NCOL = {}, 0
for _n, _k in COLS.items():
    COL[_n] = NCOL
    NCOL += _k


def wait(eng, sem, value):
    if isinstance(value, int) and value <= 0:
        return
    eng.wait_ge(sem, value)


class Chain:

    def __init__(self, eng, sem):
        self.eng, self.sem, self.base, self.k, self.g, self.per = eng, sem, 0, 0, None, 0

    def link(self, ins, fence=False):
        self.k += 1
        ins.then_inc(self.sem, 1)
        v = self.base + self.k
        if self.g is not None:
            v = self.base + (self.g - self.first) * self.per + self.k
        self.eng.wait_ge(self.sem, v)
        if fence and self.g is not None:
            self.eng.nop(nofuse=True)

    def groups(self, count, body, peel=1):
        for g in range(peel):
            start = self.k
            body(g)
        self.per = self.k - start
        self.base, self.k, self.first = self.base + self.k, 0, peel
        with self.eng.Fori(peel, count) as g:
            self.g = g
            body(g)
            self.g = None
        assert self.k == self.per
        self.base, self.k = self.base + (count - peel) * self.per, 0


def plain_groups(eng, count, body):
    body(0)
    with eng.Fori(1, count) as g:
        body(g)


def build(nc, a, out):
    ctx = ExitStack()
    with ctx:
        def sb(name, shape, dt=F32):
            return ctx.enter_context(nc.sbuf_tensor(name, shape, dt))

        def sem(name):
            return ctx.enter_context(nc.semaphore(name))

        def table(name, width):
            return nc.dram_tensor(name, (NP, width), F32).ap()

        t_xn, t_hs, t_xn1, t_xs, t_y = (table(n, D) for n in ("t_xn", "t_hs", "t_xn1", "t_xs", "t_y"))
        t_x2, t_xn2, t_x3, t_xn3 = (table(n, D) for n in ("t_x2", "t_xn2", "t_x3", "t_xn3"))
        t_qk = table("t_qk", D1)
        t_sum = nc.dram_tensor("t_sum", (SUMROWS, D1), F32).ap()
        t_chunk = nc.dram_tensor("t_chunk", (CT * P, 2 * P), F32).ap()
        t_carry = nc.dram_tensor("t_carry", (C + 1, D1), F32).ap()
        t_ni = nc.dram_tensor("t_ni", (2, CT * P), I32).ap()
        t_kv, t_q = table("t_kv", 2 * HID), table("t_q", HID)
        t_w = nc.dram_tensor("t_w", (1, NP), F32).ap()
        t_att = nc.dram_tensor("t_att", (1, CR * P), F32).ap()
        t_score = nc.dram_tensor("t_score", (1, CR * P), F32).ap()

        src_c = sb("src_c", [P, C], I32)
        slot_c = sb("slot_c", [P, C])
        wt = sb("wt", [P, C])
        reg_s = sb("reg_s", [P, 5 * CR + C])
        reg_g = sb("reg_g", [P, 2 * B * D1 + B * P])
        w_mix = sb("w_mix", [P, KD, D])
        w_qk = sb("w_qk", [P, KD, D1])
        w_qkv = sb("w_qkv", [P, KD, 3 * HID])
        w_out = sb("w_out", [P, D])
        w_m2 = sb("w_m2", [P, D])
        w_v = sb("w_v", [P, KD, D])
        w_s = sb("w_s", [P, KD, D])
        w_ff1 = sb("w_ff1", [P, KD, FF1])
        w_ff2 = sb("w_ff2", [P, K1, D])
        w_r = sb("w_r", [P, KD, EX])
        w_bo = sb("w_bo", [EX, D])
        mem_v = sb("mem_v", [MEM, HID + 1])
        rows = sb("rows", [P, len(ROWS), D])
        cols = sb("cols", [P, NCOL])
        qk_bias = sb("qk_bias", [P, D1])
        nb = sb("nb", [P, 2, 4200])
        ident = sb("ident", [P, P])
        lower = sb("lower", [P, P])
        ones = sb("ones", [P, P])
        riota = sb("riota", [P, P])
        piota = sb("piota", [P, 1])
        iotai = sb("iotai", [P, P + 1 + NT], I32)
        nid = sb("nid", [P, 2, NT])
        look = sb("look", [P, 6, NT])
        cidx = sb("cidx", [P, NT], I32)
        sumrow = sb("sumrow", [P, NT], I32)
        carryrow = sb("carryrow", [P, NT], I32)
        qrow = sb("qrow", [P, NT], I32)
        chunkn = sb("chunkn", [P, 5, 2 * CT])
        chunki = sb("chunki", [P, 2, CT], I32)
        nrow = sb("nrow", [1, 2, CT * P], I32)
        lidx = sb("lidx", [P, 2, LK], I32)
        tidx = sb("tidx", [P, 4], I32)
        half = sb("half", [P, 16])
        headmask = sb("headmask", [P, P])
        padneg = sb("padneg", [P, NT])
        dots = sb("dots", [P, PAIRS, P])
        fold = sb("fold", [P, PAIRS, D])
        w_all = sb("w_all", [P, NT])
        w_rank = sb("w_rank", [P, NT])
        above = sb("above", [P, NT])
        sel = sb("sel", [P, NT])
        pick = sb("pick", [P, 4, NT])
        kmax = sb("kmax", [P, HID])
        kneg = sb("kneg", [P, HID])
        ctxv = sb("ctxv", [P, HID + 1])
        ctxn = sb("ctxn", [P, 2, P])
        small = sb("small", [P, 64])
        srow = sb("srow", [1, 4, P])
        moe = sb("moe", [P, 6, 2 * EX])
        sidx = sb("sidx", [P, 2, H], I32)
        dcol = sb("dcol", [P, 2, H])
        scol = sb("scol", [P, B])
        zrow = sb("zrow", [P, D1])

        def view(reg, off, *dims):
            n = 1
            for d in dims:
                n *= d
            v = reg[:, off:off + n]
            if len(dims) == 2:
                v = v.rearrange("p (a b) -> p a b", b=dims[1])
            if len(dims) == 3:
                v = v.rearrange("p (a b c) -> p a b c", b=dims[1], c=dims[2])
            return v

        s_wneigh = view(reg_s, 0, KD, D)
        s_wkv = view(reg_s, 512, KD, 2 * INNER)
        s_wq = view(reg_s, 2560, PAIRS, D)
        s_wout = view(reg_s, 3584, PAIRS, D)
        s_w1 = view(reg_s, 4608, KD, FF)
        s_w2 = view(reg_s, 6656, KF, D)
        s_wqT = view(reg_s, 8704, KD, D)
        s_wkT = fold[:, :, :].rearrange("p a b -> p (a b)")[:, 0:KD * D1].rearrange("p (a b) -> p a b", b=D1)
        score, s_prev, s_next, s_a, s_b, s_c = (view(reg_s, i * CR, CR) for i in range(6))
        score_c = view(reg_s, 5 * CR, C)
        s_wo = view(reg_s, 0, EX, KD, D)
        GR = view(reg_g, 0, B, D1)
        ZR = view(reg_g, B * D1, B, D1)
        SEL = view(reg_g, 2 * B * D1, B, P)
        c_dst, c_cum, c_slot = (view(reg_g, i * CT * P, CT, P) for i in range(3))
        firsts = view(reg_g, 3 * CT * P, C)
        sign_junk = reg_g[:, 3 * CT * P + C:3 * CT * P + C + C // 2].bitcast(BF16)
        zeros = reg_g[:, 3 * CT * P + C + C // 2:3 * CT * P + C + C // 2 + ZPER * D1]
        found = view(reg_g, 0, 2 * LK, 2 * P)
        match = view(reg_g, 2 * LK * 2 * P, LK, EC)
        w_bcast = view(reg_g, 0, NP)
        junk = reg_g[:, NP:NP + NP // 2].bitcast(BF16)
        g_w1 = view(reg_g, 0, EX, KD, D)
        g_w2 = view(reg_g, 4096, EX, KD, D)

        carried = view(reg_g, 8192, 2, D1)

        psT = [ctx.enter_context(nc.psum_tensor(f"psT{i}", [P, 512], F32)) for i in range(2)]
        psA = [ctx.enter_context(nc.psum_tensor(f"psA{i}", [P, 512], F32)) for i in range(2)]
        psB = [ctx.enter_context(nc.psum_tensor(f"psB{i}", [P, 1024], F32)) for i in range(2)]
        psZ = [psA[0], psA[1], psB[0], psB[1]]

        def nbuf(s, off, n):
            return nb[:, s, off:off + n]

        def row(name):
            return rows[:, ROW[name], :]

        def col(name, i=0, n=1):
            return cols[:, COL[name] + i:COL[name] + i + n]

        loaded = sem("loaded")
        consts = sem("consts")
        phase = sem("phase")
        dve_step, pool_step, act_step = sem("dve_step"), sem("pool_step"), sem("act_step")
        ld = [sem("ld0"), sem("ld1")]
        sta = [sem("sta0"), sem("sta1")]
        stb = [sem("stb0"), sem("stb1")]
        stc = [sem("stc0"), sem("stc1")]
        std = [sem("std0"), sem("std1")]
        summed = sem("summed")
        c_sem = [sem("c_sem0"), sem("c_sem1")]
        ld_sum = [sem("ld_sum0"), sem("ld_sum1")]
        st_qk = [sem("st_qk0"), sem("st_qk1")]
        zeroed = sem("zeroed")
        lk, lk_ps, lk_g, lk_ok, lk_st, turned_ps, turned_sb = (
            sem(n) for n in ("lk", "lk_ps", "lk_g", "lk_ok", "lk_st", "turned_ps", "turned_sb"))
        lk_in = [sem("lk_in0"), sem("lk_in1")]
        g_sem = [sem(f"gather{i}") for i in range(B)]
        z_sem = [sem(f"scatter{i}") for i in range(B)]
        misc = sem("misc")
        out_done = sem("out_done")

        class Base:
            pass

        names = ["xT_ps", "xT_sb", "var_ok", "rstd_ok", "xn_ok", "mm_a", "mm_b", "ev_a", "ev_b", "hs_ok",
                 "sq_red", "rstd_kv", "v_ok", "dots_ps", "dots_ok", "sum_ok", "res_ok", "tT_ps", "tT_sb",
                 "ff_ps", "ff_sb", "q_max", "q_exp", "var2_ok", "rstd2_ok", "rstd3_ok"]
        sg = {n: sem(n) for n in names}
        pe_one, dve_one, act_one = sem("pe_one"), sem("dve_one"), sem("act_one")
        idx_ok, dcol_ok, row_ps, sel_ok, sum_ps, sum_sb, carry_ok, scored = (
            sem(n) for n in ("idx_ok", "dcol_ok", "row_ps", "sel_ok", "sum_ps", "sum_sb", "carry_ok", "scored"))
        scan_ok, shifted, attention_ok, moe_var, moe_root, moe_ok, q_clear, ones_ok, tidx_ok, scores_ok = (
            sem(n) for n in ("scan_ok", "shifted", "attention_ok", "moe_var", "moe_root", "moe_ok", "q_clear",
                             "ones_ok", "tidx_ok", "scores_ok"))
        l1_ps, l1_sb, l2_ps, l2_sb, lo_ps, lo_ok = (
            sem(n) for n in ("l1_ps", "l1_sb", "l2_ps", "l2_sb", "lo_ps", "lo_ok"))

        used = {"P1": ["xT_ps", "xT_sb", "var_ok", "rstd_ok", "xn_ok", "mm_a", "mm_b", "ev_a", "ev_b", "hs_ok",
                       "sq_red", "rstd_kv", "v_ok", "dots_ps", "dots_ok"],
                "P3": ["xT_ps", "xT_sb", "var_ok", "rstd_ok", "xn_ok", "mm_a", "ev_a", "sum_ok"],
                "P3b": ["xT_ps", "xT_sb", "mm_b", "ev_b", "mm_a", "res_ok"],
                "P4": ["xT_ps", "xT_sb", "var_ok", "rstd_ok", "xn_ok", "mm_a", "ev_a", "mm_b", "ev_b",
                       "q_max", "q_exp", "res_ok", "var2_ok", "rstd2_ok", "sum_ok", "hs_ok"],
                "P4b": ["q_max", "q_exp", "mm_a", "ev_a"],
                "P6": ["xT_ps", "xT_sb", "mm_a", "ev_a", "var_ok", "rstd_ok", "xn_ok", "tT_ps", "tT_sb",
                       "ff_ps", "ff_sb", "mm_b", "var2_ok", "rstd2_ok", "sq_red", "rstd_kv", "res_ok",
                       "dots_ok", "v_ok", "rstd3_ok"],
                "P7": ["xT_ps", "xT_sb", "mm_a", "q_max", "q_exp", "tT_ps", "tT_sb", "res_ok", "ev_a", "mm_b",
                       "sum_ok"]}
        bases, count = {}, {n: 0 for n in names}
        for ph, ns in used.items():
            bases[ph] = dict(count)
            for n in ns:
                count[n] += NT
        ld_base, k = {}, 0
        for ph, n in (("P1", 1), ("P3", 2), ("P3b", 1), ("P4", 2), ("P4b", 1), ("P6", 3), ("P7", 2)):
            ld_base[ph] = (k, 16 * n)
            k += 16 * n * NG
        st_used = {"P1": "ab", "P3": "abc", "P3b": "a", "P4": "abd", "P4b": "", "P6": "ab", "P7": "a"}
        st_base, cnt = {}, {c: 0 for c in "abcd"}
        st_extra = {"P4": {"d": 1}}
        for ph, cs in st_used.items():
            st_base[ph] = dict(cnt)
            for c in cs:
                cnt[c] += 16 * NG * (1 + st_extra.get(ph, {}).get(c, 0))
        stores = {"a": sta, "b": stb, "c": stc, "d": std}

        def sig(ph, n):
            assert n in used[ph], (ph, n)
            return sg[n], bases[ph][n]

        def need(eng, ph, n, value):
            if isinstance(value, int) and value <= 0:
                return
            s, b = sig(ph, n)
            eng.wait_ge(s, b + value)

        def stored(eng, ph, c, s, g, per=1):
            assert c in st_used[ph]
            if isinstance(g, int) and g <= 0:
                return
            eng.wait_ge(stores[c][s], st_base[ph][c] + 16 * per * g)

        def landed(eng, ph, s, g):
            b, per = ld_base[ph]
            eng.wait_ge(ld[s], b + per * (g + 1))

        tiles_before = {"P3": 0, "P6": NT}

        def sums_complete(eng, ph, t):
            eng.wait_ge(summed, tiles_before[ph] + t + 1)

        def qk_stored(eng, s, g):
            if isinstance(g, int) and g <= 0:
                return
            eng.wait_ge(st_qk[s], 16 * g)

        def phase_end(eng, k):
            eng.drain().then_inc(phase, 1)
            eng.wait_ge(phase, 5 * k)

        def tile_rows(t):
            return bass.ds(t * P, P)

        loads = [
            (src_c[:, :], a["src_c"]),
            (rows[:, :, :].rearrange("p a b -> p (a b)"), a["rows"]),
            (cols[:, :], a["cols"]),
            (s_wneigh, a["W_neigh"]), (s_wkv, a["Wkv"]), (s_wq, a["Wq"]), (s_wout, a["WoutT"]),
            (s_w1, a["w1"]), (s_w2, a["w2"]), (s_wqT, a["wqT"]), (s_wkT, a["wkTb"]),
            (w_mix[:, :, :], a["W_self"]), (w_qkv[:, :, :], a["w_qkv"]), (w_out[:, :], a["w_out"]),
            (w_v[:, :, :], a["wv"]), (w_s[:, :, :], a["ws"]), (w_ff1[:, :, :], a["w_ff1"]),
            (w_ff2[:, :, :], a["w_ff2"]), (w_r[:, :, :], a["Wr"]), (w_bo[:, :], a["bo"]),
            (mem_v[:, 0:HID], a["mem_v"]),
            (view(reg_g, 0, CT * P).bitcast(I32), a["dst_ov"]), (firsts.bitcast(I32), a["first"]),
        ]
        NLOAD = 16 * len(loads)
        N_CONST = 13

        block = ctx.enter_context(nc.Block())

        @block.sync
        def _(sp):
            for dst_ap, src_ap in loads:
                if len(dst_ap.shape) == 3:
                    src_ap = src_ap.rearrange("p (a b) -> p a b", b=dst_ap.shape[2])
                sp.dma_start(dst_ap, src_ap).then_inc(loaded, 16)

            def hold(ph, n, value):
                need(sp, ph, n, value)
                sp.nop(nofuse=True)

            def pairs(prologue_load, load, store):
                for s in range(2):
                    load(s, s, 0, True)

                def body(g, last=False):
                    if not last:
                        for s in range(2):
                            load(2 * g + 2 + s, s, g + 1, False)
                    for s in range(2):
                        store(2 * g + s, s, g)
                body(0)
                with sp.Fori(1, NG - 1) as g:
                    body(g)
                body(NG - 1, True)

            tc = t_chunk.rearrange("(i p) c -> p i c", p=P)
            sp.wait_ge(lk, 1)
            sp.dma_start(tc[:, :, 0:P], c_dst).then_inc(lk_st, 16)
            sp.wait_ge(lk, 2)
            sp.dma_start(tc[:, :, P:2 * P], c_cum).then_inc(lk_st, 16)
            for i in range(2):
                sp.dma_start(t_ni[i, :].rearrange("(i p) -> p i", p=P), chunki[:, i, :],
                             allow_slow_non_contiguous=True).then_inc(lk_st, 16)
            sp.wait_ge(lk_st, 64)
            sp.dma_start(nrow[0:1, :, :], t_ni.rearrange("(a i) c -> a i c", a=1)).then_inc(lk_st, 16)

            def load(t, s, g, first):
                if not first:
                    hold("P1", "xn_ok", t - 1)
                sp.dma_start(nbuf(s, 0, D), a["x"][tile_rows(t), :]).then_inc(ld[s], 16)

            def store(t, s, g):
                hold("P1", "xn_ok", t + 1)
                sp.dma_start(t_xn[tile_rows(t), :], nbuf(s, 256, D)).then_inc(sta[s], 16)
                hold("P1", "hs_ok", t + 1)
                sp.dma_start(t_hs[tile_rows(t), :], nbuf(s, 1280, D)).then_inc(stb[s], 16)
                sp.dma_start(t_sum[bass.ds(t * (ZPER * P), ZPER * P), :].rearrange("(p r) c -> p (r c)", r=ZPER),
                             zeros).then_inc(zeroed, 16)
            pairs(True, load, store)
            sp.wait_ge(consts, N_CONST)
            with sp.Fori(0, NT) as t:
                sp.dma_start(t_qk[tile_rows(t), :], zrow[:, :]).then_inc(zeroed, 16)
            sp.dma_start(t_carry[C:C + 1, :], zrow[0:1, :]).then_inc(zeroed, 16)
            sp.dma_start(t_score[0:1, C * EC:CR * P], zrow[0:1, 0:CR * P - C * EC]).then_inc(zeroed, 16)
            sp.wait_ge(zeroed, (2 * NT + 2) * 16)
            for s in range(2):
                stored(sp, "P1", "a", s, NG)
                stored(sp, "P1", "b", s, NG)
            phase_end(sp, 1)

            def first_rows(i, it, h):
                return nc.values_load_multi_w_load_instructions(
                    nrow[0:1, i, bass.ds(it * B + h * H, H)], [mybir.EngineType.SP], min_val=0,
                    max_val=2 * FULL, skip_runtime_bounds_check_because="worked out from the chunk's number")[1]

            def chunk_rows(first, table_, move):
                why = "every chunk's rows lie in the table"
                last = table_.shape[0]
                with sp.If(first >= FULL):
                    at = nc.s_assert_within(first - FULL, 0, last - P, skip_runtime_bounds_check_because=why)
                    move(table_[bass.ds(at, P), :], P)
                with sp.Else():
                    at = nc.s_assert_within(first, 0, last - FEW, skip_runtime_bounds_check_because=why)
                    move(table_[bass.ds(at, FEW), :], FEW)

            def store_sums(chunk0, z0):
                def body(it):
                    for h in range(2):
                        first = first_rows(1, it, h)
                        for k in range(H):
                            s = h * H + k
                            sp.wait_ge(carry_ok, chunk0 + it * B + s + 1)
                            sp.nop(nofuse=True)
                            chunk_rows(first[k], t_sum, lambda there, n: sp.dma_start(
                                there, ZR[0:n, s, :]).then_inc(z_sem[s], 16))
                plain_groups(sp, NB, body)
                for s in range(B):
                    sp.wait_ge(z_sem[s], z0 + 16 * NB)

            sp.wait_ge(lk_st, 80)
            store_sums(0, 0)
            phase_end(sp, 2)

            def load(t, s, g, first):
                if not first:
                    hold("P3", "var_ok", t - 1)
                sp.dma_start(nbuf(s, 0, D), a["x"][tile_rows(t), :]).then_inc(ld[s], 16)
                sp.dma_start(nbuf(s, 256, D), t_xn[tile_rows(t), :]).then_inc(ld[s], 16)

            def store(t, s, g):
                hold("P3", "xn_ok", t + 1)
                sp.dma_start(t_xn1[tile_rows(t), :], nbuf(s, 1536, D)).then_inc(sta[s], 16)
                hold("P3", "sum_ok", t + 1)
                sp.dma_start(t_xs[tile_rows(t), :], nbuf(s, 1792, D)).then_inc(stb[s], 16)
                hold("P3", "ev_a", t + 1)
                sp.dma_start(t_w[0, bass.ds(t * P, P)].rearrange("(p a) -> p a", a=1),
                             nbuf(s, 2304, 1)).then_inc(stc[s], 16)
            pairs(True, load, store)
            for s in range(2):
                for c in "abc":
                    stored(sp, "P3", c, s, NG)
            sp.dma_start(w_bcast, t_w[0:1, :].to_broadcast([P, NP])).then_inc(misc, 16)
            sp.wait_ge(misc, 16)
            phase_end(sp, 3)

            def load(t, s, g, first):
                if not first:
                    hold("P3b", "xT_ps", t - 1)
                sp.dma_start(nbuf(s, 0, D), t_xn1[tile_rows(t), :]).then_inc(ld[s], 16)

            def store(t, s, g):
                hold("P3b", "res_ok", t + 1)
                sp.dma_start(t_y[tile_rows(t), :], nbuf(s, 2048, D)).then_inc(sta[s], 16)
            pairs(True, load, store)
            for s in range(2):
                stored(sp, "P3b", "a", s, NG)
            phase_end(sp, 4)

            def load(t, s, g, first):
                if not first:
                    hold("P4", "sum_ok", t - 1)
                sp.dma_start(nbuf(s, 0, D), t_xs[tile_rows(t), :]).then_inc(ld[s], 16)
                sp.dma_start(nbuf(s, 256, D), t_y[tile_rows(t), :]).then_inc(ld[s], 16)

            def store(t, s, g):
                hold("P4", "sum_ok", t + 1)
                sp.dma_start(t_x2[tile_rows(t), :], nbuf(s, 512, D)).then_inc(sta[s], 16)
                hold("P4", "xn_ok", t + 1)
                sp.dma_start(t_xn2[tile_rows(t), :], nbuf(s, 768, D)).then_inc(stb[s], 16)
                hold("P4", "ev_b", t + 1)
                sp.dma_start(t_kv[tile_rows(t), :], nbuf(s, 1792, 2 * HID)).then_inc(std[s], 16)
                hold("P4", "res_ok", t + 1)
                sp.dma_start(t_q[tile_rows(t), :], nbuf(s, 2560, HID)).then_inc(std[s], 16)
            pairs(True, load, store)
            for s in range(2):
                stored(sp, "P4", "a", s, NG)
                stored(sp, "P4", "b", s, NG)
                qk_stored(sp, s, NG)
                stored(sp, "P4", "d", s, NG, 2)
            phase_end(sp, 5)

            def load(t, s, g, first):
                if not first:
                    hold("P4b", "mm_a", t - 1)
                sp.dma_start(nbuf(s, 0, 2 * HID), t_kv[tile_rows(t), :]).then_inc(ld[s], 16)
            pairs(True, load, lambda t, s, g: None)
            phase_end(sp, 6)

            sp.dma_start(s_a.bitcast(I32), a["dprev_r"]).then_inc(misc, 16)
            sp.dma_start(s_b.bitcast(I32), a["dst_r"]).then_inc(misc, 16)
            sp.dma_start(s_next.bitcast(I32), a["dnext_r"]).then_inc(misc, 16)
            sp.wait_ge(q_clear, 1)

            def body(it):
                for h in range(2):
                    first = first_rows(0, it, h)
                    for k in range(H):
                        s = h * H + k
                        if not isinstance(it, int):
                            sp.wait_ge(sum_ps, C + it * B + s - B + 1)
                            sp.nop(nofuse=True)
                        chunk_rows(first[k], t_qk, lambda there, n: sp.dma_start(
                            ZR[0:n, s, :], there).then_inc(z_sem[s], 16))
            plain_groups(sp, NB, body)
            for i in range(CT):
                n = min(P, C - i * P)
                sp.wait_ge(turned_sb, CT + i + 1)
                sp.dma_start(t_score[0, i * P * EC:(i * P + n) * EC].rearrange("(c q) -> c q", q=EC),
                             reg_g[0:n, i * P + 1:(i + 1) * P]).then_inc(misc, 16)
            sp.wait_ge(misc, 64 + 16 * CT)
            sp.dma_start(score, t_score[0, :].rearrange("(p c) -> p c", c=CR)).then_inc(misc, 16)
            sp.dma_start(s_c, a["ew_r"]).then_inc(misc, 16)
            sp.wait_ge(attention_ok, 1)
            sp.dma_start(t_att[0, :].rearrange("(p c) -> p c", c=CR), s_c).then_inc(misc, 16)
            sp.wait_ge(misc, 112 + 16 * CT)
            for i in range(CT):
                n = min(P, C - i * P)
                sp.dma_start(reg_g[0:n, i * P + 1:(i + 1) * P],
                             t_att[0, i * P * EC:(i * P + n) * EC].rearrange("(c q) -> c q", q=EC)).then_inc(misc, 16)
            phase_end(sp, 7)
            store_sums(C, 32 * NB)
            phase_end(sp, 8)

            sp.dma_start(view(reg_g, 0, 4096), a["W1"]).then_inc(misc, 16)
            sp.dma_start(view(reg_g, 4096, 4096), a["W2"]).then_inc(misc, 16)
            sp.dma_start(view(reg_s, 0, 4096), a["Wo"]).then_inc(misc, 16)

            def load(t, s, g, first):
                if not first:
                    hold("P6", "res_ok", t - 1)
                sp.dma_start(nbuf(s, 0, D), t_x2[tile_rows(t), :]).then_inc(ld[s], 16)
                sp.dma_start(nbuf(s, 256, D), t_xn2[tile_rows(t), :]).then_inc(ld[s], 16)
                sp.dma_start(nbuf(s, 769, HID), t_q[tile_rows(t), :]).then_inc(ld[s], 16)

            def store(t, s, g):
                hold("P6", "res_ok", t + 1)
                sp.dma_start(t_x3[tile_rows(t), :], nbuf(s, 3584, D)).then_inc(sta[s], 16)
                hold("P6", "dots_ok", t + 1)
                sp.dma_start(t_xn3[tile_rows(t), :], nbuf(s, 3840, D)).then_inc(stb[s], 16)
            pairs(True, load, store)
            for s in range(2):
                stored(sp, "P6", "a", s, NG)
                stored(sp, "P6", "b", s, NG)
            phase_end(sp, 9)

            def load(t, s, g, first):
                if not first:
                    hold("P7", "ev_a", t - 1)
                sp.dma_start(nbuf(s, 0, D), t_x3[tile_rows(t), :]).then_inc(ld[s], 16)
                sp.dma_start(nbuf(s, 256, D), t_xn3[tile_rows(t), :]).then_inc(ld[s], 16)

            def store(t, s, g):
                sp.wait_ge(lo_ok, g * 2 * EX + 2 * EX - 1 + s)
                sp.nop(nofuse=True)
                if isinstance(t, int) and t >= NT - 2:
                    n = TAIL if t == NT - 2 else 0
                    if n:
                        sp.dma_start(out[t * P:t * P + n, :], nbuf(s, 1792, D)[0:n, :]).then_inc(sta[s], 16)
                else:
                    sp.dma_start(out[tile_rows(t), :], nbuf(s, 1792, D)).then_inc(sta[s], 16)
            pairs(True, load, store)
            stored(sp, "P7", "a", 0, NG)
            stored(sp, "P7", "a", 1, NG - 1)

        @block.gpsimd
        def _(po):
            ch = Chain(po, pool_step)
            nc.gpsimd.memset(ident[:, :], 0.0).then_inc(consts, 1)
            nc.gpsimd.memset(lower[:, :], 1.0).then_inc(consts, 1)
            nc.gpsimd.iota(iotai[:, 0:P], [[1, P]], base=0, channel_multiplier=0).then_inc(consts, 1)
            nc.gpsimd.iota(iotai[:, P:P + 1], [[1, 1]], base=0, channel_multiplier=1).then_inc(consts, 1)
            nc.gpsimd.iota(iotai[:, P + 1:P + 1 + NT], [[P, NT]], base=0, channel_multiplier=1).then_inc(consts, 1)
            nc.gpsimd.memset(padneg[:, :], 0.0).then_inc(consts, 1)
            po.wait_ge(consts, 6)
            nc.gpsimd.affine_select(out=ident[:, :], in_=ident[:, :], compare_op=ALU.not_equal, fill=1.0,
                                    base=0, pattern=[[-1, P]], channel_multiplier=1).then_inc(consts, 1)
            nc.gpsimd.affine_select(out=lower[:, :], in_=lower[:, :], compare_op=ALU.is_gt, fill=0.0,
                                    base=0, pattern=[[1, P]], channel_multiplier=-1).then_inc(consts, 1)
            nc.gpsimd.affine_select(out=padneg[:, :], in_=padneg[:, :], compare_op=ALU.is_ge, fill=NEG,
                                    base=N - 1, pattern=[[-P, NT]], channel_multiplier=-1).then_inc(consts, 1)
            nc.gpsimd.memset(half[:, :], -0.5).then_inc(consts, 1)
            nc.gpsimd.memset(ones[:, :], 1.0).then_inc(consts, 1)
            nc.gpsimd.memset(zrow[:, :], 0.0).then_inc(consts, 1)
            nc.gpsimd.memset(mem_v[:, HID:HID + 1], 1.0).then_inc(consts, 1)
            po.wait_ge(consts, N_CONST)

            def root(ph, var, rstd, t, s, src_off, dst_off):
                need(po, ph, var, t + 1)
                nc.gpsimd.tensor_tensor(nbuf(s, dst_off, 1), nbuf(s, src_off, 1), half[:, 0:1],
                                        ALU.pow).then_inc(sg[rstd], 1)

            po.wait_ge(moe_var, 2)
            for i in (4, 5):
                nc.gpsimd.tensor_tensor(moe[:, i, :], moe[:, i, :], half[:, 0:2 * EX],
                                        ALU.pow).then_inc(moe_root, 1)

            def body(g):
                for s in range(2):
                    root("P1", "var_ok", "rstd_ok", 2 * g + s, s, 4108, 4110)
                for s in range(2):
                    need(po, "P1", "sq_red", 2 * g + s + 1)
                    nc.gpsimd.tensor_tensor(nbuf(s, 4160, 8), nbuf(s, 4144, 8), half[:, 0:8],
                                            ALU.pow).then_inc(sg["rstd_kv"], 1)
            plain_groups(po, NG, body)
            phase_end(po, 1)

            po.wait_ge(lk, 3)

            def body(g):
                for h in range(2):
                    n = 2 * g + h
                    wait(po, lk_ok, n - 1)
                    if not isinstance(g, int):
                        po.nop(nofuse=True)
                    nc.gpsimd.tensor_copy(lidx[:, h, :], cidx[:, bass.ds(n * LK, LK)]).then_inc(lk_g, 1)
                    po.wait_ge(lk_g, n + 1)
                    po.nop(nofuse=True)
                    for k in range(LK):
                        nc.gpsimd.indirect_dma_start(
                            out=found[:, h * LK + k, :], out_offset=None, in_=t_chunk[:, :],
                            in_offset=bass.IndirectOffsetOnAxis(ap=lidx[:, h, k:k + 1], axis=0)
                        ).then_inc(lk_in[h], 16)
            plain_groups(po, NT // (2 * LK), body)

            def gather_pass(table_, used_up, u0, i0):
                def body(it):
                    for h in range(2):
                        if not isinstance(it, int):
                            po.wait_ge(used_up, u0 + it * B + h * H - H)
                            po.nop(nofuse=True)
                        nc.gpsimd.tensor_copy(sidx[:, h, :], src_c[:, bass.ds(it * B + h * H, H)]).then_inc(idx_ok, 1)
                        po.wait_ge(idx_ok, i0 + it * 2 + h + 1)
                        po.nop(nofuse=True)
                        for k in range(H):
                            s = h * H + k
                            nc.gpsimd.indirect_dma_start(
                                out=GR[:, s, 0:D], out_offset=None, in_=table_[:, :],
                                in_offset=bass.IndirectOffsetOnAxis(ap=sidx[:, h, k:k + 1], axis=0)
                            ).then_inc(g_sem[s], 16)
                plain_groups(po, NB, body)

            po.wait_ge(ones_ok, 1)
            gather_pass(t_hs, sum_ps, 0, 0)
            phase_end(po, 2)

            def by_node(t, s, n, rows_):
                nc.gpsimd.tensor_copy(tidx[:, s:s + 1], rows_[:, bass.ds(t, 1)]).then_inc(tidx_ok, 1)
                po.wait_ge(tidx_ok, n)
                po.nop(nofuse=True)
                return bass.IndirectOffsetOnAxis(ap=tidx[:, s:s + 1], axis=0)

            def fetch_sums(t, s, n):
                nc.gpsimd.tensor_copy(tidx[:, 2 + s:3 + s], carryrow[:, bass.ds(t, 1)]).then_inc(tidx_ok, 1)
                where = by_node(t, s, n, sumrow)
                nc.gpsimd.indirect_dma_start(out=nbuf(s, 512, D1), out_offset=None, in_=t_sum[:, :],
                                             in_offset=where).then_inc(ld_sum[s], 16)
                nc.gpsimd.indirect_dma_start(out=carried[:, s, :], out_offset=None, in_=t_carry[:, :],
                                             in_offset=bass.IndirectOffsetOnAxis(ap=tidx[:, 2 + s:3 + s], axis=0)
                                             ).then_inc(ld_sum[s], 16)

            def ahead(n0, ph, used_up, body):
                for s in range(2):
                    fetch_sums(s, s, n0 + 2 * s + 2)

                def whole(g, last=False):
                    for s in range(2):
                        po.wait_ge(ld_sum[s], 32 * (tiles_before[ph] // 2 + g + 1))
                        nc.gpsimd.tensor_tensor(nbuf(s, 512, D1), nbuf(s, 512, D1), carried[:, s, :],
                                                ALU.add).then_inc(summed, 1)
                    body(g)
                    if not last:
                        for s in range(2):
                            t = 2 * g + s
                            need(po, ph, used_up, t + 1)
                            po.wait_ge(summed, tiles_before[ph] + t + 1)
                            po.nop(nofuse=True)
                            fetch_sums(t + 2, s, n0 + 2 * t + 6)
                whole(0)
                with po.Fori(1, NG - 1) as g:
                    whole(g)
                whole(NG - 1, True)

            def body(g):
                for s in range(2):
                    root("P3", "var_ok", "rstd_ok", 2 * g + s, s, 4108, 4110)
                for s in range(2):
                    need(po, "P3", "xn_ok", 2 * g + s + 1)
                    stored(po, "P3", "b", s, g)
                    nc.gpsimd.tensor_tensor(nbuf(s, 1792, D), nbuf(s, 1280, D), nbuf(s, 1536, D),
                                            ALU.add).then_inc(sg["sum_ok"], 1)
            ahead(0, "P3", "var_ok", body)
            phase_end(po, 3)
            phase_end(po, 4)

            def body(g):
                for s in range(2):
                    root("P4", "var_ok", "rstd_ok", 2 * g + s, s, 4108, 4110)
                for s in range(2):
                    root("P4", "var2_ok", "rstd2_ok", 2 * g + s, s, 4112, 4114)
                for s in range(2):
                    t = 2 * g + s
                    qk_stored(po, s, g)
                    if not isinstance(g, int):
                        po.nop(nofuse=True)
                    where = by_node(t, s, 2 * NT + t + 1, qrow)
                    need(po, "P4", "ev_a", t + 1)
                    po.nop(nofuse=True)
                    nc.gpsimd.indirect_dma_start(out=t_qk[:, :], out_offset=where, in_=nbuf(s, 1280, D1),
                                                 in_offset=None, bounds_check=NP - 1,
                                                 oob_is_err=False).then_inc(st_qk[s], 16)
            plain_groups(po, NG, body)
            phase_end(po, 5)
            phase_end(po, 6)

            po.wait_ge(q_clear, 1)
            gather_pass(t_xn2, scored, 0, 2 * NB)
            phase_end(po, 7)
            po.wait_ge(ones_ok, 2)
            gather_pass(t_xn2, sum_ps, 2 * C, 4 * NB)
            phase_end(po, 8)

            def body(g):
                for s in range(2):
                    root("P6", "var_ok", "rstd_ok", 2 * g + s, s, 4108, 4110)
                for s in range(2):
                    root("P6", "sq_red", "rstd_kv", 2 * g + s, s, 4112, 4114)
                for s in range(2):
                    root("P6", "var2_ok", "rstd2_ok", 2 * g + s, s, 4108, 4110)
                for s in range(2):
                    need(po, "P6", "v_ok", 2 * g + s + 1)
                    nc.gpsimd.tensor_tensor(nbuf(s, 4110, 1), nbuf(s, 4108, 1), half[:, 0:1],
                                            ALU.pow).then_inc(sg["rstd3_ok"], 1)
            ahead(3 * NT, "P6", "sq_red", body)
            phase_end(po, 9)

        @block.tensor
        def _(pe):
            mm, tr = nc.tensor.matmul, nc.tensor.transpose

            def flip(ph, s, src_off, ps, ps_off=0, n=KD, name="xT_ps"):
                for k in range(n):
                    last = tr(ps[:, ps_off + k * P:ps_off + (k + 1) * P], nbuf(s, src_off + k * P, P), ident[:, :])
                if name:
                    last.then_inc(sg[name], 1)
                return last

            pe.wait_ge(consts, N_CONST)
            pe.wait_ge(loaded, NLOAD)
            pe.wait_ge(dve_one, 1)
            for c in range(KD):
                for k in range(KD):
                    last = mm(psA[c][:, 0:D1], s_wqT[:, k, c * P:(c + 1) * P], s_wkT[:, k, :],
                              start=(k == 0), stop=(k == KD - 1))
            for k in range(KD):
                last = mm(psB[0][:, 0:D1], col("bq", k).to_broadcast([P, P]), s_wkT[:, k, :],
                          start=(k == 0), stop=(k == KD - 1))
            last.then_inc(pe_one, 1)
            pe.wait_ge(dve_one, 2)
            pe.wait_ge(lk, 1)
            mm(psA[0][:, 0:2 * CT], lower[:, :], chunkn[:, 0, :], start=True, stop=True)
            mm(psA[0][:, 64:64 + 2 * CT], ones[:, :], chunkn[:, 0, :], start=True, stop=True).then_inc(lk_ps, 1)

            def turn(base, src):
                for i in range(CT):
                    if base + i >= 2:
                        pe.wait_ge(turned_sb, base + i - 1)
                    part = src(i)
                    n = part.shape[0]
                    tr(psT[i % 2][0:part.shape[1], 0:n], part, ident[0:n, 0:n]).then_inc(turned_ps, 1)
            turn(0, lambda i: c_slot[:, i, :])
            pe.wait_ge(turned_sb, CT)
            pe.wait_ge(lk, 2)

            def body(g):
                for s in range(2):
                    need(pe, "P1", "xn_ok", 2 * g + s + 1)
                    flip("P1", s, 256, psT[s])
                for s in range(2):
                    t = 2 * g + s
                    need(pe, "P1", "xT_sb", t + 1)
                    need(pe, "P1", "ev_a", t - 1)
                    for k in range(KD):
                        last = mm(psA[s][:, 0:D], nbuf(s, 512 + k * P, P), s_wneigh[:, k, :],
                                  start=(k == 0), stop=(k == KD - 1))
                    last.then_inc(sg["mm_a"], 1)
                    need(pe, "P1", "ev_b", t)
                    for n in range(2):
                        for k in range(KD):
                            last = mm(psB[0][:, n * 512:(n + 1) * 512], nbuf(s, 512 + k * P, P),
                                      s_wkv[:, k, n * 512:(n + 1) * 512], start=(k == 0), stop=(k == KD - 1))
                    last.then_inc(sg["mm_b"], 1)
                for s in range(2):
                    t = 2 * g + s
                    need(pe, "P1", "v_ok", t + 1)
                    need(pe, "P1", "dots_ok", t)
                    for j in range(PAIRS):
                        last = mm(psB[1][:, j * P:(j + 1) * P], nbuf(s, 3584 + j * P, P),
                                  nbuf(s, 1536 + j * P, P), start=True, stop=True)
                    last.then_inc(sg["dots_ps"], 1)
            plain_groups(pe, NG, body)
            phase_end(pe, 1)

            def sum_pass(chunk0, g0, e0):
                def body(it):
                    for s in range(B):
                        pe.wait_ge(sel_ok, chunk0 + it * B + s + 1)
                        pe.wait_ge(g_sem[s], g0 + it * 16 + 16)
                        if not (isinstance(it, int) and s < 4):
                            pe.wait_ge(sum_sb, e0 + it * B + s - 3)
                        mm(psZ[s % 4][:, 0:D1], SEL[:, s, :], GR[:, s, :], start=True,
                           stop=True).then_inc(sum_ps, 1)
                plain_groups(pe, NB, body)

            pe.wait_ge(dve_one, 3)
            for j in range(PAIRS):
                last = mm(psB[j // 2][:, (j % 2) * 512:(j % 2) * 512 + D], dots[:, j, :], s_wout[:, j, :],
                          start=True, stop=True)
            last.then_inc(pe_one, 1)
            pe.wait_ge(act_one, 1)
            for c in range(KD):
                for j in range(PAIRS):
                    last = mm(psA[c][:, 0:D], s_wq[:, j, c * P:(c + 1) * P], fold[:, j, :],
                              start=(j == 0), stop=(j == PAIRS - 1))
            last.then_inc(pe_one, 1)
            pe.wait_ge(lk, 4)
            mm(psB[0][:, 0:NT], lower[:, :], look[:, 0, :], start=True, stop=True)
            mm(psB[0][:, 64:64 + NT], ones[:, :], look[:, 0, :], start=True, stop=True).then_inc(lk_ps, 1)
            pe.wait_ge(dve_one, 5)
            pe.wait_ge(lk, 5)
            sum_pass(0, 0, 0)
            phase_end(pe, 2)

            def body(g):
                for s in range(2):
                    landed(pe, "P3", s, g)
                    flip("P3", s, 256, psT[s])
                for s in range(2):
                    t = 2 * g + s
                    need(pe, "P3", "xT_sb", t + 1)
                    need(pe, "P3", "var_ok", t - 1)
                    for k in range(KD):
                        last = mm(psA[s][:, 0:D], nbuf(s, 769 + k * P, P), w_mix[:, k, :],
                                  start=(k == 0), stop=(k == KD - 1))
                    last.then_inc(sg["mm_a"], 1)
            plain_groups(pe, NG, body)
            phase_end(pe, 3)

            def body(g):
                for s in range(2):
                    landed(pe, "P3b", s, g)
                    flip("P3b", s, 0, psT[s])
                for s in range(2):
                    t = 2 * g + s
                    need(pe, "P3b", "xT_sb", t + 1)
                    for m in range(KF):
                        for k in range(KD):
                            last = mm(psB[s][:, m * P:(m + 1) * P], s_w1[:, k, m * P:(m + 1) * P],
                                      nbuf(s, 256 + k * P, P), start=(k == 0), stop=(k == KD - 1))
                    last.then_inc(sg["mm_b"], 1)
                for s in range(2):
                    t = 2 * g + s
                    need(pe, "P3b", "ev_b", t + 1)
                    need(pe, "P3b", "res_ok", t - 1)
                    for m in range(KF):
                        last = mm(psA[s][:, 0:D], nbuf(s, 512 + m * P, P), s_w2[:, m, :],
                                  start=(m == 0), stop=(m == KF - 1))
                    last.then_inc(sg["mm_a"], 1)
            plain_groups(pe, NG, body)
            phase_end(pe, 4)

            pe.wait_ge(dve_one, 6)
            tr(psT[0][0:1, 0:P], small[:, 0:1], ident[:, :]).then_inc(pe_one, 1)
            pe.wait_ge(dve_one, 7)
            tr(psT[0][:, P:P + 1], small[0:1, 1:2].to_broadcast([1, P]), ident[0:1, 0:1]).then_inc(pe_one, 1)
            pe.wait_ge(dve_one, 8)
            mm(psT[1][:, 0:NT], lower[:, :], pick[:, 0, :], start=True, stop=True)
            mm(psT[1][:, 64:64 + NT], ones[:, :], pick[:, 0, :], start=True, stop=True).then_inc(pe_one, 1)
            pe.wait_ge(dve_one, 9)

            def body(g):
                for s in range(2):
                    t = 2 * g + s
                    need(pe, "P4", "xn_ok", t + 1)
                    flip("P4", s, 768, psT[s])
                for s in range(2):
                    t = 2 * g + s
                    need(pe, "P4", "xT_sb", t + 1)
                    need(pe, "P4", "ev_a", t - 1)
                    for k in range(KD):
                        last = mm(psA[s][:, 0:D1], nbuf(s, 1024 + k * P, P), w_qk[:, k, :],
                                  start=(k == 0), stop=(k == KD - 1))
                    last.then_inc(sg["mm_a"], 1)
                    need(pe, "P4", "q_max", t - 1)
                    for k in range(KD):
                        last = mm(psB[s][:, 0:3 * HID], nbuf(s, 1024 + k * P, P), w_qkv[:, k, :],
                                  start=(k == 0), stop=(k == KD - 1))
                    last.then_inc(sg["mm_b"], 1)
            plain_groups(pe, NG, body)
            phase_end(pe, 5)

            tr(psT[0][:, 0:P], kmax[:, :], ident[:, :]).then_inc(pe_one, 1)
            pe.wait_ge(dve_one, 11)
            tr(psT[0][:, P:2 * P], small[:, 2:3].to_broadcast([P, P]), ident[:, :]).then_inc(pe_one, 1)
            pe.wait_ge(act_one, 2)
            tr(psT[1][0:MEM, 0:P], small[:, 8:8 + MEM], ident[:, :]).then_inc(pe_one, 1)
            pe.wait_ge(dve_one, 13)
            mm(psT[1][:, P:P + HID + 1], nbuf(0, 1024, P)[0:MEM, :], mem_v[:, :],
               start=True, stop=True).then_inc(pe_one, 1)

            def body(g):
                for s in range(2):
                    t = 2 * g + s
                    need(pe, "P4b", "q_exp", t + 1)
                    need(pe, "P4b", "ev_a", t - 1)
                    mm(psA[s][:, 0:HID + 1], nbuf(s, 512, P), nbuf(s, 640, HID + 1),
                       start=True, stop=True).then_inc(sg["mm_a"], 1)
            plain_groups(pe, NG, body)
            pe.wait_ge(dve_one, 16)
            tr(psT[0][:, 0:P], ctxn[:, 0, :], ident[:, :]).then_inc(pe_one, 1)
            pe.wait_ge(act_one, 3)
            mm(psA[0][:, 0:D], ctxn[:, 1, :], w_out[:, :], start=True, stop=True).then_inc(pe_one, 1)
            phase_end(pe, 6)

            def body(it):
                for h in range(2):
                    pe.wait_ge(dcol_ok, it * 2 + h + 1)
                    for k in range(H):
                        if k % 4 == 0 and not (isinstance(it, int) and it == 0 and h == 0):
                            pe.wait_ge(sel_ok, C + it * B + h * H - H + k + 4)
                        tr(psT[k // 4][:, (k % 4) * P:(k % 4 + 1) * P],
                           dcol[:, h, k:k + 1].to_broadcast([P, P]), ident[:, :]).then_inc(row_ps, 1)
                    for k in range(H):
                        s = h * H + k
                        pe.wait_ge(sel_ok, C + it * B + s + 1)
                        pe.wait_ge(z_sem[s], 16 * NB + it * 16 + 16)
                        if not (isinstance(it, int) and s < 4):
                            pe.wait_ge(scored, it * B + s - 3)
                        mm(psZ[s % 4][:, 0:D1], SEL[:, s, :], ZR[:, s, :], start=True,
                           stop=True).then_inc(sum_ps, 1)
            plain_groups(pe, NB, body)
            pe.wait_ge(scores_ok, 1)
            turn(CT, lambda i: score_c[:, i * P:min((i + 1) * P, C)])
            for i in range(4):
                pe.wait_ge(scan_ok, 2 * i + 1)
                tr(psA[0][0:1, 0:P], small[:, 16:17], ident[:, :])
                tr(psA[0][0:1, P:2 * P], small[:, 17:18], ident[:, :]).then_inc(pe_one, 1)
                pe.wait_ge(scan_ok, 2 * i + 2)
                tr(psA[1][:, 0:1], srow[0:1, 3, :], ident[0:1, 0:1]).then_inc(pe_one, 1)
            pe.wait_ge(misc, 112 + 32 * CT)
            turn(2 * CT, lambda i: reg_g[0:min(P, C - i * P), i * P:(i + 1) * P])
            phase_end(pe, 7)
            sum_pass(2 * C, 32 * NB, C)
            phase_end(pe, 8)

            def body(g):
                for s in range(2):
                    landed(pe, "P6", s, g)
                    sums_complete(pe, "P6", 2 * g + s)
                    flip("P6", s, 256, psB[s], 0, name=None)
                    flip("P6", s, 512, psB[s], 2 * P, name=None)
                    flip("P6", s, 769, psB[s], 4 * P, n=1)
                for s in range(2):
                    t = 2 * g + s
                    need(pe, "P6", "xT_sb", t + 1)
                    need(pe, "P6", "ev_a", t - 1)
                    for k in range(KD):
                        mm(psA[s][:, 0:D], nbuf(s, 1024 + k * P, P), w_s[:, k, :], start=(k == 0), stop=False)
                    for k in range(KD):
                        mm(psA[s][:, 0:D], nbuf(s, 1280 + k * P, P), w_v[:, k, :],
                           start=False, stop=(k == KD - 1))
                    mm(psA[s][:, D:2 * D], nbuf(s, 1536, P), w_m2[:, :],
                       start=True, stop=True).then_inc(sg["mm_a"], 1)
                for s in range(2):
                    need(pe, "P6", "xn_ok", 2 * g + s + 1)
                    flip("P6", s, 1920, psT[s], name="tT_ps")
                for s in range(2):
                    need(pe, "P6", "tT_sb", 2 * g + s + 1)
                    for m in range(K1):
                        for k in range(KD):
                            last = mm(psB[s][:, m * P:(m + 1) * P], w_ff1[:, k, m * P:(m + 1) * P],
                                      nbuf(s, 2176 + k * P, P), start=(k == 0), stop=(k == KD - 1))
                    last.then_inc(sg["ff_ps"], 1)
                for s in range(2):
                    need(pe, "P6", "ff_sb", 2 * g + s + 1)
                    for m in range(K1):
                        last = mm(psT[s][:, D:2 * D], nbuf(s, 2432 + m * P, P), w_ff2[:, m, :],
                                  start=(m == 0), stop=(m == K1 - 1))
                    last.then_inc(sg["mm_b"], 1)
            plain_groups(pe, NG, body)
            phase_end(pe, 9)

            pe.wait_ge(misc, 112 + 32 * CT + 48)

            def body(g):
                for s in range(2):
                    landed(pe, "P7", s, g)
                    flip("P7", s, 256, psT[s])
                for s in range(2):
                    t = 2 * g + s
                    need(pe, "P7", "xT_sb", t + 1)
                    for k in range(KD):
                        last = mm(psT[s][:, D:D + EX], nbuf(s, 512 + k * P, P), w_r[:, k, :],
                                  start=(k == 0), stop=(k == KD - 1))
                    last.then_inc(sg["mm_a"], 1)
                for s in range(2):
                    need(pe, "P7", "sum_ok", 2 * g + s + 1)
                    tr(psT[s][0:EX, 384:512], nbuf(s, 4120, EX), ident[:, :]).then_inc(sg["tT_ps"], 1)
                for s in range(2):
                    need(pe, "P7", "tT_sb", 2 * g + s + 1)
                    wait(pe, lo_ok, g * 2 * EX - 1 + s)
                    mm(psA[s][:, 0:D], nbuf(s, 2304, P)[0:EX, :], w_bo[:, :],
                       start=True, stop=True).then_inc(sg["mm_b"], 1)
                for e in range(EX):
                    for s in range(2):
                        n = g * 2 * EX + e * 2 + s
                        wait(pe, l1_sb, n - 1)
                        for m in range(KD):
                            for k in range(KD):
                                last = mm(psB[s][:, m * P:(m + 1) * P], g_w1[:, e, k, m * P:(m + 1) * P],
                                          nbuf(s, 512 + k * P, P), start=(k == 0), stop=(k == KD - 1))
                        last.then_inc(l1_ps, 1)
                    for s in range(2):
                        n = g * 2 * EX + e * 2 + s
                        wait(pe, l1_sb, n + 1)
                        for m in range(KD):
                            for k in range(KD):
                                last = mm(psB[s][:, 512 + m * P:512 + (m + 1) * P],
                                          g_w2[:, e, k, m * P:(m + 1) * P],
                                          nbuf(s, 768 + k * P, P), start=(k == 0), stop=(k == KD - 1))
                        last.then_inc(l2_ps, 1)
                    for s in range(2):
                        n = g * 2 * EX + e * 2 + s
                        wait(pe, l2_sb, n + 1)
                        if e == 0:
                            need(pe, "P7", "ev_a", 2 * g + s + 1)
                        else:
                            wait(pe, lo_ok, n - 1)
                        for k in range(KD):
                            last = mm(psA[s][:, 0:D], nbuf(s, 1024 + k * P, P), s_wo[:, e, k, :],
                                      start=(k == 0), stop=(k == KD - 1))
                        last.then_inc(lo_ps, 1)
            plain_groups(pe, NG, body)

        @block.scalar
        def _(act):
            cp, fn = nc.scalar.copy, nc.scalar.activation
            def turned(base, dst):
                for i in range(CT):
                    act.wait_ge(turned_ps, base + i + 1)
                    to = dst(i)
                    cp(to, psT[i % 2][0:to.shape[0], 0:to.shape[1]]).then_inc(turned_sb, 1)

            def chunk_cols(reg):
                return lambda i: reg[:, i * P:min((i + 1) * P, C)]
            turned(0, chunk_cols(slot_c))

            def body(g):
                for s in range(2):
                    t = 2 * g + s
                    need(act, "P1", "xT_ps", t + 1)
                    need(act, "P1", "mm_b", t - 1)
                    cp(nbuf(s, 512, D), psT[s][:, 0:D]).then_inc(sg["xT_sb"], 1)
                for s in range(2):
                    t = 2 * g + s
                    need(act, "P1", "mm_a", t + 1)
                    need(act, "P1", "hs_ok", t - 1)
                    cp(nbuf(s, 768, D), psA[s][:, 0:D]).then_inc(sg["ev_a"], 1)
                    need(act, "P1", "mm_b", t + 1)
                    need(act, "P1", "dots_ps", t - 1)
                    cp(nbuf(s, 1536, 1024), psB[0][:, :])
                    need(act, "P1", "sq_red", t - 1)
                    fn(nbuf(s, 2560, 1024), psB[0][:, :], ACT.Square).then_inc(sg["ev_b"], 1)
                for s in range(2):
                    t = 2 * g + s
                    fn(sign_junk, firsts, ACT.Sign, bias=nid[:, 1, bass.ds(t, 1)], scale=-1.0,
                       accum_out=look[:, 1, bass.ds(t, 1)]).then_inc(act_step, 1)
                    act.wait_ge(act_step, t + 1)
            act.wait_ge(lk, 2)
            plain_groups(act, NG, body)
            phase_end(act, 1)

            act.wait_ge(pe_one, 2)
            for j in range(PAIRS):
                last = nc.scalar.mul(fold[:, j, :], psB[j // 2][:, (j % 2) * 512:(j % 2) * 512 + D], 1.0 / N)
            last.then_inc(act_one, 1)

            def empty_pass(c0, k0, z0):
                def store_carries(it, h):
                    act.wait_ge(carry_ok, k0 + it * B + h * H + H)
                    act.nop(nofuse=True)
                    act.dma_start(t_carry[bass.ds(it * B + h * H, H), :].rearrange("(a s) c -> a s c", a=1),
                                  ZR[0:1, h * H:h * H + H, :]).then_inc(c_sem[h], 16)

                def body(it, first=False):
                    for s in range(B):
                        c = it * B + s
                        act.wait_ge(sum_ps, c0 + c + 1)
                        wait(act, z_sem[s], z0 + (0 if first else 16 * it))
                        if s % H == 0:
                            wait(act, c_sem[s // H], (c_base + 16 * it) if not first else 0)
                        if not first:
                            act.wait_ge(carry_ok, k0 + c - B + 2)
                        cp(ZR[:, s, :], psZ[s % 4][:, 0:D1]).then_inc(sum_sb, 1)
                        if s == H + CARRY_LAG:
                            store_carries(it, 0)
                        if s == CARRY_LAG and not first:
                            store_carries(it - 1, 1)
                c_base = 16 * NB * (k0 // C)
                body(0, True)
                with act.Fori(1, NB) as it:
                    body(it)
                store_carries(NB - 1, 1)
                for h in range(2):
                    act.wait_ge(c_sem[h], c_base + 16 * NB)
            act.wait_ge(consts, N_CONST)
            empty_pass(0, 0, 0)
            phase_end(act, 2)

            def body(g):
                for s in range(2):
                    t = 2 * g + s
                    need(act, "P3", "xT_ps", t + 1)
                    need(act, "P3", "mm_a", t - 1)
                    cp(nbuf(s, 769, D), psT[s][:, 0:D]).then_inc(sg["xT_sb"], 1)
            plain_groups(act, NG, body)
            phase_end(act, 3)

            def body(g):
                for s in range(2):
                    t = 2 * g + s
                    need(act, "P3b", "xT_ps", t + 1)
                    need(act, "P3b", "mm_b", t - 1)
                    cp(nbuf(s, 256, D), psT[s][:, 0:D]).then_inc(sg["xT_sb"], 1)
                for s in range(2):
                    t = 2 * g + s
                    need(act, "P3b", "mm_b", t + 1)
                    need(act, "P3b", "mm_a", t - 1)
                    for m in range(KF):
                        last = fn(nbuf(s, 512 + m * P, P), psB[s][:, m * P:(m + 1) * P], ACT.Gelu_apprx_tanh,
                                  bias=col("ffn_b1", m))
                    last.then_inc(sg["ev_b"], 1)
            plain_groups(act, NG, body)
            phase_end(act, 4)

            def body(g):
                for s in range(2):
                    t = 2 * g + s
                    need(act, "P4", "xT_ps", t + 1)
                    need(act, "P4", "mm_b", t - 1)
                    cp(nbuf(s, 1024, D), psT[s][:, 0:D]).then_inc(sg["xT_sb"], 1)
                for s in range(2):
                    t = 2 * g + s
                    need(act, "P4", "q_max", t + 1)
                    fn(nbuf(s, 2176, HID), nbuf(s, 2048, HID), ACT.Exp).then_inc(sg["q_exp"], 1)
            plain_groups(act, NG, body)
            phase_end(act, 5)

            act.wait_ge(dve_one, 12)
            fn(small[:, 8:8 + MEM], col("mem_k", 0, MEM), ACT.Exp, bias=small[:, 3:4]).then_inc(act_one, 1)

            def body(g):
                for s in range(2):
                    t = 2 * g + s
                    need(act, "P4b", "q_max", t + 1)
                    fn(nbuf(s, 512, P), nbuf(s, 256, P), ACT.Exp).then_inc(sg["q_exp"], 1)
            plain_groups(act, NG, body)
            act.wait_ge(pe_one, 11)
            cp(ctxn[:, 1, :], psT[0][:, 0:P]).then_inc(act_one, 1)
            phase_end(act, 6)

            turned(CT, lambda i: reg_g[0:min(P, C - i * P), i * P:(i + 1) * P])
            act.wait_ge(shifted, 1)
            fn(s_c, s_c, ACT.Exp).then_inc(act_one, 1)
            turned(2 * CT, chunk_cols(wt))
            phase_end(act, 7)
            empty_pass(2 * C, C, 32 * NB)
            phase_end(act, 8)

            def body(g):
                for s in range(2):
                    t = 2 * g + s
                    need(act, "P6", "xT_ps", t + 1)
                    need(act, "P6", "mm_a", t - 1)
                    cp(nbuf(s, 1024, 5 * P), psB[s][:, 0:5 * P]).then_inc(sg["xT_sb"], 1)
                for s in range(2):
                    t = 2 * g + s
                    need(act, "P6", "tT_ps", t + 1)
                    need(act, "P6", "ff_ps", t - 1)
                    cp(nbuf(s, 2176, D), psT[s][:, 0:D]).then_inc(sg["tT_sb"], 1)
                for s in range(2):
                    t = 2 * g + s
                    need(act, "P6", "ff_ps", t + 1)
                    need(act, "P6", "mm_b", t - 1)
                    for m in range(K1):
                        last = fn(nbuf(s, 2432 + m * P, P), psB[s][:, m * P:(m + 1) * P], ACT.Gelu_apprx_tanh,
                                  bias=col("b_ff1", m))
                    last.then_inc(sg["ff_sb"], 1)
            plain_groups(act, NG, body)
            phase_end(act, 9)

            act.wait_ge(moe_ok, 1)

            def body(g):
                for s in range(2):
                    t = 2 * g + s
                    need(act, "P7", "xT_ps", t + 1)
                    wait(act, l1_ps, g * 2 * EX - 1 + s)
                    cp(nbuf(s, 512, D), psT[s][:, 0:D]).then_inc(sg["xT_sb"], 1)
                for s in range(2):
                    need(act, "P7", "q_max", 2 * g + s + 1)
                    fn(nbuf(s, 4128, EX), nbuf(s, 4120, EX), ACT.Exp,
                       accum_out=nbuf(s, 4140, 1)).then_inc(sg["q_exp"], 1)
                for s in range(2):
                    need(act, "P7", "tT_ps", 2 * g + s + 1)
                    cp(nbuf(s, 2304, P)[0:EX, :], psT[s][0:EX, 384:512]).then_inc(sg["tT_sb"], 1)
                for e in range(EX):
                    for s in range(2):
                        n = g * 2 * EX + e * 2 + s
                        wait(act, l1_ps, n + 1)
                        wait(act, l2_ps, n - 1)
                        for m in range(KD):
                            i = e * KD + m
                            last = fn(nbuf(s, 768 + m * P, P), psB[s][:, m * P:(m + 1) * P], ACT.Relu,
                                      bias=moe[:, 1, i:i + 1], scale=moe[:, 0, i:i + 1])
                        last.then_inc(l1_sb, 1)
                    for s in range(2):
                        n = g * 2 * EX + e * 2 + s
                        wait(act, l2_ps, n + 1)
                        wait(act, lo_ps, n - 1)
                        for m in range(KD):
                            i = e * KD + m
                            last = fn(nbuf(s, 1024 + m * P, P), psB[s][:, 512 + m * P:512 + (m + 1) * P],
                                      ACT.Relu, bias=moe[:, 3, i:i + 1], scale=moe[:, 2, i:i + 1])
                        last.then_inc(l2_sb, 1)
            plain_groups(act, NG, body)

        @block.vector
        def _(v):
            ch = Chain(v, dve_step)
            link = ch.link
            tt, ts, stt = nc.vector.tensor_tensor, nc.vector.tensor_scalar, nc.vector.scalar_tensor_tensor
            red = nc.vector.tensor_reduce
            one = [0]

            def signal(ins):
                one[0] += 1
                ins.then_inc(dve_one, 1)
                v.wait_ge(dve_one, one[0])

            def stats(s, src, ph, var="var_ok", out_off=4108):
                link(nc.vector.bn_stats(nbuf(s, 4100, 6), nbuf(s, src, D)), True)
                link(nc.vector.bn_aggr(nbuf(s, 4106, 2), nbuf(s, 4100, 6)))
                ts(nbuf(s, out_off, 1), nbuf(s, 4107, 1), LN_EPS, None, ALU.add).then_inc(sg[var], 1)

            def normal(s, src, dst, name):
                ins = ts(nbuf(s, dst, D), nbuf(s, src, D), nbuf(s, 4106, 1), nbuf(s, 4110, 1),
                         ALU.subtract, ALU.mult)
                if name:
                    ins.then_inc(sg[name], 1)
                return ins

            link(nc.vector.memset(wt[:, :], 1.0))
            link(nc.vector.memset(wt[0:1, :], 0.0))
            nc.vector.memset(dots[:, :, :], 0.0)
            link(nc.vector.memset(headmask[:, :], 0.0))
            for h in range(HEADS):
                link(nc.vector.memset(headmask[h * DH:(h + 1) * DH, h * DH:(h + 1) * DH], 1.0))
            v.wait_ge(loaded, NLOAD)
            kvw = s_wkv.rearrange("p a (h d) -> p (a h) d", d=L0_DH)
            link(red(small[:, 0:2 * KD * L0_HEADS], kvw, AX.X, ALU.add))
            link(ts(small[:, 0:2 * KD * L0_HEADS], small[:, 0:2 * KD * L0_HEADS], 1.0 / L0_DH, None, ALU.mult))
            signal(tt(kvw, kvw, small[:, 0:2 * KD * L0_HEADS].unsqueeze(2).to_broadcast(
                [P, 2 * KD * L0_HEADS, L0_DH]), ALU.subtract))
            for k in range(KD):
                link(ts(w_qkv[:, k, :], w_qkv[:, k, :], col("g_pre", k), None, ALU.mult))
            v.wait_ge(pe_one, 1)
            for c in range(KD):
                link(ts(w_qk[:, c, :], psA[c][:, 0:D1], D ** -0.5, None, ALU.mult))
            signal(ts(qk_bias[:, :], psB[0][:, 0:D1], D ** -0.5, None, ALU.mult))

            flat = lambda r: r.rearrange("p a b -> p (a b)")
            link(nc.vector.tensor_copy(flat(c_dst), flat(c_dst).bitcast(I32)))
            link(nc.vector.tensor_copy(firsts, firsts.bitcast(I32)))
            link(nc.vector.memset(c_slot[:, :, 0:1], 0.0))
            link(tt(c_slot[:, :, 1:P], c_dst[:, :, 1:P], c_dst[:, :, 0:P - 1], ALU.not_equal))
            link(nc.vector.tensor_tensor_scan(flat(c_cum), flat(c_slot), flat(c_slot), 0.0, ALU.add, ALU.max))
            link(tt(chunkn[:, 0, 0:CT], c_cum[:, :, P - 1], c_cum[:, :, 0], ALU.subtract))
            link(ts(chunkn[:, 0, CT:2 * CT], chunkn[:, 0, 0:CT], float(FEW), None, ALU.is_ge))
            tt(c_slot, c_cum[:, :, P - 1:P].to_broadcast([P, CT, P]), c_cum, ALU.subtract).then_inc(lk, 1)
            v.wait_ge(consts, N_CONST)
            link(nc.vector.memset(zeros, 0.0))
            link(nc.vector.tensor_copy(riota[:, :], iotai[:, 0:P]))
            link(nc.vector.tensor_copy(piota[:, :], iotai[:, P:P + 1]))
            link(nc.vector.tensor_copy(nid[:, 0, :], iotai[:, P + 1:P + 1 + NT]))
            link(ts(nid[:, 1, :], nid[:, 0, :], 0.5, None, ALU.add))
            v.wait_ge(lk_ps, 1)
            link(nc.vector.tensor_copy(chunkn[:, 1, :], psA[0][:, 64:64 + 2 * CT]))
            for q in (slice(0, CT), slice(CT, 2 * CT)):
                link(nc.vector.tensor_tensor_scan(chunkn[:, 2, q], chunkn[:, 1, q], chunkn[:, 1, q], 0.0,
                                                  ALU.add, ALU.max))
            link(tt(chunkn[:, 2, :], chunkn[:, 2, :], chunkn[:, 1, :], ALU.subtract))
            link(tt(chunkn[:, 2, :], psA[0][:, 0:2 * CT], chunkn[:, 2, :], ALU.add))
            link(tt(chunkn[:, 3, 0:CT], chunkn[:, 2, 0:CT], chunkn[:, 0, 0:CT], ALU.add))
            link(ts(chunkn[:, 3, 0:CT], chunkn[:, 3, 0:CT], -1.0, float(N + 1), ALU.mult, ALU.add))
            link(stt(chunki[:, 0, :], chunkn[:, 0, CT:2 * CT], float(FULL), chunkn[:, 3, 0:CT],
                     ALU.mult, ALU.add))
            link(ts(chunkn[:, 3, CT:2 * CT], nid[:, 0, 0:CT], float(FEW), None, ALU.mult))
            link(stt(chunkn[:, 4, 0:CT], chunkn[:, 2, CT:2 * CT], float(P - FEW), chunkn[:, 3, CT:2 * CT],
                     ALU.mult, ALU.add))
            link(stt(chunki[:, 1, :], chunkn[:, 0, CT:2 * CT], float(FULL), chunkn[:, 4, 0:CT],
                     ALU.mult, ALU.add))
            link(nc.vector.tensor_copy(c_cum, c_slot))
            nc.vector.tensor_copy(c_cum[:, :, 0], chunkn[:, 4, 0:CT]).then_inc(lk, 1)

            v.wait_ge(consts, N_CONST)
            for i, l in ((0, "1"), (1, "2")):
                ts(moe[:, 4 + i, :], col("v" + l, 0, 2 * EX), BN_EPS, None, ALU.add).then_inc(moe_var, 1)
            v.wait_ge(moe_root, 2)
            for i, l in ((0, "1"), (1, "2")):
                scale, bias = moe[:, 2 * i, :], moe[:, 2 * i + 1, :]
                link(tt(scale, col("g" + l, 0, 2 * EX), moe[:, 4 + i, :], ALU.mult))
                link(tt(bias, col("b" + l, 0, 2 * EX), col("m" + l, 0, 2 * EX), ALU.subtract))
                link(tt(bias, bias, scale, ALU.mult))
                last = tt(bias, bias, col("be" + l, 0, 2 * EX), ALU.add)
                if i == 0:
                    link(last)
            last.then_inc(moe_ok, 1)

            def body(g):
                for s in range(2):
                    landed(v, "P1", s, g)
                    if not isinstance(g, int):
                        v.nop(nofuse=True)
                    stats(s, 0, "P1")
                for s in range(2):
                    need(v, "P1", "rstd_ok", 2 * g + s + 1)
                    stored(v, "P1", "a", s, g)
                    normal(s, 0, 256, "xn_ok")
                for s in range(2):
                    t = 2 * g + s
                    need(v, "P1", "ev_a", t + 1)
                    if not isinstance(g, int):
                        v.nop(nofuse=True)
                    h, wk, m8 = nbuf(s, 768, D), nbuf(s, 1024, D), nbuf(s, 4120, 8)
                    for r in range(TOPK_ROUNDS):
                        link(nc.vector.max(m8, h if r == 0 else wk), True)
                        link(nc.vector.match_replace(wk, m8, h if r == 0 else wk, NEG), r < TOPK_ROUNDS - 1)
                    stored(v, "P1", "b", s, g)
                    stt(nbuf(s, 1280, D), wk, NEG, h, ALU.is_equal, ALU.mult).then_inc(sg["hs_ok"], 1)
                    need(v, "P1", "ev_b", t + 1)
                    link(red(nbuf(s, 4128, 16), nbuf(s, 2560, 1024).rearrange("p (h d) -> p h d", d=L0_DH),
                             AX.X, ALU.add))
                    link(ts(nbuf(s, 4128, 16), nbuf(s, 4128, 16), 1.0 / L0_DH, LN_EPS, ALU.mult, ALU.add))
                    tt(nbuf(s, 4144, 8), nbuf(s, 4128, 8), nbuf(s, 4136, 8), ALU.mult).then_inc(sg["sq_red"], 1)
                for s in range(2):
                    t = 2 * g + s
                    need(v, "P1", "rstd_kv", t + 1)
                    need(v, "P1", "dots_ps", t - 1)
                    tt(nbuf(s, 3584, INNER).rearrange("p (h d) -> p h d", d=L0_DH),
                       nbuf(s, 1536 + INNER, INNER).rearrange("p (h d) -> p h d", d=L0_DH),
                       nbuf(s, 4160, 8).unsqueeze(2).to_broadcast([P, L0_HEADS, L0_DH]),
                       ALU.mult).then_inc(sg["v_ok"], 1)
                for s in range(2):
                    t = 2 * g + s
                    need(v, "P1", "dots_ps", t + 1)
                    need(v, "P1", "dots_ok", t)
                    dd = dots[:, :, :].rearrange("p a b -> p (a b)")
                    tt(dd, psB[1][:, 0:INNER], dd, ALU.add).then_inc(sg["dots_ok"], 1)
            ch.groups(NG, body)
            need(v, "P1", "dots_ok", NT)
            phase_end(v, 1)

            link(nc.vector.memset(dots[0:64, :, 64:128], 0.0))
            signal(nc.vector.memset(dots[64:128, :, 0:64], 0.0))
            v.wait_ge(pe_one, 3)
            for c in range(KD):
                signal(tt(w_mix[:, c, :], psA[c][:, 0:D], w_mix[:, c, :], ALU.add))

            look3 = [look[:, i, :] for i in range(6)]
            link(ts(look3[1], look3[1], float(C), 0.5, ALU.add, ALU.mult))
            link(ts(look3[1], look3[1], -1.0, 0.0, ALU.add, ALU.max))
            nc.vector.tensor_copy(cidx[:, :], look3[1]).then_inc(lk, 1)

            def body(g):
                for h in range(2):
                    n = 2 * g + h
                    v.wait_ge(lk_in[h], 16 * LK * (g + 1))
                    fd = found[:, h * LK:(h + 1) * LK, :]
                    tiles = bass.ds(n * LK, LK)
                    link(tt(match, fd[:, :, 1:P], nid[:, 0, tiles].unsqueeze(2).to_broadcast([P, LK, EC]),
                            ALU.is_equal))
                    link(red(look[:, 0, tiles], match, AX.X, ALU.max))
                    link(nc.vector.tensor_copy(look[:, 3, tiles], fd[:, :, P]))
                    link(tt(look[:, 5, tiles], fd[:, :, 0], nid[:, 0, tiles], ALU.is_equal))
                    link(tt(match, match, fd[:, :, P + 1:2 * P], ALU.mult))
                    red(look[:, 2, tiles], match, AX.X, ALU.max).then_inc(lk_ok, 1)
                    v.wait_ge(lk_ok, n + 1)
            ch.groups(NT // (2 * LK), body)
            v.sem_inc(lk, 1)
            link(stt(look3[5], look3[2], 0.0, look3[5], ALU.is_gt, ALU.mult))
            link(tt(look3[5], look3[5], look3[0], ALU.mult))
            link(ts(look3[1], look3[1], -float(C + 1), None, ALU.add))
            link(tt(look3[5], look3[5], look3[1], ALU.mult))
            link(ts(carryrow[:, :], look3[5], float(C), None, ALU.add))
            link(tt(look3[2], look3[3], look3[2], ALU.add))
            link(ts(look3[2], look3[2], -float(ZROW), None, ALU.add))
            link(tt(look3[2], look3[2], look3[0], ALU.mult))
            link(ts(sumrow[:, :], look3[2], float(ZROW), None, ALU.add))
            v.wait_ge(lk_ps, 2)
            link(nc.vector.tensor_copy(look3[3], psB[0][:, 64:64 + NT]))
            link(nc.vector.tensor_tensor_scan(look3[4], look3[3], look3[3], 0.0, ALU.add, ALU.max))
            link(tt(look3[4], look3[4], look3[3], ALU.subtract))
            link(tt(look3[4], psB[0][:, 0:NT], look3[4], ALU.add))
            link(ts(look3[4], look3[4], -1.0, float(N) + FAR, ALU.mult, ALU.add))
            link(stt(qrow[:, :], look3[0], -FAR, look3[4], ALU.mult, ALU.add))
            v.sem_inc(lk, 1)

            def sum_pass(c0, k0):
                def carry(c, s):
                    v.wait_ge(sum_sb, k0 + c + 1)
                    before = zrow[0:1, :] if isinstance(c, int) and c == 0 else ZR[0:1, (s - 1) % B, :]
                    if not isinstance(c, int) or k0 + c > 0:
                        v.wait_ge(carry_ok, k0 + c)
                    stt(ZR[0:1, s, :], before, slot_c[0:1, bass.ds(c, 1)], ZR[0:1, s, :],
                        ALU.mult, ALU.add).then_inc(carry_ok, 1)

                def body(it):
                    for s in range(B):
                        c = it * B + s
                        wait(v, sum_ps, c0 + c - B + 1)
                        ts(SEL[:, s, :], riota[:, :], slot_c[:, bass.ds(c, 1)], wt[:, bass.ds(c, 1)],
                           ALU.is_equal, ALU.mult).then_inc(sel_ok, 1)
                        if s >= LAG:
                            carry(c - LAG, s - LAG)
                        elif not (isinstance(it, int) and it == 0):
                            carry(c - LAG, s - LAG + B)
                body(0)
                body(1)
                with v.Fori(2, NB) as it:
                    body(it)
                for k in range(LAG):
                    carry(C - LAG + k, B - LAG + k)
            link(ts(slot_c[0:1, :], slot_c[0:1, :], 0.0, None, ALU.is_equal))
            nc.vector.memset(GR[:, :, D:D1], 1.0).then_inc(ones_ok, 1)
            sum_pass(0, 0)
            phase_end(v, 2)

            def body(g):
                for s in range(2):
                    t = 2 * g + s
                    landed(v, "P3", s, g)
                    sums_complete(v, "P3", t)
                    ag, c = nbuf(s, 512, D), nbuf(s, 4120, 1)
                    link(ts(c, nbuf(s, 512 + D, 1), 1.0, None, ALU.max))
                    link(nc.vector.reciprocal(c, c))
                    link(stt(ag, ag, c, nbuf(s, 0, D), ALU.mult, ALU.add))
                    link(tt(ag, ag, row("bout"), ALU.add))
                    need(v, "P3", "mm_a", t + 1)
                    need(v, "P3", "sum_ok", t - 1)
                    link(tt(nbuf(s, 1280, D), psA[s][:, 0:D], ag, ALU.add), True)
                    stats(s, 1280, "P3")
                for s in range(2):
                    t = 2 * g + s
                    need(v, "P3", "rstd_ok", t + 1)
                    stored(v, "P3", "a", s, g)
                    ins = normal(s, 1280, 1536, "xn_ok")
                    need(v, "P3", "xn_ok", t + 1)
                    link(stt(nbuf(s, 2048, D), nbuf(s, 1536, D), 1.0, row("wr"), ALU.mult, ALU.mult,
                             accum_out=nbuf(s, 4121, 1)))
                    link(ts(nbuf(s, 4122, 1), nbuf(s, 4121, 1), col("ffn_br"), None, ALU.add))
                    link(nc.vector.tensor_copy(w_all[:, bass.ds(t, 1)], nbuf(s, 4122, 1)))
                    stored(v, "P3", "c", s, g)
                    ts(nbuf(s, 2304, 1), nbuf(s, 4122, 1), padneg[:, bass.ds(t, 1)], None,
                       ALU.add).then_inc(sg["ev_a"], 1)
                    need(v, "P3", "ev_a", t + 1)
                    link(nc.vector.tensor_copy(w_rank[:, bass.ds(t, 1)], nbuf(s, 2304, 1)))
            ch.groups(NG, body)
            phase_end(v, 3)

            def body(g):
                for s in range(2):
                    t = 2 * g + s
                    link(ts(junk, w_bcast, w_rank[:, bass.ds(t, 1)], None, ALU.is_gt, ALU.add,
                            accum_out=nbuf(s, 4130, 1)))
                    link(nc.vector.tensor_copy(above[:, bass.ds(t, 1)], nbuf(s, 4130, 1)))
                    need(v, "P3b", "mm_a", t + 1)
                    stored(v, "P3b", "a", s, g)
                    link(tt(nbuf(s, 2048, D), psA[s][:, 0:D], row("ffn_b2"), ALU.add))
                    ts(nbuf(s, 2048, D), nbuf(s, 2048, D), w_all[:, bass.ds(t, 1)], None,
                       ALU.mult).then_inc(sg["res_ok"], 1)
            ch.groups(NG, body)
            phase_end(v, 4)

            link(ts(pick[:, 1, :], above[:, :], float(KEEP), NEG, ALU.is_ge, ALU.mult))
            link(stt(pick[:, 1, :], w_rank[:, :], -1.0, pick[:, 1, :], ALU.mult, ALU.add))
            assert one[0] == 5
            signal(red(small[:, 0:1], pick[:, 1, :], AX.X, ALU.max))
            v.wait_ge(pe_one, 4)
            signal(red(small[0:1, 1:2], psT[0][0:1, 0:P], AX.X, ALU.max))
            v.wait_ge(pe_one, 5)
            link(ts(small[:, 4:5], psT[0][:, P:P + 1], -1.0, None, ALU.mult))
            signal(ts(pick[:, 0, :], w_rank[:, :], small[:, 4:5], None, ALU.is_equal))
            v.wait_ge(pe_one, 6)
            link(nc.vector.tensor_copy(pick[:, 3, :], psT[1][:, 64:64 + NT]))
            link(nc.vector.memset(pick[:, 2, :], 0.0))
            link(nc.vector.tensor_tensor_scan(pick[:, 1, :], pick[:, 3, :], pick[:, 2, :], 0.0, ALU.add, ALU.add))
            link(tt(pick[:, 1, :], pick[:, 1, :], pick[:, 3, :], ALU.subtract))
            link(tt(pick[:, 1, :], psT[1][:, 0:NT], pick[:, 1, :], ALU.add))
            link(tt(pick[:, 1, :], pick[:, 1, :], pick[:, 0, :], ALU.mult))
            link(tt(pick[:, 1, :], pick[:, 1, :], above[:, :], ALU.add))
            signal(ts(sel[:, :], pick[:, 1, :], float(KEEP), None, ALU.is_lt))
            signal(nc.vector.memset(kmax[:, :], NEG))

            def body(g):
                for s in range(2):
                    t = 2 * g + s
                    landed(v, "P4", s, g)
                    stored(v, "P4", "a", s, g)
                    stt(nbuf(s, 512, D), nbuf(s, 256, D), sel[:, bass.ds(t, 1)], nbuf(s, 0, D),
                        ALU.mult, ALU.add).then_inc(sg["sum_ok"], 1)
                    need(v, "P4", "sum_ok", t + 1)
                    if not isinstance(g, int):
                        v.nop(nofuse=True)
                    stats(s, 512, "P4")
                for s in range(2):
                    t = 2 * g + s
                    need(v, "P4", "rstd_ok", t + 1)
                    stored(v, "P4", "b", s, g)
                    normal(s, 512, 768, "xn_ok")
                    need(v, "P4", "xn_ok", t + 1)
                    link(stt(nbuf(s, 2816, D), nbuf(s, 768, D), 1.0, nbuf(s, 768, D), ALU.mult, ALU.mult,
                             accum_out=nbuf(s, 4111, 1)))
                    ts(nbuf(s, 4112, 1), nbuf(s, 4111, 1), 1e-24, None, ALU.max).then_inc(sg["var2_ok"], 1)
                for s in range(2):
                    t = 2 * g + s
                    need(v, "P4", "mm_a", t + 1)
                    qk_stored(v, s, g)
                    tt(nbuf(s, 1280, D1), psA[s][:, 0:D1], qk_bias[:, :], ALU.add).then_inc(sg["ev_a"], 1)
                    need(v, "P4", "rstd2_ok", t + 1)
                    link(ts(nbuf(s, 4115, 1), nbuf(s, 4114, 1), float(D) ** 0.5, None, ALU.mult))
                    need(v, "P4", "mm_b", t + 1)
                    stored(v, "P4", "d", s, g, 2)
                    qkv = psB[s]
                    ts(nbuf(s, 1792 + HID, HID), qkv[:, 2 * HID:3 * HID], nbuf(s, 4115, 1), None, ALU.mult)
                    ts(nbuf(s, 1792, HID), qkv[:, HID:2 * HID], nbuf(s, 4115, 1), padneg[:, bass.ds(t, 1)],
                       ALU.mult, ALU.add).then_inc(sg["ev_b"], 1)
                    need(v, "P4", "ev_b", t + 1)
                    need(v, "P4", "hs_ok", t)
                    tt(kmax[:, :], kmax[:, :], nbuf(s, 1792, HID), ALU.max).then_inc(sg["hs_ok"], 1)
                    q3 = nbuf(s, 2048, HID).rearrange("p (h d) -> p h d", d=DH)
                    link(ts(nbuf(s, 2048, HID), qkv[:, 0:HID], nbuf(s, 4115, 1), None, ALU.mult))
                    link(red(nbuf(s, 4120, HEADS), q3, AX.X, ALU.max))
                    tt(q3, q3, nbuf(s, 4120, HEADS).unsqueeze(2).to_broadcast([P, HEADS, DH]),
                       ALU.subtract).then_inc(sg["q_max"], 1)
                for s in range(2):
                    t = 2 * g + s
                    need(v, "P4", "q_exp", t + 1)
                    e3 = nbuf(s, 2176, HID).rearrange("p (h d) -> p h d", d=DH)
                    link(red(nbuf(s, 4124, HEADS), e3, AX.X, ALU.add))
                    link(nc.vector.reciprocal(nbuf(s, 4124, HEADS), nbuf(s, 4124, HEADS)))
                    link(ts(nbuf(s, 4124, HEADS), nbuf(s, 4124, HEADS), DH ** -0.5, None, ALU.mult))
                    tt(nbuf(s, 2560, HID).rearrange("p (h d) -> p h d", d=DH), e3,
                       nbuf(s, 4124, HEADS).unsqueeze(2).to_broadcast([P, HEADS, DH]),
                       ALU.mult).then_inc(sg["res_ok"], 1)
            ch.groups(NG, body)
            need(v, "P4", "hs_ok", NT)
            phase_end(v, 5)

            v.wait_ge(pe_one, 7)
            link(red(small[:, 2:3], psT[0][:, 0:P], AX.X, ALU.max))
            link(red(small[:, 5:6], col("mem_k", 0, MEM), AX.X, ALU.max))
            signal(tt(small[:, 2:3], small[:, 2:3], small[:, 5:6], ALU.max))
            signal(ts(small[:, 3:4], small[:, 2:3], -1.0, None, ALU.mult))
            v.wait_ge(pe_one, 8)
            link(nc.vector.tensor_copy(kneg[:, :], psT[0][:, P:2 * P]))
            v.wait_ge(pe_one, 9)
            signal(nc.vector.tensor_copy(nbuf(0, 1024, P)[0:MEM, :], psT[1][0:MEM, 0:P]))
            v.wait_ge(pe_one, 10)
            link(nc.vector.tensor_copy(ctxv[:, :], psT[1][:, P:P + HID + 1]))
            for s in range(2):
                link(nc.vector.memset(nbuf(s, 640 + HID, 1), 1.0))

            def body(g):
                for s in range(2):
                    t = 2 * g + s
                    landed(v, "P4b", s, g)
                    need(v, "P4b", "mm_a", t - 1)
                    nc.vector.tensor_copy(nbuf(s, 640, HID), nbuf(s, HID, HID))
                    need(v, "P4b", "q_exp", t - 1)
                    tt(nbuf(s, 256, P), nbuf(s, 0, P), kneg[:, :], ALU.subtract).then_inc(sg["q_max"], 1)
                for s in range(2):
                    t = 2 * g + s
                    need(v, "P4b", "mm_a", t + 1)
                    need(v, "P4b", "ev_a", t)
                    tt(ctxv[:, :], psA[s][:, 0:HID + 1], ctxv[:, :], ALU.add).then_inc(sg["ev_a"], 1)
            ch.groups(NG, body)
            need(v, "P4b", "ev_a", NT)
            signal(nc.vector.reciprocal(small[:, 6:7], ctxv[:, HID:HID + 1]))
            signal(ts(ctxn[:, 0, :], ctxv[:, 0:HID], small[:, 6:7], None, ALU.mult))
            signal(tt(ctxn[:, 0, :], ctxn[:, 0, :], headmask[:, :], ALU.mult))
            v.wait_ge(pe_one, 12)
            link(nc.vector.tensor_copy(w_m2[:, :], psA[0][:, 0:D]))
            phase_end(v, 6)

            link(nc.vector.memset(reg_g[:, 0:2 * B * D1], 0.0))
            nc.vector.memset(GR[:, :, D:D1], 1.0).then_inc(q_clear, 1)
            v.wait_ge(q_clear, 1)

            def scored_chunk(c, s, rnd):
                v.wait_ge(sum_ps, C + c + 1)
                v.wait_ge(g_sem[s], 16 * NB + 16 * (rnd + 1))
                wait(v, scored, c)
                stt(nbuf(0, 0, D1), psZ[s % 4][:, 0:D1], 1.0, GR[:, s, :], ALU.mult, ALU.mult,
                    accum_out=scol[:, s:s + 1]).then_inc(scored, 1)
                if s % H == H - 1:
                    v.wait_ge(scored, c + 1)
                    link(nc.vector.tensor_copy(score_c[:, bass.ds(c - (H - 1), H)], scol[:, s - (H - 1):s + 1]))

            def body(it):
                for s in range(B):
                    c = it * B + s
                    if s % H == 0:
                        h = s // H
                        nc.vector.tensor_copy(dcol[:, h, :], slot_c[:, bass.ds(c, H)]).then_inc(dcol_ok, 1)
                    if s % 4 == 0:
                        v.wait_ge(row_ps, c + 4)
                    wait(v, sum_ps, C + c - B + 1)
                    k = s % H
                    ts(SEL[:, s, :], psT[k // 4][:, (k % 4) * P:(k % 4 + 1) * P], piota[:, :], None,
                       ALU.is_equal).then_inc(sel_ok, 1)
                    if s >= LAG:
                        scored_chunk(c - LAG, s - LAG, it)
                    elif not (isinstance(it, int) and it == 0):
                        scored_chunk(c - LAG, s - LAG + B, it - 1)
            ch.groups(NB, body, peel=2)
            for k in range(LAG):
                scored_chunk(C - LAG + k, B - LAG + k, NB - 1)
            v.sem_inc(scores_ok, 1)
            v.wait_ge(misc, 96 + 16 * CT)
            link(nc.vector.memset(reg_g[:, 0:CT * P].rearrange("p (i q) -> p i q", q=P)[:, :, 0:1], 0.0))
            link(tt(s_prev, s_b.bitcast(I32), s_a.bitcast(I32), ALU.is_equal))
            link(tt(s_next, s_b.bitcast(I32), s_next.bitcast(I32), ALU.is_equal))
            link(stt(s_a, s_c, col("we"), score, ALU.mult, ALU.add))
            link(ts(score, s_a, col("be"), None, ALU.add))

            def scan(dst, keep, x, op0, op1, neutral, back, i):
                def d(ap):
                    return ap[:, ::-1] if back else ap
                link(nc.vector.tensor_tensor_scan(d(dst), d(keep), d(x), neutral, op0, op1))
                link(nc.vector.tensor_copy(small[:, 16:17], dst[:, 0:1] if back else dst[:, CR - 1:CR]))
                red(small[:, 17:18], keep, AX.X, ALU.min).then_inc(scan_ok, 1)
                v.wait_ge(pe_one, 13 + 2 * i)
                link(nc.vector.tensor_copy(srow[0:1, 0, :], psA[0][0:1, 0:P]))
                link(nc.vector.tensor_copy(srow[0:1, 1, :], psA[0][0:1, P:2 * P]))
                r = (lambda k: srow[0:1, k, ::-1]) if back else (lambda k: srow[0:1, k, :])
                link(nc.vector.tensor_tensor_scan(r(2), r(1), r(0), neutral, op0, op1))
                link(nc.vector.memset(srow[0:1, 3, :], neutral))
                into, of = (slice(0, P - 1), slice(1, P)) if back else (slice(1, P), slice(0, P - 1))
                nc.vector.tensor_copy(srow[0:1, 3, into], srow[0:1, 2, of]).then_inc(scan_ok, 1)
                v.wait_ge(pe_one, 14 + 2 * i)
                link(nc.vector.tensor_copy(small[:, 18:19], psA[1][:, 0:1]))
                link(nc.vector.tensor_tensor_scan(d(dst), d(keep), d(x), small[:, 18:19], op0, op1))

            link(ts(s_a, s_prev, 1.0, BIG, ALU.subtract, ALU.mult))
            scan(s_b, s_a, score, ALU.add, ALU.max, -BIG, False, 0)
            link(ts(s_a, s_next, 1.0, BIG, ALU.subtract, ALU.mult))
            scan(s_c, s_a, s_b, ALU.add, ALU.max, -BIG, True, 1)
            tt(s_c, score, s_c, ALU.subtract).then_inc(shifted, 1)
            v.wait_ge(act_one, 4)
            scan(s_b, s_prev, s_c, ALU.mult, ALU.add, 0.0, False, 2)
            link(ts(s_a, s_next, -1.0, 1.0, ALU.mult, ALU.add))
            link(tt(s_b, s_b, s_a, ALU.mult))
            scan(s_a, s_next, s_b, ALU.mult, ALU.add, 0.0, True, 3)
            link(ts(s_a, s_a, 1e-12, None, ALU.max))
            link(nc.vector.reciprocal(s_a, s_a))
            tt(s_c, s_c, s_a, ALU.mult).then_inc(attention_ok, 1)
            phase_end(v, 7)
            nc.vector.memset(GR[:, :, D:D1], 1.0).then_inc(ones_ok, 1)
            sum_pass(2 * C, C)
            phase_end(v, 8)

            def body(g):
                for s in range(2):
                    t = 2 * g + s
                    landed(v, "P6", s, g)
                    sums_complete(v, "P6", t)
                    need(v, "P6", "mm_a", t + 1)
                    r, m, xn2 = nbuf(s, 2944, D), nbuf(s, 1664, D), nbuf(s, 256, D)
                    link(tt(r, psA[s][:, 0:D], row("bs"), ALU.add))
                    tt(m, psA[s][:, D:2 * D], row("b_out"), ALU.add).then_inc(sg["ev_a"], 1)
                    need(v, "P6", "ev_a", t + 1)
                    link(stt(r, row("bv"), nbuf(s, 512 + D, 1), r, ALU.mult, ALU.add))
                    link(tt(r, r, xn2, ALU.add), True)
                    link(stt(nbuf(s, 3200, D), m, 1.0, m, ALU.mult, ALU.mult, accum_out=nbuf(s, 4111, 1)))
                    ts(nbuf(s, 4112, 1), nbuf(s, 4111, 1), 1e-24, None, ALU.max).then_inc(sg["sq_red"], 1)
                    stats(s, 2944, "P6")
                for s in range(2):
                    t = 2 * g + s
                    z, m = nbuf(s, 1920, D), nbuf(s, 1664, D)
                    need(v, "P6", "rstd_ok", t + 1)
                    link(normal(s, 2944, 1920, None))
                    link(tt(z, z, row("g1"), ALU.mult))
                    tt(z, z, row("b1"), ALU.add).then_inc(sg["xn_ok"], 1)
                    need(v, "P6", "rstd_kv", t + 1)
                    link(ts(nbuf(s, 4115, 1), nbuf(s, 4114, 1), float(D) ** 0.5, None, ALU.mult))
                    link(stt(m, m, nbuf(s, 4115, 1), row("g_out"), ALU.mult, ALU.mult))
                    link(tt(m, m, nbuf(s, 256, D), ALU.add))
                for s in range(2):
                    t = 2 * g + s
                    u = nbuf(s, 3200, D)
                    need(v, "P6", "mm_b", t + 1)
                    need(v, "P6", "xn_ok", t + 1)
                    link(tt(u, psT[s][:, D:2 * D], row("b_ff2"), ALU.add))
                    link(tt(u, u, nbuf(s, 1920, D), ALU.add), True)
                    stats(s, 3200, "P6", "var2_ok")
                for s in range(2):
                    t = 2 * g + s
                    u, x3 = nbuf(s, 3200, D), nbuf(s, 3584, D)
                    need(v, "P6", "rstd2_ok", t + 1)
                    link(normal(s, 3200, 3200, None))
                    link(tt(u, u, row("g2"), ALU.mult))
                    link(tt(u, u, row("b2"), ALU.add))
                    link(tt(u, u, nbuf(s, 1664, D), ALU.add))
                    stored(v, "P6", "a", s, g)
                    tt(x3, u, nbuf(s, 0, D), ALU.add).then_inc(sg["res_ok"], 1)
                    need(v, "P6", "res_ok", t + 1)
                    if not isinstance(g, int):
                        v.nop(nofuse=True)
                    stats(s, 3584, "P6", "v_ok")
                for s in range(2):
                    t = 2 * g + s
                    need(v, "P6", "rstd3_ok", t + 1)
                    stored(v, "P6", "b", s, g)
                    normal(s, 3584, 3840, "dots_ok")
            ch.groups(NG, body)
            phase_end(v, 9)

            def body(g):
                for s in range(2):
                    wait(v, lo_ok, g * 2 * EX - 1 + s)
                    need(v, "P7", "mm_a", 2 * g + s + 1)
                    lg = nbuf(s, 4120, EX)
                    link(tt(lg, psT[s][:, D:D + EX], col("moe_br", 0, EX), ALU.add))
                    link(red(nbuf(s, 4137, 1), lg, AX.X, ALU.max))
                    ts(lg, lg, nbuf(s, 4137, 1), None, ALU.subtract).then_inc(sg["q_max"], 1)
                for s in range(2):
                    need(v, "P7", "q_exp", 2 * g + s + 1)
                    link(nc.vector.reciprocal(nbuf(s, 4141, 1), nbuf(s, 4140, 1)))
                    ts(nbuf(s, 4120, EX), nbuf(s, 4128, EX), nbuf(s, 4141, 1), None,
                       ALU.mult).then_inc(sg["sum_ok"], 1)
                for s in range(2):
                    t = 2 * g + s
                    landed(v, "P7", s, g)
                    need(v, "P7", "mm_b", t + 1)
                    tt(nbuf(s, 1536, D), psA[s][:, 0:D], nbuf(s, 0, D), ALU.add).then_inc(sg["ev_a"], 1)
                for e in range(EX):
                    for s in range(2):
                        n = g * 2 * EX + e * 2 + s
                        wait(v, lo_ps, n + 1)
                        if e == 0:
                            need(v, "P7", "ev_a", 2 * g + s + 1)
                        else:
                            v.wait_ge(lo_ok, n - 1)
                        dst = 1536
                        if e == EX - 1:
                            stored(v, "P7", "a", s, g)
                            dst = 1792
                        stt(nbuf(s, dst, D), psA[s][:, 0:D], nbuf(s, 4120 + e, 1), nbuf(s, 1536, D),
                            ALU.mult, ALU.add).then_inc(lo_ok, 1)
            ch.groups(NG, body)


def kernel(**inputs):
    import concourse.bacc as bacc
    from concourse.bass_utils import run_bass_kernel_spmd

    x = {k: np.asarray(v) for k, v in inputs.items()}

    def fold_rows(w):
        k = w.shape[0] // P
        return w.reshape(k, P, w.shape[1]).transpose(1, 0, 2).reshape(P, k * w.shape[1])

    def columns(v):
        return v.reshape(-1, P).T

    def every(v):
        return np.broadcast_to(v.reshape(1, -1), (P, v.size))

    def experts(w):
        return w.reshape(EX, KD, P, D).transpose(2, 0, 1, 3).reshape(P, EX * KD * D)

    src = np.concatenate([x["src"], np.zeros(C * EC - E, np.int32)])
    dst = np.concatenate([x["dst"], np.full(CR * P - E, N, np.int32)])
    none = np.full(1, -1, np.int32)
    prev, nxt = np.concatenate([none, dst[:-1]]), np.concatenate([dst[1:], none])
    ew = np.concatenate([x["edge_weight"], np.zeros(CR * P - E, np.float32)])
    over = np.full((CT * P, P), N, np.int32)
    over[:C, 1:] = dst[:C * EC].reshape(C, EC)
    over[:C, 0] = prev[:C * EC:EC]
    f = "L1_ffn_"
    parts = {"ffn_b1": columns(x["L0_ffn_b1"]), "b_ff1": columns(x["L1_gnn_b_ff1"]),
             "g_pre": columns(x["L1_mix_g_pre"]), "bq": columns(x["L1_gnn_bq"]),
             "ffn_br": every(x["L0_ffn_br"]), "we": every(x["L1_gnn_we"]), "be": every(x["L1_gnn_be"]),
             "moe_br": every(x[f + "br"]), "mem_k": x["L1_mix_mem_kv"][0].reshape(HID, MEM)}
    for n in ("b1", "g1", "be1", "m1", "v1", "b2", "g2", "be2", "m2", "v2"):
        parts[n] = columns(x[f + n].reshape(-1))
    rowv = {"bout": "L0_mix_bout", "wr": "L0_ffn_wr", "ffn_b2": "L0_ffn_b2", "bs": "L1_gnn_bs", "bv": "L1_gnn_bv",
            "g1": "L1_gnn_g1", "b1": "L1_gnn_b1", "g2": "L1_gnn_g2", "b2": "L1_gnn_b2",
            "b_ff2": "L1_gnn_b_ff2", "b_out": "L1_mix_b_out", "g_out": "L1_mix_g_out"}
    arrays = {
        "x": np.concatenate([x["x"], np.zeros((NP - N, D), np.float32)]),
        "src_c": np.concatenate([np.zeros((1, C), np.int32), src.reshape(C, EC).T]),
        "dst_r": dst.reshape(P, CR), "dprev_r": prev.reshape(P, CR), "dnext_r": nxt.reshape(P, CR),
        "dst_ov": over.reshape(CT, P, P).transpose(1, 0, 2).reshape(P, CT * P), "first": every(over[:C, 1]),
        "ew_r": ew.reshape(P, CR),
        "rows": np.concatenate([every(x[rowv[n]]) for n in ROWS], 1),
        "cols": np.concatenate([parts[n] for n in COLS], 1),
        "W_neigh": fold_rows(x["L0_gnn_W_neigh"]), "W_self": fold_rows(x["L0_gnn_W_self"]),
        "Wkv": fold_rows(x["L0_mix_Wqkv"][INNER:].T), "Wq": fold_rows(x["L0_mix_Wqkv"][:INNER]),
        "WoutT": fold_rows(x["L0_mix_Wout"].T), "w1": fold_rows(x["L0_ffn_w1"]), "w2": fold_rows(x["L0_ffn_w2"]),
        "wqT": fold_rows(x["L1_gnn_wq"].T),
        "wkTb": fold_rows(np.concatenate([x["L1_gnn_wk"].T, x["L1_gnn_bk"].reshape(D, 1)], 1)),
        "w_qkv": fold_rows(x["L1_mix_w_qkv"]), "w_out": x["L1_mix_w_out"],
        "wv": fold_rows(x["L1_gnn_wv"]), "ws": fold_rows(x["L1_gnn_ws"]),
        "w_ff1": fold_rows(x["L1_gnn_w_ff1"]), "w_ff2": fold_rows(x["L1_gnn_w_ff2"]),
        "Wr": fold_rows(x[f + "Wr"]), "bo": x[f + "bo"],
        "mem_v": x["L1_mix_mem_kv"][1].reshape(HID, MEM).T,
        "W1": experts(x[f + "W1"]), "W2": experts(x[f + "W2"]), "Wo": experts(x[f + "Wo"]),
    }
    arrays = {"in_" + k: np.ascontiguousarray(v) for k, v in arrays.items()}
    nc = bacc.Bacc("TRN2", target_bir_lowering=False, num_devices=1)
    aps = {k[3:]: nc.dram_tensor(k, v.shape, mybir.dt.from_np(v.dtype), kind="ExternalInput").ap()
           for k, v in arrays.items()}
    out = nc.dram_tensor("out_0", (N, D), F32, kind="ExternalOutput").ap()
    build(nc, aps, out)
    r = run_bass_kernel_spmd(nc, [arrays], core_ids=[0])
    return r.results[0]["out_0"]
```

```python
import numpy as np
import concourse.bass as bass
import concourse.mybir as mybir
from contextlib import ExitStack

F32 = mybir.dt.float32
I32 = mybir.dt.int32
BF16 = mybir.dt.bfloat16
ALU = mybir.AluOpType
ACT = mybir.ActivationFunctionType
AX = mybir.AxisListType

P = 128
N = 6250
E = 206250
D = 256
KD = D // P
D1 = D + 1
NT = 50
NG = NT // 2
NP = NT * P
TAIL = N - (NT - 2) * P
EC = P - 1
H = 8
B = 2 * H
NB = -(-E // (EC * B))
C = B * NB
CT = -(-C // P)
CR = -(-C * EC // P)
FF_COLS = 4170
CARRY_LAG = 5
LAG = 4
FEW = 16
ZPER = 11
SUMROWS = NT * ZPER * P
ZROW = SUMROWS - P
assert C * FEW + (N + 1) // FEW * (P - FEW) <= ZROW
FULL = 1 << 17
assert FULL > SUMROWS and FULL > NT * P
LK = 5
TOPK_ROUNDS = 32 // 8
L0_HEADS, L0_DH = 8, 64
INNER = L0_HEADS * L0_DH
PAIRS = INNER // P
FF = 4 * D
KF = FF // P
KEEP = max(1, int(0.5 * N)) - 1
HEADS, DH, MEM = 4, 32, 4
HID = HEADS * DH
FF1 = 2 * D
K1 = FF1 // P
EX = 8
LN_EPS = 1e-5
BN_EPS = 1e-3
BIG = 1e30
FAR = 65536.0
NEG = -3.0e38

ROWS = ["bout", "wr", "ffn_b2", "bs", "bv", "g1", "b1", "g2", "b2", "b_ff2", "b_out", "g_out"]
COLS = {"ffn_b1": KF, "b_ff1": K1, "g_pre": KD, "bq": KD, "ffn_br": 1, "we": 1, "be": 1, "moe_br": EX,
        "b1": 2 * EX, "g1": 2 * EX, "be1": 2 * EX, "m1": 2 * EX, "v1": 2 * EX,
        "b2": 2 * EX, "g2": 2 * EX, "be2": 2 * EX, "m2": 2 * EX, "v2": 2 * EX, "mem_k": MEM}
ROW = {n: i for i, n in enumerate(ROWS)}
COL, NCOL = {}, 0
for _n, _k in COLS.items():
    COL[_n] = NCOL
    NCOL += _k


def wait(eng, sem, value):
    if isinstance(value, int) and value <= 0:
        return
    eng.wait_ge(sem, value)


class Chain:

    def __init__(self, eng, sem):
        self.eng, self.sem, self.base, self.k, self.g, self.per = eng, sem, 0, 0, None, 0

    def link(self, ins, fence=False):
        self.k += 1
        ins.then_inc(self.sem, 1)
        self.settle(fence)

    def near(self, ins, fence=False):
        self.k += 1
        ins.then_inc(self.sem, 1)
        self.settle(fence, 1)

    def settle(self, fence=False, under_way=0):
        v = self.base + self.k - under_way
        if self.g is not None:
            v = self.base + (self.g - self.first) * self.per + self.k - under_way
        self.eng.wait_ge(self.sem, v)
        if fence and self.g is not None:
            self.eng.nop(nofuse=True)

    def groups(self, count, body, peel=1, start=0):
        begin, peel = start, start + peel
        for g in range(begin, peel):
            start = self.k
            body(g)
        self.per = self.k - start
        self.base, self.k, self.first = self.base + self.k, 0, peel
        with self.eng.Fori(peel, count) as g:
            self.g = g
            body(g)
            self.g = None
        assert self.k == self.per
        self.base, self.k = self.base + (count - peel) * self.per, 0


def plain_groups(eng, count, body):
    body(0)
    with eng.Fori(1, count) as g:
        body(g)


def ahead_groups(eng, count, body):
    body(0)
    with eng.Fori(1, count - 1) as g:
        body(g)
    body(count - 1, True)


def build(nc, a, out):
    ctx = ExitStack()
    with ctx:
        def sb(name, shape, dt=F32):
            return ctx.enter_context(nc.sbuf_tensor(name, shape, dt))

        def sem(name):
            return ctx.enter_context(nc.semaphore(name))

        def table(name, width):
            return nc.dram_tensor(name, (NP, width), F32).ap()

        t_xn, t_hs, t_xn1, t_xs, t_y = (table(n, D) for n in ("t_xn", "t_hs", "t_xn1", "t_xs", "t_y"))
        t_x2, t_xn2, t_x3, t_xn3 = (table(n, D) for n in ("t_x2", "t_xn2", "t_x3", "t_xn3"))
        t_qk = table("t_qk", D1)
        t_sum = nc.dram_tensor("t_sum", (SUMROWS, D1), F32).ap()
        t_chunk = nc.dram_tensor("t_chunk", (CT * P, 2 * P), F32).ap()
        t_carry = nc.dram_tensor("t_carry", (C + 1, D1), F32).ap()
        t_ni = nc.dram_tensor("t_ni", (2, CT * P), I32).ap()
        t_kv, t_q = table("t_kv", 2 * HID), table("t_q", HID)
        t_w = nc.dram_tensor("t_w", (1, NP), F32).ap()
        t_att = nc.dram_tensor("t_att", (1, CR * P), F32).ap()
        t_score = nc.dram_tensor("t_score", (1, CR * P), F32).ap()

        src_c = sb("src_c", [P, C], I32)
        slot_c = sb("slot_c", [P, C])
        wt = sb("wt", [P, C])
        reg_s = sb("reg_s", [P, 5 * CR + C])
        reg_g = sb("reg_g", [P, 2 * B * D1 + B * P])
        w_mix = sb("w_mix", [P, KD, D])
        w_qk = sb("w_qk", [P, KD, D1])
        w_qkv = sb("w_qkv", [P, KD, 3 * HID])
        w_out = sb("w_out", [P, D])
        w_m2 = sb("w_m2", [P, D])
        w_v = sb("w_v", [P, KD, D])
        w_s = sb("w_s", [P, KD, D])
        w_ff1 = sb("w_ff1", [P, KD, FF1])
        w_ff2 = sb("w_ff2", [P, K1, D])
        w_r = sb("w_r", [P, KD, EX])
        w_bo = sb("w_bo", [EX, D])
        mem_v = sb("mem_v", [MEM, HID + 1])
        rows = sb("rows", [P, len(ROWS), D])
        cols = sb("cols", [P, NCOL])
        qk_bias = sb("qk_bias", [P, D1])
        nb = sb("nb", [P, 2, 4200])
        ident = sb("ident", [P, P])
        lower = sb("lower", [P, P])
        ones = sb("ones", [P, P])
        riota = sb("riota", [P, P])
        piota = sb("piota", [P, 1])
        iotai = sb("iotai", [P, P + 1 + NT], I32)
        nid = sb("nid", [P, 2, NT])
        look = sb("look", [P, 6, NT])
        cidx = sb("cidx", [P, NT], I32)
        sumrow = sb("sumrow", [P, NT], I32)
        carryrow = sb("carryrow", [P, NT], I32)
        qrow = sb("qrow", [P, NT], I32)
        chunkn = sb("chunkn", [P, 5, 2 * CT])
        chunki = sb("chunki", [P, 2, CT], I32)
        nrow = sb("nrow", [1, 2, CT * P], I32)
        lidx = sb("lidx", [P, 2, LK], I32)
        tidx = sb("tidx", [P, 4], I32)
        half = sb("half", [P, 16])
        headmask = sb("headmask", [P, P])
        padneg = sb("padneg", [P, NT])
        dots = sb("dots", [P, PAIRS, P])
        fold = sb("fold", [P, PAIRS, D])
        w_all = sb("w_all", [P, NT])
        w_rank = sb("w_rank", [P, NT])
        above = sb("above", [P, NT])
        sel = sb("sel", [P, NT])
        pick = sb("pick", [P, 4, NT])
        kmax = sb("kmax", [P, HID])
        kneg = sb("kneg", [P, HID])
        ctxv = sb("ctxv", [P, HID + 1])
        ctxn = sb("ctxn", [P, 2, P])
        small = sb("small", [P, 64])
        srow = sb("srow", [1, 4, P])
        moe = sb("moe", [P, 6, 2 * EX])
        sidx = sb("sidx", [P, 2, H], I32)
        dcol = sb("dcol", [P, 2, H])
        scol = sb("scol", [P, B])
        zrow = sb("zrow", [P, D1])

        def view(reg, off, *dims):
            n = 1
            for d in dims:
                n *= d
            v = reg[:, off:off + n]
            if len(dims) == 2:
                v = v.rearrange("p (a b) -> p a b", b=dims[1])
            if len(dims) == 3:
                v = v.rearrange("p (a b c) -> p a b c", b=dims[1], c=dims[2])
            return v

        s_wneigh = view(reg_s, 0, KD, D)
        s_wkv = view(reg_s, 512, KD, 2 * INNER)
        s_wq = view(reg_s, 2560, PAIRS, D)
        s_wout = view(reg_s, 3584, PAIRS, D)
        s_w1 = view(reg_s, 4608, KD, FF)
        s_w2 = view(reg_s, 6656, KF, D)
        s_wqT = view(reg_s, 8704, KD, D)
        s_wkT = fold[:, :, :].rearrange("p a b -> p (a b)")[:, 0:KD * D1].rearrange("p (a b) -> p a b", b=D1)
        score, s_prev, s_next, s_a, s_b, s_c = (view(reg_s, i * CR, CR) for i in range(6))
        score_c = view(reg_s, 5 * CR, C)
        s_wo = view(reg_s, 0, EX, KD, D)
        GR = view(reg_g, 0, B, D1)
        ZR = view(reg_g, B * D1, B, D1)
        SEL = view(reg_g, 2 * B * D1, B, P)
        c_dst, c_cum, c_slot = (view(reg_g, i * CT * P, CT, P) for i in range(3))
        firsts = view(reg_g, 3 * CT * P, C)
        sign_junk = reg_g[:, 3 * CT * P + C:3 * CT * P + C + C // 2].bitcast(BF16)
        zeros = reg_g[:, 3 * CT * P + C + C // 2:3 * CT * P + C + C // 2 + ZPER * D1]
        found = view(reg_g, 0, 2 * LK, 2 * P)
        match = view(reg_g, 2 * LK * 2 * P, LK, EC)
        w_bcast = view(reg_g, 0, NP)
        junk = reg_g[:, NP:NP + NP // 2].bitcast(BF16)
        g_w1 = view(reg_g, 0, EX, KD, D)
        g_w2 = view(reg_g, 4096, EX, KD, D)

        ff_rest = view(reg_s, EX * KD * D, 2, D)
        square_junk = view(reg_s, EX * KD * D + 2 * D, 2, D)
        carried = view(reg_g, 8192, 2, D1)

        psT = [ctx.enter_context(nc.psum_tensor(f"psT{i}", [P, 512], F32)) for i in range(2)]
        psA = [ctx.enter_context(nc.psum_tensor(f"psA{i}", [P, 512], F32)) for i in range(2)]
        psB = [ctx.enter_context(nc.psum_tensor(f"psB{i}", [P, 1024], F32)) for i in range(2)]
        psZ = [psA[0], psA[1], psB[0], psB[1]]

        def nbuf(s, off, n):
            return nb[:, s, off:off + n]

        def row(name):
            return rows[:, ROW[name], :]

        def col(name, i=0, n=1):
            return cols[:, COL[name] + i:COL[name] + i + n]

        loaded = sem("loaded")
        consts = sem("consts")
        phase = sem("phase")
        dve_step, pool_step, act_step = sem("dve_step"), sem("pool_step"), sem("act_step")
        ld = [sem("ld0"), sem("ld1")]
        sta = [sem("sta0"), sem("sta1")]
        stb = [sem("stb0"), sem("stb1")]
        stc = [sem("stc0"), sem("stc1")]
        std = [sem("std0"), sem("std1")]
        summed = sem("summed")
        c_sem = [sem("c_sem0"), sem("c_sem1")]
        ld_sum = [sem("ld_sum0"), sem("ld_sum1")]
        st_qk = [sem("st_qk0"), sem("st_qk1")]
        zeroed = sem("zeroed")
        lk, lk_ps, lk_g, lk_ok, lk_st, turned_ps, turned_sb = (
            sem(n) for n in ("lk", "lk_ps", "lk_g", "lk_ok", "lk_st", "turned_ps", "turned_sb"))
        lk_in = [sem("lk_in0"), sem("lk_in1")]
        g_sem = [sem(f"gather{i}") for i in range(B)]
        z_sem = [sem(f"scatter{i}") for i in range(B)]
        misc = sem("misc")

        names = ["xT_ps", "xT_sb", "var_ok", "rstd_ok", "xn_ok", "mm_a", "mm_b", "ev_a", "ev_b", "hs_ok",
                 "sq_red", "rstd_kv", "v_ok", "dots_ps", "dots_ok", "sum_ok", "res_ok", "tT_ps", "tT_sb",
                 "ff_ps", "ff_sb", "q_max", "q_exp", "var2_ok", "rstd2_ok", "rstd3_ok"]
        sg = {n: sem(n) for n in names}
        pe_one, dve_one, act_one = sem("pe_one"), sem("dve_one"), sem("act_one")
        idx_ok, dcol_ok, row_ps, sel_ok, sum_ps, sum_sb, carry_ok, scored = (
            sem(n) for n in ("idx_ok", "dcol_ok", "row_ps", "sel_ok", "sum_ps", "sum_sb", "carry_ok", "scored"))
        scan_ok, shifted, attention_ok, moe_var, moe_root, moe_ok, q_clear, ones_ok, tidx_ok, scores_ok = (
            sem(n) for n in ("scan_ok", "shifted", "attention_ok", "moe_var", "moe_root", "moe_ok", "q_clear",
                             "ones_ok", "tidx_ok", "scores_ok"))
        l1_ps, l1_sb, l2_ps, l2_sb, lo_ps, lo_ok = (
            sem(n) for n in ("l1_ps", "l1_sb", "l2_ps", "l2_sb", "lo_ps", "lo_ok"))

        used = {"P1": ["xT_ps", "xT_sb", "var_ok", "rstd_ok", "xn_ok", "mm_a", "mm_b", "ev_a", "ev_b", "hs_ok",
                       "sq_red", "rstd_kv", "v_ok", "dots_ps", "dots_ok"],
                "P3": ["xT_ps", "xT_sb", "var_ok", "rstd_ok", "xn_ok", "mm_a", "ev_a", "sum_ok"],
                "P3b": ["xT_ps", "xT_sb", "mm_b", "ev_b", "mm_a", "res_ok"],
                "P4": ["xT_ps", "xT_sb", "var_ok", "rstd_ok", "xn_ok", "mm_a", "ev_a", "mm_b", "ev_b",
                       "q_max", "q_exp", "res_ok", "var2_ok", "rstd2_ok", "sum_ok", "hs_ok"],
                "P4b": ["q_max", "q_exp", "mm_a", "ev_a"],
                "P6": ["xT_ps", "xT_sb", "mm_a", "ev_a", "var_ok", "rstd_ok", "xn_ok", "tT_ps", "tT_sb",
                       "ff_ps", "ff_sb", "mm_b", "var2_ok", "rstd2_ok", "sq_red", "rstd_kv", "res_ok",
                       "dots_ok", "v_ok", "rstd3_ok", "hs_ok"],
                "P7": ["xT_ps", "xT_sb", "mm_a", "q_max", "q_exp", "tT_ps", "tT_sb", "res_ok", "ev_a", "mm_b",
                       "sum_ok"]}
        bases, count = {}, {n: 0 for n in names}
        for ph, ns in used.items():
            bases[ph] = dict(count)
            for n in ns:
                count[n] += NT
        ld_base, k = {}, 0
        for ph, n in (("P1", 1), ("P3", 2), ("P3b", 1), ("P4", 2), ("P4b", 1), ("P6", 3), ("P7", 2)):
            ld_base[ph] = (k, 16 * n)
            k += 16 * n * NG
        st_used = {"P1": "ab", "P3": "abc", "P3b": "a", "P4": "abd", "P4b": "", "P6": "ab", "P7": "a"}
        st_base, cnt = {}, {c: 0 for c in "abcd"}
        st_extra = {"P4": {"d": 1}}
        for ph, cs in st_used.items():
            st_base[ph] = dict(cnt)
            for c in cs:
                cnt[c] += 16 * NG * (1 + st_extra.get(ph, {}).get(c, 0))
        stores = {"a": sta, "b": stb, "c": stc, "d": std}

        def sig(ph, n):
            assert n in used[ph], (ph, n)
            return sg[n], bases[ph][n]

        def need(eng, ph, n, value):
            if isinstance(value, int) and value <= 0:
                return
            s, b = sig(ph, n)
            eng.wait_ge(s, b + value)

        def stored(eng, ph, c, s, g, per=1):
            assert c in st_used[ph]
            if isinstance(g, int) and g <= 0:
                return
            eng.wait_ge(stores[c][s], st_base[ph][c] + 16 * per * g)

        def landed(eng, ph, s, g):
            b, per = ld_base[ph]
            eng.wait_ge(ld[s], b + per * (g + 1))

        tiles_before = {"P3": 0, "P6": NT}

        def sums_complete(eng, ph, t):
            eng.wait_ge(summed, tiles_before[ph] + t + 1)

        def qk_stored(eng, s, g):
            if isinstance(g, int) and g <= 0:
                return
            eng.wait_ge(st_qk[s], 16 * g)

        def phase_end(eng, k):
            eng.drain().then_inc(phase, 1)
            eng.wait_ge(phase, 5 * k)

        def tile_rows(t):
            return bass.ds(t * P, P)

        loads = [
            (src_c[:, :], a["src_c"]),
            (rows[:, :, :].rearrange("p a b -> p (a b)"), a["rows"]),
            (cols[:, :], a["cols"]),
            (s_wneigh, a["W_neigh"]), (s_wkv, a["Wkv"]), (s_wq, a["Wq"]), (s_wout, a["WoutT"]),
            (s_w1, a["w1"]), (s_w2, a["w2"]), (s_wqT, a["wqT"]), (s_wkT, a["wkTb"]),
            (w_mix[:, :, :], a["W_self"]), (w_qkv[:, :, :], a["w_qkv"]), (w_out[:, :], a["w_out"]),
            (w_v[:, :, :], a["wv"]), (w_s[:, :, :], a["ws"]), (w_ff1[:, :, :], a["w_ff1"]),
            (w_ff2[:, :, :], a["w_ff2"]), (w_r[:, :, :], a["Wr"]), (w_bo[:, :], a["bo"]),
            (mem_v[:, 0:HID], a["mem_v"]),
            (view(reg_g, 0, CT * P).bitcast(I32), a["dst_ov"]), (firsts.bitcast(I32), a["first"]),
        ]
        NLOAD = 16 * len(loads)
        N_CONST = 13

        block = ctx.enter_context(nc.Block())

        @block.sync
        def _(sp):
            for dst_ap, src_ap in loads:
                if len(dst_ap.shape) == 3:
                    src_ap = src_ap.rearrange("p (a b) -> p a b", b=dst_ap.shape[2])
                sp.dma_start(dst_ap, src_ap).then_inc(loaded, 16)

            def hold(ph, n, value):
                need(sp, ph, n, value)
                sp.nop(nofuse=True)

            def pairs(load, store):
                for s in range(2):
                    load(s, s, 0, True)

                def body(g, last=False):
                    if not last:
                        for s in range(2):
                            load(2 * g + 2 + s, s, g + 1, False)
                    for s in range(2):
                        store(2 * g + s, s, g)
                body(0)
                with sp.Fori(1, NG - 1) as g:
                    body(g)
                body(NG - 1, True)

            tc = t_chunk.rearrange("(i p) c -> p i c", p=P)
            sp.wait_ge(lk, 1)
            sp.dma_start(tc[:, :, 0:P], c_dst).then_inc(lk_st, 16)
            sp.wait_ge(lk, 2)
            sp.dma_start(tc[:, :, P:2 * P], c_cum).then_inc(lk_st, 16)
            for i in range(2):
                sp.dma_start(t_ni[i, :].rearrange("(i p) -> p i", p=P), chunki[:, i, :],
                             allow_slow_non_contiguous=True).then_inc(lk_st, 16)
            sp.wait_ge(lk_st, 64)
            sp.dma_start(nrow[0:1, :, :], t_ni.rearrange("(a i) c -> a i c", a=1)).then_inc(lk_st, 16)

            def load(g, first=False):
                for s in range(2):
                    t = 2 * g + s
                    if not first:
                        hold("P1", "xn_ok", t - 1)
                    sp.dma_start(nbuf(s, 0, D), a["x"][tile_rows(t), :]).then_inc(ld[s], 16)

            def store_xn(g):
                for s in range(2):
                    t = 2 * g + s
                    hold("P1", "xn_ok", t + 1)
                    sp.dma_start(t_xn[tile_rows(t), :], nbuf(s, 256, D)).then_inc(sta[s], 16)

            def store_hs(g):
                for s in range(2):
                    t = 2 * g + s
                    hold("P1", "hs_ok", t + 1)
                    sp.dma_start(t_hs[tile_rows(t), :], nbuf(s, 1280, D)).then_inc(stb[s], 16)
                    sp.dma_start(t_sum[bass.ds(t * (ZPER * P), ZPER * P), :].rearrange(
                        "(p r) c -> p (r c)", r=ZPER), zeros).then_inc(zeroed, 16)

            load(0, True)
            store_xn(0)
            load(1)
            with sp.Fori(1, NG - 1) as g:
                store_xn(g)
                load(g + 1)
                store_hs(g - 1)
            store_xn(NG - 1)
            store_hs(NG - 2)
            store_hs(NG - 1)
            sp.wait_ge(consts, N_CONST)
            sp.dma_start(t_carry[C:C + 1, :], zrow[0:1, :]).then_inc(zeroed, 16)
            sp.dma_start(t_score[0:1, C * EC:CR * P], zrow[0:1, 0:CR * P - C * EC]).then_inc(zeroed, 16)
            sp.wait_ge(zeroed, (NT + 2) * 16)
            for s in range(2):
                stored(sp, "P1", "a", s, NG)
                stored(sp, "P1", "b", s, NG)
            phase_end(sp, 1)

            def first_rows(i, it, h):
                return nc.values_load_multi_w_load_instructions(
                    nrow[0:1, i, bass.ds(it * B + h * H, H)], [mybir.EngineType.SP], min_val=0,
                    max_val=2 * FULL, skip_runtime_bounds_check_because="worked out from the chunk's number")[1]

            def chunk_rows(first, table_, move):
                why = "every chunk's rows lie in the table"
                last = table_.shape[0]
                with sp.If(first >= FULL):
                    at = nc.s_assert_within(first - FULL, 0, last - P, skip_runtime_bounds_check_because=why)
                    move(table_[bass.ds(at, P), :], P)
                with sp.Else():
                    at = nc.s_assert_within(first, 0, last - FEW, skip_runtime_bounds_check_because=why)
                    move(table_[bass.ds(at, FEW), :], FEW)

            def store_sums(chunk0, z0):
                def body(it):
                    for h in range(2):
                        first = first_rows(1, it, h)
                        for k in range(H):
                            s = h * H + k
                            sp.wait_ge(carry_ok, chunk0 + it * B + s + 1)
                            sp.nop(nofuse=True)
                            chunk_rows(first[k], t_sum, lambda there, n: sp.dma_start(
                                there, ZR[0:n, s, :]).then_inc(z_sem[s], 16))
                plain_groups(sp, NB, body)
                for s in range(B):
                    sp.wait_ge(z_sem[s], z0 + 16 * NB)

            sp.wait_ge(lk_st, 80)
            store_sums(0, 0)
            phase_end(sp, 2)

            def load(t, s, g, first):
                if not first:
                    hold("P3", "var_ok", t - 1)
                sp.dma_start(nbuf(s, 0, D), a["x"][tile_rows(t), :]).then_inc(ld[s], 16)
                sp.dma_start(nbuf(s, 256, D), t_xn[tile_rows(t), :]).then_inc(ld[s], 16)

            def store(t, s, g):
                hold("P3", "xn_ok", t + 1)
                sp.dma_start(t_xn1[tile_rows(t), :], nbuf(s, 1536, D)).then_inc(sta[s], 16)
                hold("P3", "sum_ok", t + 1)
                sp.dma_start(t_xs[tile_rows(t), :], nbuf(s, 1792, D)).then_inc(stb[s], 16)
                hold("P3", "ev_a", t + 1)
                sp.dma_start(t_w[0, bass.ds(t * P, P)].rearrange("(p a) -> p a", a=1),
                             nbuf(s, 2304, 1)).then_inc(stc[s], 16)
            pairs(load, store)
            for s in range(2):
                for c in "abc":
                    stored(sp, "P3", c, s, NG)
            sp.dma_start(w_bcast, t_w[0:1, :].to_broadcast([P, NP])).then_inc(misc, 16)
            sp.wait_ge(misc, 16)
            phase_end(sp, 3)

            def load(t, s, g, first):
                if not first:
                    hold("P3b", "xT_ps", t - 1)
                sp.dma_start(nbuf(s, 0, D), t_xn1[tile_rows(t), :]).then_inc(ld[s], 16)

            def store(t, s, g):
                hold("P3b", "res_ok", t + 1)
                sp.dma_start(t_y[tile_rows(t), :], nbuf(s, 2048, D)).then_inc(sta[s], 16)
                sp.dma_start(t_qk[tile_rows(t), :], zrow[:, :]).then_inc(zeroed, 16)
            pairs(load, store)
            for s in range(2):
                stored(sp, "P3b", "a", s, NG)
            sp.wait_ge(zeroed, (2 * NT + 2) * 16)
            phase_end(sp, 4)

            def load(g, first=False):
                for s in range(2):
                    t = 2 * g + s
                    if not first:
                        hold("P4", "sum_ok", t - 1)
                    sp.dma_start(nbuf(s, 0, D), t_xs[tile_rows(t), :]).then_inc(ld[s], 16)
                    sp.dma_start(nbuf(s, 256, D), t_y[tile_rows(t), :]).then_inc(ld[s], 16)

            def store_tokens(g):
                for s in range(2):
                    t = 2 * g + s
                    hold("P4", "sum_ok", t + 1)
                    sp.dma_start(t_x2[tile_rows(t), :], nbuf(s, 512, D)).then_inc(sta[s], 16)
                    hold("P4", "xn_ok", t + 1)
                    sp.dma_start(t_xn2[tile_rows(t), :], nbuf(s, 768, D)).then_inc(stb[s], 16)

            def store_kv_q(g):
                for s in range(2):
                    t = 2 * g + s
                    hold("P4", "ev_b", t + 1)
                    sp.dma_start(t_kv[tile_rows(t), :], nbuf(s, 1792, 2 * HID)).then_inc(std[s], 16)
                    hold("P4", "res_ok", t + 1)
                    sp.dma_start(t_q[tile_rows(t), :], nbuf(s, 2560, HID)).then_inc(std[s], 16)

            load(0, True)
            load(1)
            store_tokens(0)
            with sp.Fori(1, NG - 1) as g:
                load(g + 1)
                store_tokens(g)
                store_kv_q(g - 1)
            store_tokens(NG - 1)
            store_kv_q(NG - 2)
            store_kv_q(NG - 1)
            for s in range(2):
                stored(sp, "P4", "a", s, NG)
                stored(sp, "P4", "b", s, NG)
                qk_stored(sp, s, NG)
                stored(sp, "P4", "d", s, NG, 2)
            phase_end(sp, 5)

            def load(t, s, g, first):
                if not first:
                    hold("P4b", "q_max", t - 1)
                sp.dma_start(nbuf(s, 0, 2 * HID), t_kv[tile_rows(t), :]).then_inc(ld[s], 16)
            pairs(load, lambda t, s, g: None)
            phase_end(sp, 6)

            sp.dma_start(s_a.bitcast(I32), a["dprev_r"]).then_inc(misc, 16)
            sp.dma_start(s_b.bitcast(I32), a["dst_r"]).then_inc(misc, 16)
            sp.dma_start(s_next.bitcast(I32), a["dnext_r"]).then_inc(misc, 16)
            sp.wait_ge(q_clear, 1)

            def body(it):
                for h in range(2):
                    first = first_rows(0, it, h)
                    for k in range(H):
                        s = h * H + k
                        if not isinstance(it, int):
                            sp.wait_ge(sum_ps, C + it * B + s - B + 1)
                            sp.nop(nofuse=True)
                        chunk_rows(first[k], t_qk, lambda there, n: sp.dma_start(
                            ZR[0:n, s, :], there).then_inc(z_sem[s], 16))
            plain_groups(sp, NB, body)
            for i in range(CT):
                n = min(P, C - i * P)
                sp.wait_ge(turned_sb, CT + i + 1)
                sp.dma_start(t_score[0, i * P * EC:(i * P + n) * EC].rearrange("(c q) -> c q", q=EC),
                             reg_g[0:n, i * P + 1:(i + 1) * P]).then_inc(misc, 16)
            sp.wait_ge(misc, 64 + 16 * CT)
            sp.dma_start(score, t_score[0, :].rearrange("(p c) -> p c", c=CR)).then_inc(misc, 16)
            sp.dma_start(s_c, a["ew_r"]).then_inc(misc, 16)
            sp.wait_ge(attention_ok, 1)
            sp.dma_start(t_att[0, :].rearrange("(p c) -> p c", c=CR), s_c).then_inc(misc, 16)
            sp.wait_ge(misc, 112 + 16 * CT)
            for i in range(CT):
                n = min(P, C - i * P)
                sp.dma_start(reg_g[0:n, i * P + 1:(i + 1) * P],
                             t_att[0, i * P * EC:(i * P + n) * EC].rearrange("(c q) -> c q", q=EC)).then_inc(misc, 16)
            phase_end(sp, 7)
            store_sums(C, 32 * NB)
            phase_end(sp, 8)

            sp.dma_start(view(reg_g, 0, 4096), a["W1"]).then_inc(misc, 16)
            sp.dma_start(view(reg_g, 4096, 4096), a["W2"]).then_inc(misc, 16)
            sp.dma_start(view(reg_s, 0, 4096), a["Wo"]).then_inc(misc, 16)

            def load(t, s, g, first):
                if not first:
                    hold("P6", "hs_ok", t - 1)
                sp.dma_start(nbuf(s, 0, D), t_x2[tile_rows(t), :]).then_inc(ld[s], 16)
                sp.dma_start(nbuf(s, 256, D), t_xn2[tile_rows(t), :]).then_inc(ld[s], 16)
                sp.dma_start(nbuf(s, 769, HID), t_q[tile_rows(t), :]).then_inc(ld[s], 16)

            def store(t, s, g):
                hold("P6", "res_ok", t + 1)
                sp.dma_start(t_x3[tile_rows(t), :], nbuf(s, 3584, D)).then_inc(sta[s], 16)
                hold("P6", "dots_ok", t + 1)
                sp.dma_start(t_xn3[tile_rows(t), :], nbuf(s, 3840, D)).then_inc(stb[s], 16)
            pairs(load, store)
            for s in range(2):
                stored(sp, "P6", "a", s, NG)
                stored(sp, "P6", "b", s, NG)
            phase_end(sp, 9)

            def load(t, s, g, first):
                if not first:
                    hold("P7", "ev_a", t - 1)
                sp.dma_start(nbuf(s, 0, D), t_x3[tile_rows(t), :]).then_inc(ld[s], 16)
                sp.dma_start(nbuf(s, 256, D), t_xn3[tile_rows(t), :]).then_inc(ld[s], 16)

            def store(t, s, g):
                sp.wait_ge(lo_ok, g * 2 * EX + 2 * EX - 1 + s)
                sp.nop(nofuse=True)
                if isinstance(t, int) and t >= NT - 2:
                    n = TAIL if t == NT - 2 else 0
                    if n:
                        sp.dma_start(out[t * P:t * P + n, :], nbuf(s, 1792, D)[0:n, :]).then_inc(sta[s], 16)
                else:
                    sp.dma_start(out[tile_rows(t), :], nbuf(s, 1792, D)).then_inc(sta[s], 16)
            pairs(load, store)
            stored(sp, "P7", "a", 0, NG)
            stored(sp, "P7", "a", 1, NG - 1)

        @block.gpsimd
        def _(po):
            ch = Chain(po, pool_step)
            nc.gpsimd.memset(ident[:, :], 0.0).then_inc(consts, 1)
            nc.gpsimd.memset(lower[:, :], 1.0).then_inc(consts, 1)
            nc.gpsimd.iota(iotai[:, 0:P], [[1, P]], base=0, channel_multiplier=0).then_inc(consts, 1)
            nc.gpsimd.iota(iotai[:, P:P + 1], [[1, 1]], base=0, channel_multiplier=1).then_inc(consts, 1)
            nc.gpsimd.iota(iotai[:, P + 1:P + 1 + NT], [[P, NT]], base=0, channel_multiplier=1).then_inc(consts, 1)
            nc.gpsimd.memset(padneg[:, :], 0.0).then_inc(consts, 1)
            po.wait_ge(consts, 6)
            nc.gpsimd.affine_select(out=ident[:, :], in_=ident[:, :], compare_op=ALU.not_equal, fill=1.0,
                                    base=0, pattern=[[-1, P]], channel_multiplier=1).then_inc(consts, 1)
            nc.gpsimd.affine_select(out=lower[:, :], in_=lower[:, :], compare_op=ALU.is_gt, fill=0.0,
                                    base=0, pattern=[[1, P]], channel_multiplier=-1).then_inc(consts, 1)
            nc.gpsimd.affine_select(out=padneg[:, :], in_=padneg[:, :], compare_op=ALU.is_ge, fill=NEG,
                                    base=N - 1, pattern=[[-P, NT]], channel_multiplier=-1).then_inc(consts, 1)
            nc.gpsimd.memset(half[:, :], -0.5).then_inc(consts, 1)
            nc.gpsimd.memset(ones[:, :], 1.0).then_inc(consts, 1)
            nc.gpsimd.memset(zrow[:, :], 0.0).then_inc(consts, 1)
            nc.gpsimd.memset(mem_v[:, HID:HID + 1], 1.0).then_inc(consts, 1)
            po.wait_ge(consts, N_CONST)

            def root(ph, var, rstd, t, s, src_off, dst_off):
                need(po, ph, var, t + 1)
                nc.gpsimd.tensor_tensor(nbuf(s, dst_off, 1), nbuf(s, src_off, 1), half[:, 0:1],
                                        ALU.pow).then_inc(sg[rstd], 1)

            po.wait_ge(moe_var, 2)
            for i in (4, 5):
                nc.gpsimd.tensor_tensor(moe[:, i, :], moe[:, i, :], half[:, 0:2 * EX],
                                        ALU.pow).then_inc(moe_root, 1)

            def first_roots(g):
                for s in range(2):
                    root("P1", "var_ok", "rstd_ok", 2 * g + s, s, 4108, 4110)

            def body(g, last_pair=False):
                if not last_pair:
                    first_roots(g + 1)
                for s in range(2):
                    need(po, "P1", "sq_red", 2 * g + s + 1)
                    nc.gpsimd.tensor_tensor(nbuf(s, 4160, 8), nbuf(s, 4144, 8), half[:, 0:8],
                                            ALU.pow).then_inc(sg["rstd_kv"], 1)
            first_roots(0)
            ahead_groups(po, NG, body)
            phase_end(po, 1)

            po.wait_ge(lk, 3)

            def body(g):
                for h in range(2):
                    n = 2 * g + h
                    wait(po, lk_ok, n - 1)
                    if not isinstance(g, int):
                        po.nop(nofuse=True)
                    nc.gpsimd.tensor_copy(lidx[:, h, :], cidx[:, bass.ds(n * LK, LK)]).then_inc(lk_g, 1)
                    po.wait_ge(lk_g, n + 1)
                    po.nop(nofuse=True)
                    for k in range(LK):
                        nc.gpsimd.indirect_dma_start(
                            out=found[:, h * LK + k, :], out_offset=None, in_=t_chunk[:, :],
                            in_offset=bass.IndirectOffsetOnAxis(ap=lidx[:, h, k:k + 1], axis=0)
                        ).then_inc(lk_in[h], 16)
            plain_groups(po, NT // (2 * LK), body)

            def gather_pass(table_, used_up, u0, i0):
                def body(it):
                    for h in range(2):
                        if not isinstance(it, int):
                            po.wait_ge(used_up, u0 + it * B + h * H - H)
                            po.nop(nofuse=True)
                        po.wait_ge(idx_ok, i0 + it * 2 + h + 1)
                        po.nop(nofuse=True)
                        for k in range(H):
                            s = h * H + k
                            nc.gpsimd.indirect_dma_start(
                                out=GR[:, s, 0:D], out_offset=None, in_=table_[:, :],
                                in_offset=bass.IndirectOffsetOnAxis(ap=sidx[:, h, k:k + 1], axis=0)
                            ).then_inc(g_sem[s], 16)
                plain_groups(po, NB, body)

            po.wait_ge(ones_ok, 1)
            gather_pass(t_hs, sum_ps, 0, 0)
            phase_end(po, 2)

            def by_node(t, s, n, rows_):
                nc.gpsimd.tensor_copy(tidx[:, s:s + 1], rows_[:, bass.ds(t, 1)]).then_inc(tidx_ok, 1)
                po.wait_ge(tidx_ok, n)
                po.nop(nofuse=True)
                return bass.IndirectOffsetOnAxis(ap=tidx[:, s:s + 1], axis=0)

            def fetch_sums(t, s, n):
                nc.gpsimd.tensor_copy(tidx[:, 2 + s:3 + s], carryrow[:, bass.ds(t, 1)]).then_inc(tidx_ok, 1)
                where = by_node(t, s, n, sumrow)
                nc.gpsimd.indirect_dma_start(out=nbuf(s, 512, D1), out_offset=None, in_=t_sum[:, :],
                                             in_offset=where).then_inc(ld_sum[s], 16)
                nc.gpsimd.indirect_dma_start(out=carried[:, s, :], out_offset=None, in_=t_carry[:, :],
                                             in_offset=bass.IndirectOffsetOnAxis(ap=tidx[:, 2 + s:3 + s], axis=0)
                                             ).then_inc(ld_sum[s], 16)

            def ahead(n0, ph, used_up, sums_off, first_part, second_part, third_part):
                def complete(g):
                    for s in range(2):
                        po.wait_ge(ld_sum[s], 32 * (tiles_before[ph] // 2 + g + 1))
                        if sums_off != 512:
                            need(po, ph, used_up, 2 * g + s - 1)
                        nc.gpsimd.tensor_tensor(nbuf(s, sums_off, D1), nbuf(s, 512, D1), carried[:, s, :],
                                                ALU.add).then_inc(summed, 1)

                def whole(g, last=False):
                    first_part(g)
                    if not last:
                        for s in range(2):
                            t = 2 * g + s
                            if sums_off == 512:
                                need(po, ph, used_up, t + 1)
                            po.wait_ge(summed, tiles_before[ph] + t + 1)
                            po.nop(nofuse=True)
                            fetch_sums(t + 2, s, n0 + 2 * t + 6)
                    second_part(g)
                    if not last:
                        complete(g + 1)
                    third_part(g)
                for s in range(2):
                    fetch_sums(s, s, n0 + 2 * s + 2)
                complete(0)
                whole(0)
                with po.Fori(1, NG - 1) as g:
                    whole(g)
                whole(NG - 1, True)

            def roots(g):
                for s in range(2):
                    root("P3", "var_ok", "rstd_ok", 2 * g + s, s, 4108, 4110)

            ahead(0, "P3", "var_ok", 2560, lambda g: None, roots, lambda g: None)
            phase_end(po, 3)
            phase_end(po, 4)

            def first_roots(g):
                for s in range(2):
                    root("P4", "var_ok", "rstd_ok", 2 * g + s, s, 4108, 4110)

            def second_roots(g):
                for s in range(2):
                    root("P4", "var2_ok", "rstd2_ok", 2 * g + s, s, 4112, 4114)

            def body(g, last_pair=False):
                if not last_pair:
                    first_roots(g + 1)
                for s in range(2):
                    t = 2 * g + s
                    qk_stored(po, s, g)
                    if not isinstance(g, int):
                        po.nop(nofuse=True)
                    where = by_node(t, s, 2 * NT + t + 1, qrow)
                    need(po, "P4", "ev_a", t + 1)
                    po.nop(nofuse=True)
                    nc.gpsimd.indirect_dma_start(out=t_qk[:, :], out_offset=where, in_=nbuf(s, 1280, D1),
                                                 in_offset=None, bounds_check=NP - 1,
                                                 oob_is_err=False).then_inc(st_qk[s], 16)
                if not last_pair:
                    second_roots(g + 1)
            first_roots(0)
            second_roots(0)
            ahead_groups(po, NG, body)
            phase_end(po, 5)
            phase_end(po, 6)

            po.wait_ge(q_clear, 1)
            gather_pass(t_xn2, scored, 0, 2 * NB)
            phase_end(po, 7)
            po.wait_ge(ones_ok, 2)
            gather_pass(t_xn2, sum_ps, 2 * C, 4 * NB)
            phase_end(po, 8)

            def first_roots(g):
                for s in range(2):
                    root("P6", "var_ok", "rstd_ok", 2 * g + s, s, 4108, 4110)
                for s in range(2):
                    root("P6", "sq_red", "rstd_kv", 2 * g + s, s, 4112, 4114)

            def second_roots(g):
                for s in range(2):
                    root("P6", "var2_ok", "rstd2_ok", 2 * g + s, s, FF_COLS + 8, FF_COLS + 10)

            def third_roots(g):
                for s in range(2):
                    need(po, "P6", "v_ok", 2 * g + s + 1)
                    nc.gpsimd.tensor_tensor(nbuf(s, FF_COLS + 10, 1), nbuf(s, FF_COLS + 8, 1), half[:, 0:1],
                                            ALU.pow).then_inc(sg["rstd3_ok"], 1)

            def last_pairs_roots(g):
                if not (isinstance(g, int) and g == 0):
                    third_roots(g - 1)
            ahead(3 * NT, "P6", "sq_red", 512, first_roots, last_pairs_roots, second_roots)
            third_roots(NG - 1)
            phase_end(po, 9)

        @block.tensor
        def _(pe):
            mm, tr = nc.tensor.matmul, nc.tensor.transpose

            def flip(ph, s, src_off, ps, ps_off=0, n=KD, name="xT_ps"):
                for k in range(n):
                    last = tr(ps[:, ps_off + k * P:ps_off + (k + 1) * P], nbuf(s, src_off + k * P, P), ident[:, :])
                if name:
                    last.then_inc(sg[name], 1)
                return last

            pe.wait_ge(consts, N_CONST)
            pe.wait_ge(loaded, NLOAD)
            pe.wait_ge(dve_one, 1)
            for c in range(KD):
                for k in range(KD):
                    last = mm(psA[c][:, 0:D1], s_wqT[:, k, c * P:(c + 1) * P], s_wkT[:, k, :],
                              start=(k == 0), stop=(k == KD - 1))
            for k in range(KD):
                last = mm(psB[0][:, 0:D1], col("bq", k).to_broadcast([P, P]), s_wkT[:, k, :],
                          start=(k == 0), stop=(k == KD - 1))
            last.then_inc(pe_one, 1)
            pe.wait_ge(dve_one, 2)
            pe.wait_ge(lk, 1)
            mm(psA[0][:, 0:2 * CT], lower[:, :], chunkn[:, 0, :], start=True, stop=True)
            mm(psA[0][:, 64:64 + 2 * CT], ones[:, :], chunkn[:, 0, :], start=True, stop=True).then_inc(lk_ps, 1)

            def turn(base, src):
                for i in range(CT):
                    if base + i >= 2:
                        pe.wait_ge(turned_sb, base + i - 1)
                    part = src(i)
                    n = part.shape[0]
                    tr(psT[i % 2][0:part.shape[1], 0:n], part, ident[0:n, 0:n]).then_inc(turned_ps, 1)
            turn(0, lambda i: c_slot[:, i, :])
            pe.wait_ge(turned_sb, CT)
            pe.wait_ge(lk, 2)

            def turn_tokens(g):
                for s in range(2):
                    need(pe, "P1", "xn_ok", 2 * g + s + 1)
                    flip("P1", s, 256, psT[s])

            def body(g, last_pair=False):
                for s in range(2):
                    t = 2 * g + s
                    need(pe, "P1", "xT_sb", t + 1)
                    need(pe, "P1", "ev_a", t - 1)
                    for k in range(KD):
                        last = mm(psA[s][:, 0:D], nbuf(s, 512 + k * P, P), s_wneigh[:, k, :],
                                  start=(k == 0), stop=(k == KD - 1))
                    last.then_inc(sg["mm_a"], 1)
                    need(pe, "P1", "ev_b", t)
                    for n in range(2):
                        for k in range(KD):
                            last = mm(psB[0][:, n * 512:(n + 1) * 512], nbuf(s, 512 + k * P, P),
                                      s_wkv[:, k, n * 512:(n + 1) * 512], start=(k == 0), stop=(k == KD - 1))
                    last.then_inc(sg["mm_b"], 1)
                if not last_pair:
                    turn_tokens(g + 1)
                for s in range(2):
                    t = 2 * g + s
                    need(pe, "P1", "v_ok", t + 1)
                    need(pe, "P1", "dots_ok", t)
                    for j in range(PAIRS):
                        last = mm(psB[1][:, j * P:(j + 1) * P], nbuf(s, 3584 + j * P, P),
                                  nbuf(s, 1536 + j * P, P), start=True, stop=True)
                    last.then_inc(sg["dots_ps"], 1)
            turn_tokens(0)
            ahead_groups(pe, NG, body)
            phase_end(pe, 1)

            def sum_pass(chunk0, g0, e0):
                def body(it):
                    for s in range(B):
                        pe.wait_ge(sel_ok, chunk0 + it * B + s + 1)
                        pe.wait_ge(g_sem[s], g0 + it * 16 + 16)
                        if not (isinstance(it, int) and s < 4):
                            pe.wait_ge(sum_sb, e0 + it * B + s - 3)
                        mm(psZ[s % 4][:, 0:D1], SEL[:, s, :], GR[:, s, :], start=True,
                           stop=True).then_inc(sum_ps, 1)
                plain_groups(pe, NB, body)

            pe.wait_ge(dve_one, 3)
            for j in range(PAIRS):
                last = mm(psB[j // 2][:, (j % 2) * 512:(j % 2) * 512 + D], dots[:, j, :], s_wout[:, j, :],
                          start=True, stop=True)
            last.then_inc(pe_one, 1)
            pe.wait_ge(act_one, 1)
            for c in range(KD):
                for j in range(PAIRS):
                    last = mm(psA[c][:, 0:D], s_wq[:, j, c * P:(c + 1) * P], fold[:, j, :],
                              start=(j == 0), stop=(j == PAIRS - 1))
            last.then_inc(pe_one, 1)
            pe.wait_ge(lk, 4)
            mm(psB[0][:, 0:NT], lower[:, :], look[:, 0, :], start=True, stop=True)
            mm(psB[0][:, 64:64 + NT], ones[:, :], look[:, 0, :], start=True, stop=True).then_inc(lk_ps, 1)
            pe.wait_ge(dve_one, 5)
            pe.wait_ge(lk, 5)
            sum_pass(0, 0, 0)
            phase_end(pe, 2)

            def body(g):
                for s in range(2):
                    landed(pe, "P3", s, g)
                    flip("P3", s, 256, psT[s])
                for s in range(2):
                    t = 2 * g + s
                    need(pe, "P3", "xT_sb", t + 1)
                    need(pe, "P3", "var_ok", t - 1)
                    for k in range(KD):
                        last = mm(psA[s][:, 0:D], nbuf(s, 769 + k * P, P), w_mix[:, k, :],
                                  start=(k == 0), stop=(k == KD - 1))
                    last.then_inc(sg["mm_a"], 1)
            plain_groups(pe, NG, body)
            phase_end(pe, 3)

            def body(g):
                for s in range(2):
                    landed(pe, "P3b", s, g)
                    flip("P3b", s, 0, psT[s])
                for s in range(2):
                    t = 2 * g + s
                    need(pe, "P3b", "xT_sb", t + 1)
                    for m in range(KF):
                        for k in range(KD):
                            last = mm(psB[s][:, m * P:(m + 1) * P], s_w1[:, k, m * P:(m + 1) * P],
                                      nbuf(s, 256 + k * P, P), start=(k == 0), stop=(k == KD - 1))
                    last.then_inc(sg["mm_b"], 1)
                for s in range(2):
                    t = 2 * g + s
                    need(pe, "P3b", "ev_b", t + 1)
                    need(pe, "P3b", "res_ok", t - 1)
                    for m in range(KF):
                        last = mm(psA[s][:, 0:D], nbuf(s, 512 + m * P, P), s_w2[:, m, :],
                                  start=(m == 0), stop=(m == KF - 1))
                    last.then_inc(sg["mm_a"], 1)
            plain_groups(pe, NG, body)
            phase_end(pe, 4)

            pe.wait_ge(dve_one, 6)
            tr(psT[0][0:1, 0:P], small[:, 0:1], ident[:, :]).then_inc(pe_one, 1)
            pe.wait_ge(dve_one, 7)
            tr(psT[0][:, P:P + 1], small[0:1, 1:2].to_broadcast([1, P]), ident[0:1, 0:1]).then_inc(pe_one, 1)
            pe.wait_ge(dve_one, 8)
            mm(psT[1][:, 0:NT], lower[:, :], pick[:, 0, :], start=True, stop=True)
            mm(psT[1][:, 64:64 + NT], ones[:, :], pick[:, 0, :], start=True, stop=True).then_inc(pe_one, 1)
            pe.wait_ge(dve_one, 9)

            def turn_tokens(g):
                for s in range(2):
                    need(pe, "P4", "xn_ok", 2 * g + s + 1)
                    flip("P4", s, 768, psT[s])

            def body(g, last_pair=False):
                for s in range(2):
                    t = 2 * g + s
                    need(pe, "P4", "xT_sb", t + 1)
                    need(pe, "P4", "ev_a", t - 1)
                    for k in range(KD):
                        last = mm(psA[s][:, 0:D1], nbuf(s, 1024 + k * P, P), w_qk[:, k, :],
                                  start=(k == 0), stop=(k == KD - 1))
                    last.then_inc(sg["mm_a"], 1)
                    need(pe, "P4", "q_max", t - 1)
                    for k in range(KD):
                        last = mm(psB[s][:, 0:3 * HID], nbuf(s, 1024 + k * P, P), w_qkv[:, k, :],
                                  start=(k == 0), stop=(k == KD - 1))
                    last.then_inc(sg["mm_b"], 1)
                if not last_pair:
                    turn_tokens(g + 1)
            turn_tokens(0)
            ahead_groups(pe, NG, body)
            phase_end(pe, 5)

            tr(psT[0][:, 0:P], kmax[:, :], ident[:, :]).then_inc(pe_one, 1)
            pe.wait_ge(dve_one, 11)
            tr(psT[0][:, P:2 * P], small[:, 2:3].to_broadcast([P, P]), ident[:, :]).then_inc(pe_one, 1)
            pe.wait_ge(act_one, 2)
            tr(psT[1][0:MEM, 0:P], small[:, 8:8 + MEM], ident[:, :]).then_inc(pe_one, 1)
            pe.wait_ge(dve_one, 13)
            mm(psT[1][:, P:P + HID + 1], nbuf(0, 1024, P)[0:MEM, :], mem_v[:, :],
               start=True, stop=True).then_inc(pe_one, 1)

            def body(g):
                for s in range(2):
                    t = 2 * g + s
                    need(pe, "P4b", "q_exp", t + 1)
                    need(pe, "P4b", "ev_a", t - 1)
                    mm(psA[s][:, 0:HID + 1], nbuf(s, 512, P), nbuf(s, 640, HID + 1),
                       start=True, stop=True).then_inc(sg["mm_a"], 1)
            plain_groups(pe, NG, body)
            pe.wait_ge(dve_one, 16)
            tr(psT[0][:, 0:P], ctxn[:, 0, :], ident[:, :]).then_inc(pe_one, 1)
            pe.wait_ge(act_one, 3)
            mm(psA[0][:, 0:D], ctxn[:, 1, :], w_out[:, :], start=True, stop=True).then_inc(pe_one, 1)
            phase_end(pe, 6)

            def body(it):
                for h in range(2):
                    pe.wait_ge(dcol_ok, it * 2 + h + 1)
                    for k in range(H):
                        if k % 4 == 0 and not (isinstance(it, int) and it == 0 and h == 0):
                            pe.wait_ge(sel_ok, C + it * B + h * H - H + k + 4)
                        tr(psT[k // 4][:, (k % 4) * P:(k % 4 + 1) * P],
                           dcol[:, h, k:k + 1].to_broadcast([P, P]), ident[:, :]).then_inc(row_ps, 1)
                    for k in range(H):
                        s = h * H + k
                        pe.wait_ge(sel_ok, C + it * B + s + 1)
                        pe.wait_ge(z_sem[s], 16 * NB + it * 16 + 16)
                        if not (isinstance(it, int) and s < 4):
                            pe.wait_ge(scored, it * B + s - 3)
                        mm(psZ[s % 4][:, 0:D1], SEL[:, s, :], ZR[:, s, :], start=True,
                           stop=True).then_inc(sum_ps, 1)
            plain_groups(pe, NB, body)
            pe.wait_ge(scores_ok, 1)
            turn(CT, lambda i: score_c[:, i * P:min((i + 1) * P, C)])
            for i in range(4):
                pe.wait_ge(scan_ok, 2 * i + 1)
                tr(psA[0][0:1, 0:P], small[:, 16:17], ident[:, :])
                tr(psA[0][0:1, P:2 * P], small[:, 17:18], ident[:, :]).then_inc(pe_one, 1)
                pe.wait_ge(scan_ok, 2 * i + 2)
                tr(psA[1][:, 0:1], srow[0:1, 3, :], ident[0:1, 0:1]).then_inc(pe_one, 1)
            pe.wait_ge(misc, 112 + 32 * CT)
            turn(2 * CT, lambda i: reg_g[0:min(P, C - i * P), i * P:(i + 1) * P])
            phase_end(pe, 7)
            sum_pass(2 * C, 32 * NB, C)
            phase_end(pe, 8)

            def body(g):
                for s in range(2):
                    landed(pe, "P6", s, g)
                    sums_complete(pe, "P6", 2 * g + s)
                    flip("P6", s, 256, psB[s], 0, name=None)
                    flip("P6", s, 512, psB[s], 2 * P, name=None)
                    flip("P6", s, 769, psB[s], 4 * P, n=1)
                for s in range(2):
                    t = 2 * g + s
                    need(pe, "P6", "xT_sb", t + 1)
                    need(pe, "P6", "ev_a", t - 1)
                    for k in range(KD):
                        mm(psA[s][:, 0:D], nbuf(s, 1024 + k * P, P), w_s[:, k, :], start=(k == 0), stop=False)
                    for k in range(KD):
                        mm(psA[s][:, 0:D], nbuf(s, 1280 + k * P, P), w_v[:, k, :],
                           start=False, stop=(k == KD - 1))
                    mm(psA[s][:, D:2 * D], nbuf(s, 1536, P), w_m2[:, :],
                       start=True, stop=True).then_inc(sg["mm_a"], 1)
                for s in range(2):
                    need(pe, "P6", "xn_ok", 2 * g + s + 1)
                    flip("P6", s, 1920, psT[s], name="tT_ps")
                for s in range(2):
                    need(pe, "P6", "tT_sb", 2 * g + s + 1)
                    for m in range(K1):
                        for k in range(KD):
                            last = mm(psB[s][:, m * P:(m + 1) * P], w_ff1[:, k, m * P:(m + 1) * P],
                                      nbuf(s, 2176 + k * P, P), start=(k == 0), stop=(k == KD - 1))
                    last.then_inc(sg["ff_ps"], 1)
                for s in range(2):
                    need(pe, "P6", "ff_sb", 2 * g + s + 1)
                    for m in range(K1):
                        last = mm(psT[s][:, D:2 * D], nbuf(s, 2432 + m * P, P), w_ff2[:, m, :],
                                  start=(m == 0), stop=(m == K1 - 1))
                    last.then_inc(sg["mm_b"], 1)
            plain_groups(pe, NG, body)
            phase_end(pe, 9)

            pe.wait_ge(misc, 112 + 32 * CT + 48)

            def turn_tokens(g):
                for s in range(2):
                    landed(pe, "P7", s, g)
                    flip("P7", s, 256, psT[s])

            def route(g):
                for s in range(2):
                    t = 2 * g + s
                    need(pe, "P7", "xT_sb", t + 1)
                    for k in range(KD):
                        last = mm(psT[s][:, D:D + EX], nbuf(s, 512 + k * P, P), w_r[:, k, :],
                                  start=(k == 0), stop=(k == KD - 1))
                    last.then_inc(sg["mm_a"], 1)

            def first_layer(g, e):
                for s in range(2):
                    n = g * 2 * EX + e * 2 + s
                    wait(pe, l1_sb, n - 1)
                    for m in range(KD):
                        for k in range(KD):
                            last = mm(psB[s][:, m * P:(m + 1) * P], g_w1[:, e, k, m * P:(m + 1) * P],
                                      nbuf(s, 512 + k * P, P), start=(k == 0), stop=(k == KD - 1))
                    last.then_inc(l1_ps, 1)

            def body(g, last_pair=False):
                first_layer(g, 0)
                for e in range(EX):
                    if e == 0:
                        for s in range(2):
                            need(pe, "P7", "sum_ok", 2 * g + s + 1)
                            tr(psT[s][0:EX, 384:512], nbuf(s, 4120, EX), ident[:, :]).then_inc(sg["tT_ps"], 1)
                    if e == EX - 1 and not last_pair:
                        turn_tokens(g + 1)
                    for s in range(2):
                        n = g * 2 * EX + e * 2 + s
                        wait(pe, l1_sb, n + 1)
                        for m in range(KD):
                            for k in range(KD):
                                last = mm(psB[s][:, 512 + m * P:512 + (m + 1) * P],
                                          g_w2[:, e, k, m * P:(m + 1) * P],
                                          nbuf(s, 768 + k * P, P), start=(k == 0), stop=(k == KD - 1))
                        last.then_inc(l2_ps, 1)
                    if e == 0:
                        for s in range(2):
                            need(pe, "P7", "tT_sb", 2 * g + s + 1)
                            wait(pe, lo_ok, g * 2 * EX - 1 + s)
                            mm(psA[s][:, 0:D], nbuf(s, 2304, P)[0:EX, :], w_bo[:, :],
                               start=True, stop=True).then_inc(sg["mm_b"], 1)
                    if e == EX - 1 and not last_pair:
                        route(g + 1)
                    if e < EX - 1:
                        first_layer(g, e + 1)
                    for s in range(2):
                        n = g * 2 * EX + e * 2 + s
                        wait(pe, l2_sb, n + 1)
                        if e == 0:
                            need(pe, "P7", "ev_a", 2 * g + s + 1)
                        else:
                            wait(pe, lo_ok, n - 1)
                        for k in range(KD):
                            last = mm(psA[s][:, 0:D], nbuf(s, 1024 + k * P, P), s_wo[:, e, k, :],
                                      start=(k == 0), stop=(k == KD - 1))
                        last.then_inc(lo_ps, 1)
            turn_tokens(0)
            route(0)
            ahead_groups(pe, NG, body)

        @block.scalar
        def _(act):
            cp, fn = nc.scalar.copy, nc.scalar.activation
            def turned(base, dst):
                for i in range(CT):
                    act.wait_ge(turned_ps, base + i + 1)
                    to = dst(i)
                    cp(to, psT[i % 2][0:to.shape[0], 0:to.shape[1]]).then_inc(turned_sb, 1)

            def chunk_cols(reg):
                return lambda i: reg[:, i * P:min((i + 1) * P, C)]
            turned(0, chunk_cols(slot_c))

            def tokens_out(g):
                for s in range(2):
                    t = 2 * g + s
                    need(act, "P1", "xT_ps", t + 1)
                    need(act, "P1", "mm_b", t - 1)
                    cp(nbuf(s, 512, D), psT[s][:, 0:D]).then_inc(sg["xT_sb"], 1)

            def body(g, last_pair=False):
                for s in range(2):
                    t = 2 * g + s
                    need(act, "P1", "mm_a", t + 1)
                    need(act, "P1", "hs_ok", t - 1)
                    cp(nbuf(s, 768, D), psA[s][:, 0:D]).then_inc(sg["ev_a"], 1)
                    need(act, "P1", "mm_b", t + 1)
                    need(act, "P1", "dots_ps", t - 1)
                    cp(nbuf(s, 1536, 1024), psB[0][:, :])
                    need(act, "P1", "sq_red", t - 1)
                    fn(nbuf(s, 2560, 1024), psB[0][:, :], ACT.Square).then_inc(sg["ev_b"], 1)
                if not last_pair:
                    tokens_out(g + 1)
                for s in range(2):
                    t = 2 * g + s
                    fn(sign_junk, firsts, ACT.Sign, bias=nid[:, 1, bass.ds(t, 1)], scale=-1.0,
                       accum_out=look[:, 1, bass.ds(t, 1)]).then_inc(act_step, 1)
                    act.wait_ge(act_step, t + 1)
            act.wait_ge(lk, 2)
            tokens_out(0)
            ahead_groups(act, NG, body)
            phase_end(act, 1)

            act.wait_ge(pe_one, 2)
            for j in range(PAIRS):
                last = nc.scalar.mul(fold[:, j, :], psB[j // 2][:, (j % 2) * 512:(j % 2) * 512 + D], 1.0 / N)
            last.then_inc(act_one, 1)

            def empty_pass(c0, k0, z0):
                def store_carries(it, h):
                    act.wait_ge(carry_ok, k0 + it * B + h * H + H)
                    act.nop(nofuse=True)
                    act.dma_start(t_carry[bass.ds(it * B + h * H, H), :].rearrange("(a s) c -> a s c", a=1),
                                  ZR[0:1, h * H:h * H + H, :]).then_inc(c_sem[h], 16)

                def body(it, first=False):
                    for s in range(B):
                        c = it * B + s
                        act.wait_ge(sum_ps, c0 + c + 1)
                        wait(act, z_sem[s], z0 + (0 if first else 16 * it))
                        if s % H == 0:
                            wait(act, c_sem[s // H], (c_base + 16 * it) if not first else 0)
                        if not first:
                            act.wait_ge(carry_ok, k0 + c - B + 2)
                        cp(ZR[:, s, :], psZ[s % 4][:, 0:D1]).then_inc(sum_sb, 1)
                        if s == H + CARRY_LAG:
                            store_carries(it, 0)
                        if s == CARRY_LAG and not first:
                            store_carries(it - 1, 1)
                c_base = 16 * NB * (k0 // C)
                body(0, True)
                with act.Fori(1, NB) as it:
                    body(it)
                store_carries(NB - 1, 1)
                for h in range(2):
                    act.wait_ge(c_sem[h], c_base + 16 * NB)
            act.wait_ge(consts, N_CONST)
            empty_pass(0, 0, 0)
            phase_end(act, 2)

            def body(g):
                for s in range(2):
                    t = 2 * g + s
                    need(act, "P3", "xT_ps", t + 1)
                    need(act, "P3", "mm_a", t - 1)
                    cp(nbuf(s, 769, D), psT[s][:, 0:D]).then_inc(sg["xT_sb"], 1)
            plain_groups(act, NG, body)
            phase_end(act, 3)

            def body(g):
                for s in range(2):
                    t = 2 * g + s
                    need(act, "P3b", "xT_ps", t + 1)
                    need(act, "P3b", "mm_b", t - 1)
                    cp(nbuf(s, 256, D), psT[s][:, 0:D]).then_inc(sg["xT_sb"], 1)
                for s in range(2):
                    t = 2 * g + s
                    need(act, "P3b", "mm_b", t + 1)
                    need(act, "P3b", "mm_a", t - 1)
                    for m in range(KF):
                        last = fn(nbuf(s, 512 + m * P, P), psB[s][:, m * P:(m + 1) * P], ACT.Gelu_apprx_tanh,
                                  bias=col("ffn_b1", m))
                    last.then_inc(sg["ev_b"], 1)
            plain_groups(act, NG, body)
            phase_end(act, 4)

            def tokens_out(g):
                for s in range(2):
                    t = 2 * g + s
                    need(act, "P4", "xT_ps", t + 1)
                    need(act, "P4", "mm_b", t - 1)
                    cp(nbuf(s, 1024, D), psT[s][:, 0:D]).then_inc(sg["xT_sb"], 1)

            def body(g, last_pair=False):
                for s in range(2):
                    need(act, "P4", "q_max", 2 * g + s + 1)
                    fn(nbuf(s, 2176, HID), nbuf(s, 2048, HID), ACT.Exp).then_inc(sg["q_exp"], 1)
                    if s == 0 and not last_pair:
                        tokens_out(g + 1)
            tokens_out(0)
            ahead_groups(act, NG, body)
            phase_end(act, 5)

            act.wait_ge(dve_one, 12)
            fn(small[:, 8:8 + MEM], col("mem_k", 0, MEM), ACT.Exp, bias=small[:, 3:4]).then_inc(act_one, 1)

            def body(g):
                for s in range(2):
                    t = 2 * g + s
                    need(act, "P4b", "q_max", t + 1)
                    fn(nbuf(s, 512, P), nbuf(s, 256, P), ACT.Exp).then_inc(sg["q_exp"], 1)
            plain_groups(act, NG, body)
            act.wait_ge(pe_one, 11)
            cp(ctxn[:, 1, :], psT[0][:, 0:P]).then_inc(act_one, 1)
            phase_end(act, 6)

            turned(CT, lambda i: reg_g[0:min(P, C - i * P), i * P:(i + 1) * P])
            act.wait_ge(shifted, 1)
            fn(s_c, s_c, ACT.Exp).then_inc(act_one, 1)
            turned(2 * CT, chunk_cols(wt))
            phase_end(act, 7)
            empty_pass(2 * C, C, 32 * NB)
            phase_end(act, 8)

            def body(g):
                for s in range(2):
                    t = 2 * g + s
                    need(act, "P6", "xT_ps", t + 1)
                    need(act, "P6", "mm_a", t - 1)
                    cp(nbuf(s, 1024, 5 * P), psB[s][:, 0:5 * P]).then_inc(sg["xT_sb"], 1)
                for s in range(2):
                    t = 2 * g + s
                    need(act, "P6", "tT_ps", t + 1)
                    need(act, "P6", "ff_ps", t - 1)
                    cp(nbuf(s, 2176, D), psT[s][:, 0:D]).then_inc(sg["tT_sb"], 1)
                for s in range(2):
                    t = 2 * g + s
                    need(act, "P6", "ff_ps", t + 1)
                    need(act, "P6", "mm_b", t - 1)
                    for m in range(K1):
                        last = fn(nbuf(s, 2432 + m * P, P), psB[s][:, m * P:(m + 1) * P], ACT.Gelu_apprx_tanh,
                                  bias=col("b_ff1", m))
                    last.then_inc(sg["ff_sb"], 1)
            plain_groups(act, NG, body)
            phase_end(act, 9)

            act.wait_ge(moe_ok, 1)

            def tokens_out(g):
                for s in range(2):
                    t = 2 * g + s
                    need(act, "P7", "xT_ps", t + 1)
                    wait(act, l1_ps, g * 2 * EX - 1 + s)
                    cp(nbuf(s, 512, D), psT[s][:, 0:D]).then_inc(sg["xT_sb"], 1)

            def exps(g):
                for s in range(2):
                    need(act, "P7", "q_max", 2 * g + s + 1)
                    fn(nbuf(s, 4128, EX), nbuf(s, 4150, EX), ACT.Exp,
                       accum_out=nbuf(s, 4140, 1)).then_inc(sg["q_exp"], 1)

            def body(g, last_pair=False):
                for e in range(EX):
                    for s in range(2):
                        n = g * 2 * EX + e * 2 + s
                        wait(act, l1_ps, n + 1)
                        wait(act, l2_ps, n - 1)
                        for m in range(KD):
                            i = e * KD + m
                            last = fn(nbuf(s, 768 + m * P, P), psB[s][:, m * P:(m + 1) * P], ACT.Relu,
                                      bias=moe[:, 1, i:i + 1], scale=moe[:, 0, i:i + 1])
                        last.then_inc(l1_sb, 1)
                    if e == 0:
                        for s in range(2):
                            need(act, "P7", "tT_ps", 2 * g + s + 1)
                            cp(nbuf(s, 2304, P)[0:EX, :], psT[s][0:EX, 384:512]).then_inc(sg["tT_sb"], 1)
                    if e == EX - 1 and not last_pair:
                        tokens_out(g + 1)
                    for s in range(2):
                        n = g * 2 * EX + e * 2 + s
                        wait(act, l2_ps, n + 1)
                        wait(act, lo_ps, n - 1)
                        for m in range(KD):
                            i = e * KD + m
                            last = fn(nbuf(s, 1024 + m * P, P), psB[s][:, 512 + m * P:512 + (m + 1) * P],
                                      ACT.Relu, bias=moe[:, 3, i:i + 1], scale=moe[:, 2, i:i + 1])
                        last.then_inc(l2_sb, 1)
                    if e == EX - 1 and not last_pair:
                        exps(g + 1)
            tokens_out(0)
            exps(0)
            ahead_groups(act, NG, body)

        @block.vector
        def _(v):
            ch = Chain(v, dve_step)
            link, near = ch.link, ch.near
            tt, ts, stt = nc.vector.tensor_tensor, nc.vector.tensor_scalar, nc.vector.scalar_tensor_tensor
            red = nc.vector.tensor_reduce
            one = [0]

            def signal(ins):
                one[0] += 1
                ins.then_inc(dve_one, 1)
                v.wait_ge(dve_one, one[0])

            def second(s):
                if s == 1:
                    ch.settle()

            def stats(src, ph, var="var_ok", at=4100):
                for s in range(2):
                    near(nc.vector.bn_stats(nbuf(s, at, 6), nbuf(s, src, D)), True)
                for s in range(2):
                    near(nc.vector.bn_aggr(nbuf(s, at + 6, 2), nbuf(s, at, 6)), s == 0)
                for s in range(2):
                    second(s)
                    ts(nbuf(s, at + 8, 1), nbuf(s, at + 7, 1), LN_EPS, None, ALU.add).then_inc(sg[var], 1)

            def normal(s, src, dst, name, at=4100):
                ins = ts(nbuf(s, dst, D), nbuf(s, src, D), nbuf(s, at + 6, 1), nbuf(s, at + 10, 1),
                         ALU.subtract, ALU.mult)
                if name:
                    ins.then_inc(sg[name], 1)
                return ins

            link(nc.vector.memset(wt[:, :], 1.0))
            link(nc.vector.memset(wt[0:1, :], 0.0))
            nc.vector.memset(dots[:, :, :], 0.0)
            link(nc.vector.memset(headmask[:, :], 0.0))
            for h in range(HEADS):
                link(nc.vector.memset(headmask[h * DH:(h + 1) * DH, h * DH:(h + 1) * DH], 1.0))
            v.wait_ge(loaded, NLOAD)
            kvw = s_wkv.rearrange("p a (h d) -> p (a h) d", d=L0_DH)
            link(red(small[:, 0:2 * KD * L0_HEADS], kvw, AX.X, ALU.add))
            link(ts(small[:, 0:2 * KD * L0_HEADS], small[:, 0:2 * KD * L0_HEADS], 1.0 / L0_DH, None, ALU.mult))
            signal(tt(kvw, kvw, small[:, 0:2 * KD * L0_HEADS].unsqueeze(2).to_broadcast(
                [P, 2 * KD * L0_HEADS, L0_DH]), ALU.subtract))
            for k in range(KD):
                link(ts(w_qkv[:, k, :], w_qkv[:, k, :], col("g_pre", k), None, ALU.mult))
            v.wait_ge(pe_one, 1)
            for c in range(KD):
                link(ts(w_qk[:, c, :], psA[c][:, 0:D1], D ** -0.5, None, ALU.mult))
            signal(ts(qk_bias[:, :], psB[0][:, 0:D1], D ** -0.5, None, ALU.mult))

            flat = lambda r: r.rearrange("p a b -> p (a b)")
            link(nc.vector.tensor_copy(flat(c_dst), flat(c_dst).bitcast(I32)))
            link(nc.vector.tensor_copy(firsts, firsts.bitcast(I32)))
            link(nc.vector.memset(c_slot[:, :, 0:1], 0.0))
            link(tt(c_slot[:, :, 1:P], c_dst[:, :, 1:P], c_dst[:, :, 0:P - 1], ALU.not_equal))
            link(nc.vector.tensor_tensor_scan(flat(c_cum), flat(c_slot), flat(c_slot), 0.0, ALU.add, ALU.max))
            link(tt(chunkn[:, 0, 0:CT], c_cum[:, :, P - 1], c_cum[:, :, 0], ALU.subtract))
            link(ts(chunkn[:, 0, CT:2 * CT], chunkn[:, 0, 0:CT], float(FEW), None, ALU.is_ge))
            tt(c_slot, c_cum[:, :, P - 1:P].to_broadcast([P, CT, P]), c_cum, ALU.subtract).then_inc(lk, 1)
            v.wait_ge(consts, N_CONST)
            link(nc.vector.memset(zeros, 0.0))
            link(nc.vector.tensor_copy(riota[:, :], iotai[:, 0:P]))
            link(nc.vector.tensor_copy(piota[:, :], iotai[:, P:P + 1]))
            link(nc.vector.tensor_copy(nid[:, 0, :], iotai[:, P + 1:P + 1 + NT]))
            link(ts(nid[:, 1, :], nid[:, 0, :], 0.5, None, ALU.add))
            v.wait_ge(lk_ps, 1)
            link(nc.vector.tensor_copy(chunkn[:, 1, :], psA[0][:, 64:64 + 2 * CT]))
            for q in (slice(0, CT), slice(CT, 2 * CT)):
                link(nc.vector.tensor_tensor_scan(chunkn[:, 2, q], chunkn[:, 1, q], chunkn[:, 1, q], 0.0,
                                                  ALU.add, ALU.max))
            link(tt(chunkn[:, 2, :], chunkn[:, 2, :], chunkn[:, 1, :], ALU.subtract))
            link(tt(chunkn[:, 2, :], psA[0][:, 0:2 * CT], chunkn[:, 2, :], ALU.add))
            link(tt(chunkn[:, 3, 0:CT], chunkn[:, 2, 0:CT], chunkn[:, 0, 0:CT], ALU.add))
            link(ts(chunkn[:, 3, 0:CT], chunkn[:, 3, 0:CT], -1.0, float(N + 1), ALU.mult, ALU.add))
            link(stt(chunki[:, 0, :], chunkn[:, 0, CT:2 * CT], float(FULL), chunkn[:, 3, 0:CT],
                     ALU.mult, ALU.add))
            link(ts(chunkn[:, 3, CT:2 * CT], nid[:, 0, 0:CT], float(FEW), None, ALU.mult))
            link(stt(chunkn[:, 4, 0:CT], chunkn[:, 2, CT:2 * CT], float(P - FEW), chunkn[:, 3, CT:2 * CT],
                     ALU.mult, ALU.add))
            link(stt(chunki[:, 1, :], chunkn[:, 0, CT:2 * CT], float(FULL), chunkn[:, 4, 0:CT],
                     ALU.mult, ALU.add))
            link(nc.vector.tensor_copy(c_cum, c_slot))
            nc.vector.tensor_copy(c_cum[:, :, 0], chunkn[:, 4, 0:CT]).then_inc(lk, 1)

            v.wait_ge(consts, N_CONST)
            for i, l in ((0, "1"), (1, "2")):
                ts(moe[:, 4 + i, :], col("v" + l, 0, 2 * EX), BN_EPS, None, ALU.add).then_inc(moe_var, 1)
            v.wait_ge(moe_root, 2)
            for i, l in ((0, "1"), (1, "2")):
                scale, bias = moe[:, 2 * i, :], moe[:, 2 * i + 1, :]
                link(tt(scale, col("g" + l, 0, 2 * EX), moe[:, 4 + i, :], ALU.mult))
                link(tt(bias, col("b" + l, 0, 2 * EX), col("m" + l, 0, 2 * EX), ALU.subtract))
                link(tt(bias, bias, scale, ALU.mult))
                last = tt(bias, bias, col("be" + l, 0, 2 * EX), ALU.add)
                if i == 0:
                    link(last)
            last.then_inc(moe_ok, 1)

            def front(g):
                for s in range(2):
                    landed(v, "P1", s, g)
                if not isinstance(g, int):
                    v.nop(nofuse=True)
                stats(0, "P1")

            def tokens(g):
                for s in range(2):
                    need(v, "P1", "rstd_ok", 2 * g + s + 1)
                    stored(v, "P1", "a", s, g)
                    normal(s, 0, 256, "xn_ok")

            def body(g, last_pair=False):
                if not last_pair:
                    front(g + 1)
                for s in range(2):
                    t = 2 * g + s
                    need(v, "P1", "ev_a", t + 1)
                    if not isinstance(g, int):
                        v.nop(nofuse=True)
                    h, wk, m8 = nbuf(s, 768, D), nbuf(s, 1024, D), nbuf(s, 4120, 8)
                    for r in range(TOPK_ROUNDS):
                        link(nc.vector.max(m8, h if r == 0 else wk), True)
                        link(nc.vector.match_replace(wk, m8, h if r == 0 else wk, NEG), r < TOPK_ROUNDS - 1)
                    stored(v, "P1", "b", s, g)
                    stt(nbuf(s, 1280, D), wk, NEG, h, ALU.is_equal, ALU.mult).then_inc(sg["hs_ok"], 1)
                    need(v, "P1", "ev_b", t + 1)
                    link(red(nbuf(s, 4128, 16), nbuf(s, 2560, 1024).rearrange("p (h d) -> p h d", d=L0_DH),
                             AX.X, ALU.add))
                    link(ts(nbuf(s, 4128, 16), nbuf(s, 4128, 16), 1.0 / L0_DH, LN_EPS, ALU.mult, ALU.add))
                    tt(nbuf(s, 4144, 8), nbuf(s, 4128, 8), nbuf(s, 4136, 8), ALU.mult).then_inc(sg["sq_red"], 1)
                    if s == 0 and not last_pair:
                        tokens(g + 1)
                for s in range(2):
                    t = 2 * g + s
                    need(v, "P1", "rstd_kv", t + 1)
                    need(v, "P1", "dots_ps", t - 1)
                    tt(nbuf(s, 3584, INNER).rearrange("p (h d) -> p h d", d=L0_DH),
                       nbuf(s, 1536 + INNER, INNER).rearrange("p (h d) -> p h d", d=L0_DH),
                       nbuf(s, 4160, 8).unsqueeze(2).to_broadcast([P, L0_HEADS, L0_DH]),
                       ALU.mult).then_inc(sg["v_ok"], 1)
                for s in range(2):
                    t = 2 * g + s
                    need(v, "P1", "dots_ps", t + 1)
                    need(v, "P1", "dots_ok", t)
                    dd = dots[:, :, :].rearrange("p a b -> p (a b)")
                    tt(dd, psB[1][:, 0:INNER], dd, ALU.add).then_inc(sg["dots_ok"], 1)
            front(0)
            tokens(0)
            ch.groups(NG - 1, body)
            body(NG - 1, True)
            need(v, "P1", "dots_ok", NT)
            phase_end(v, 1)

            link(nc.vector.memset(dots[0:64, :, 64:128], 0.0))
            signal(nc.vector.memset(dots[64:128, :, 0:64], 0.0))
            v.wait_ge(pe_one, 3)
            for c in range(KD):
                signal(tt(w_mix[:, c, :], psA[c][:, 0:D], w_mix[:, c, :], ALU.add))

            look3 = [look[:, i, :] for i in range(6)]
            link(ts(look3[1], look3[1], float(C), 0.5, ALU.add, ALU.mult))
            link(ts(look3[1], look3[1], -1.0, 0.0, ALU.add, ALU.max))
            nc.vector.tensor_copy(cidx[:, :], look3[1]).then_inc(lk, 1)

            def body(g):
                for h in range(2):
                    n = 2 * g + h
                    v.wait_ge(lk_in[h], 16 * LK * (g + 1))
                    fd = found[:, h * LK:(h + 1) * LK, :]
                    tiles = bass.ds(n * LK, LK)
                    link(tt(match, fd[:, :, 1:P], nid[:, 0, tiles].unsqueeze(2).to_broadcast([P, LK, EC]),
                            ALU.is_equal))
                    link(red(look[:, 0, tiles], match, AX.X, ALU.max))
                    link(nc.vector.tensor_copy(look[:, 3, tiles], fd[:, :, P]))
                    link(tt(look[:, 5, tiles], fd[:, :, 0], nid[:, 0, tiles], ALU.is_equal))
                    link(tt(match, match, fd[:, :, P + 1:2 * P], ALU.mult))
                    red(look[:, 2, tiles], match, AX.X, ALU.max).then_inc(lk_ok, 1)
                    v.wait_ge(lk_ok, n + 1)
            ch.groups(NT // (2 * LK), body)
            v.sem_inc(lk, 1)
            link(stt(look3[5], look3[2], 0.0, look3[5], ALU.is_gt, ALU.mult))
            link(tt(look3[5], look3[5], look3[0], ALU.mult))
            link(ts(look3[1], look3[1], -float(C + 1), None, ALU.add))
            link(tt(look3[5], look3[5], look3[1], ALU.mult))
            link(ts(carryrow[:, :], look3[5], float(C), None, ALU.add))
            link(tt(look3[2], look3[3], look3[2], ALU.add))
            link(ts(look3[2], look3[2], -float(ZROW), None, ALU.add))
            link(tt(look3[2], look3[2], look3[0], ALU.mult))
            link(ts(sumrow[:, :], look3[2], float(ZROW), None, ALU.add))
            v.wait_ge(lk_ps, 2)
            link(nc.vector.tensor_copy(look3[3], psB[0][:, 64:64 + NT]))
            link(nc.vector.tensor_tensor_scan(look3[4], look3[3], look3[3], 0.0, ALU.add, ALU.max))
            link(tt(look3[4], look3[4], look3[3], ALU.subtract))
            link(tt(look3[4], psB[0][:, 0:NT], look3[4], ALU.add))
            link(ts(look3[4], look3[4], -1.0, float(N) + FAR, ALU.mult, ALU.add))
            link(stt(qrow[:, :], look3[0], -FAR, look3[4], ALU.mult, ALU.add))
            v.sem_inc(lk, 1)

            def indices(it, h):
                nc.vector.tensor_copy(sidx[:, h, :], src_c[:, bass.ds(it * B + h * H, H)]).then_inc(idx_ok, 1)

            def next_indices(it, s, last_block):
                if s == H // 2 and not (isinstance(it, int) and it == 0):
                    indices(it, 1)
                if s == H + H // 2 and not last_block:
                    indices(it + 1, 0)

            def sum_pass(c0, k0):
                def carry(c, s):
                    v.wait_ge(sum_sb, k0 + c + 1)
                    before = zrow[0:1, :] if isinstance(c, int) and c == 0 else ZR[0:1, (s - 1) % B, :]
                    if not isinstance(c, int) or k0 + c > 0:
                        v.wait_ge(carry_ok, k0 + c)
                    stt(ZR[0:1, s, :], before, slot_c[0:1, bass.ds(c, 1)], ZR[0:1, s, :],
                        ALU.mult, ALU.add).then_inc(carry_ok, 1)

                def body(it, last_block=False):
                    for s in range(B):
                        c = it * B + s
                        wait(v, sum_ps, c0 + c - B + 1)
                        ts(SEL[:, s, :], riota[:, :], slot_c[:, bass.ds(c, 1)], wt[:, bass.ds(c, 1)],
                           ALU.is_equal, ALU.mult).then_inc(sel_ok, 1)
                        if s >= LAG:
                            carry(c - LAG, s - LAG)
                        elif not (isinstance(it, int) and it == 0):
                            carry(c - LAG, s - LAG + B)
                        next_indices(it, s, last_block)
                indices(0, 0)
                indices(0, 1)
                body(0)
                body(1)
                with v.Fori(2, NB - 1) as it:
                    body(it)
                body(NB - 1, True)
                for k in range(LAG):
                    carry(C - LAG + k, B - LAG + k)
            link(ts(slot_c[0:1, :], slot_c[0:1, :], 0.0, None, ALU.is_equal))
            nc.vector.memset(GR[:, :, D:D1], 1.0).then_inc(ones_ok, 1)
            sum_pass(0, 0)
            phase_end(v, 2)

            def body(g):
                ag, c = ([nbuf(s, off, n) for s in range(2)] for off, n in ((2560, D), (4120, 1)))
                for s in range(2):
                    landed(v, "P3", s, g)
                    sums_complete(v, "P3", 2 * g + s)
                    near(ts(c[s], nbuf(s, 2560 + D, 1), 1.0, None, ALU.max))
                for s in range(2):
                    near(nc.vector.reciprocal(c[s], c[s]))
                for s in range(2):
                    near(stt(ag[s], ag[s], c[s], nbuf(s, 0, D), ALU.mult, ALU.add))
                for s in range(2):
                    near(tt(ag[s], ag[s], row("bout"), ALU.add))
                for s in range(2):
                    t = 2 * g + s
                    need(v, "P3", "mm_a", t + 1)
                    need(v, "P3", "sum_ok", t - 1)
                    near(tt(nbuf(s, 1280, D), psA[s][:, 0:D], ag[s], ALU.add), True)
                stats(1280, "P3")
                for s in range(2):
                    need(v, "P3", "rstd_ok", 2 * g + s + 1)
                    stored(v, "P3", "a", s, g)
                    normal(s, 1280, 1536, "xn_ok")
                for s in range(2):
                    need(v, "P3", "xn_ok", 2 * g + s + 1)
                    stored(v, "P3", "b", s, g)
                    tt(nbuf(s, 1792, D), nbuf(s, 1280, D), nbuf(s, 1536, D), ALU.add).then_inc(sg["sum_ok"], 1)
                for s in range(2):
                    near(stt(nbuf(s, 2048, D), nbuf(s, 1536, D), 1.0, row("wr"), ALU.mult, ALU.mult,
                             accum_out=nbuf(s, 4121, 1)))
                for s in range(2):
                    near(ts(nbuf(s, 4122, 1), nbuf(s, 4121, 1), col("ffn_br"), None, ALU.add))
                for s in range(2):
                    near(nc.vector.tensor_copy(w_all[:, bass.ds(2 * g + s, 1)], nbuf(s, 4122, 1)))
                for s in range(2):
                    stored(v, "P3", "c", s, g)
                    ts(nbuf(s, 2304, 1), nbuf(s, 4122, 1), padneg[:, bass.ds(2 * g + s, 1)], None,
                       ALU.add).then_inc(sg["ev_a"], 1)
                for s in range(2):
                    need(v, "P3", "ev_a", 2 * g + s + 1)
                    link(nc.vector.tensor_copy(w_rank[:, bass.ds(2 * g + s, 1)], nbuf(s, 2304, 1)))
            ch.groups(NG, body)
            phase_end(v, 3)

            def body(g):
                for s in range(2):
                    t = 2 * g + s
                    link(ts(junk, w_bcast, w_rank[:, bass.ds(t, 1)], None, ALU.is_gt, ALU.add,
                            accum_out=above[:, bass.ds(t, 1)]))
                    need(v, "P3b", "mm_a", t + 1)
                    stored(v, "P3b", "a", s, g)
                    link(tt(nbuf(s, 2048, D), psA[s][:, 0:D], row("ffn_b2"), ALU.add))
                    ts(nbuf(s, 2048, D), nbuf(s, 2048, D), w_all[:, bass.ds(t, 1)], None,
                       ALU.mult).then_inc(sg["res_ok"], 1)
            ch.groups(NG, body)
            phase_end(v, 4)

            link(ts(pick[:, 1, :], above[:, :], float(KEEP), NEG, ALU.is_ge, ALU.mult))
            link(stt(pick[:, 1, :], w_rank[:, :], -1.0, pick[:, 1, :], ALU.mult, ALU.add))
            assert one[0] == 5
            signal(red(small[:, 0:1], pick[:, 1, :], AX.X, ALU.max))
            v.wait_ge(pe_one, 4)
            signal(red(small[0:1, 1:2], psT[0][0:1, 0:P], AX.X, ALU.max))
            v.wait_ge(pe_one, 5)
            link(ts(small[:, 4:5], psT[0][:, P:P + 1], -1.0, None, ALU.mult))
            signal(ts(pick[:, 0, :], w_rank[:, :], small[:, 4:5], None, ALU.is_equal))
            v.wait_ge(pe_one, 6)
            link(nc.vector.tensor_copy(pick[:, 3, :], psT[1][:, 64:64 + NT]))
            link(nc.vector.memset(pick[:, 2, :], 0.0))
            link(nc.vector.tensor_tensor_scan(pick[:, 1, :], pick[:, 3, :], pick[:, 2, :], 0.0, ALU.add, ALU.add))
            link(tt(pick[:, 1, :], pick[:, 1, :], pick[:, 3, :], ALU.subtract))
            link(tt(pick[:, 1, :], psT[1][:, 0:NT], pick[:, 1, :], ALU.add))
            link(tt(pick[:, 1, :], pick[:, 1, :], pick[:, 0, :], ALU.mult))
            link(tt(pick[:, 1, :], pick[:, 1, :], above[:, :], ALU.add))
            signal(ts(sel[:, :], pick[:, 1, :], float(KEEP), None, ALU.is_lt))
            signal(nc.vector.memset(kmax[:, :], NEG))

            def front(g):
                for s in range(2):
                    t = 2 * g + s
                    landed(v, "P4", s, g)
                    stored(v, "P4", "a", s, g)
                    stt(nbuf(s, 512, D), nbuf(s, 256, D), sel[:, bass.ds(t, 1)], nbuf(s, 0, D),
                        ALU.mult, ALU.add).then_inc(sg["sum_ok"], 1)
                need(v, "P4", "sum_ok", 2 * g + 2)
                if not isinstance(g, int):
                    v.nop(nofuse=True)
                stats(512, "P4")

            def tokens(g):
                for s in range(2):
                    need(v, "P4", "rstd_ok", 2 * g + s + 1)
                    stored(v, "P4", "b", s, g)
                    normal(s, 512, 768, "xn_ok")

            def squares(g):
                for s in range(2):
                    need(v, "P4", "xn_ok", 2 * g + s + 1)
                    near(stt(nbuf(s, 2816, D), nbuf(s, 768, D), 1.0, nbuf(s, 768, D), ALU.mult, ALU.mult,
                             accum_out=nbuf(s, 4111, 1)))
                for s in range(2):
                    second(s)
                    ts(nbuf(s, 4112, 1), nbuf(s, 4111, 1), 1e-24, None, ALU.max).then_inc(sg["var2_ok"], 1)

            def body(g, last_pair=False):
                if not last_pair:
                    front(g + 1)
                for s in range(2):
                    t = 2 * g + s
                    need(v, "P4", "mm_a", t + 1)
                    qk_stored(v, s, g)
                    tt(nbuf(s, 1280, D1), psA[s][:, 0:D1], qk_bias[:, :], ALU.add).then_inc(sg["ev_a"], 1)
                    need(v, "P4", "rstd2_ok", t + 1)
                    link(ts(nbuf(s, 4115, 1), nbuf(s, 4114, 1), float(D) ** 0.5, None, ALU.mult))
                    need(v, "P4", "mm_b", t + 1)
                    stored(v, "P4", "d", s, g, 2)
                    qkv = psB[s]
                    ts(nbuf(s, 1792 + HID, HID), qkv[:, 2 * HID:3 * HID], nbuf(s, 4115, 1), None, ALU.mult)
                    ts(nbuf(s, 1792, HID), qkv[:, HID:2 * HID], nbuf(s, 4115, 1), padneg[:, bass.ds(t, 1)],
                       ALU.mult, ALU.add).then_inc(sg["ev_b"], 1)
                    need(v, "P4", "ev_b", t + 1)
                    need(v, "P4", "hs_ok", t)
                    tt(kmax[:, :], kmax[:, :], nbuf(s, 1792, HID), ALU.max).then_inc(sg["hs_ok"], 1)
                    q3 = nbuf(s, 2048, HID).rearrange("p (h d) -> p h d", d=DH)
                    link(ts(nbuf(s, 2048, HID), qkv[:, 0:HID], nbuf(s, 4115, 1), None, ALU.mult))
                    link(red(nbuf(s, 4120, HEADS), q3, AX.X, ALU.max))
                    tt(q3, q3, nbuf(s, 4120, HEADS).unsqueeze(2).to_broadcast([P, HEADS, DH]),
                       ALU.subtract).then_inc(sg["q_max"], 1)
                    if s == 0 and not last_pair:
                        tokens(g + 1)
                if not last_pair:
                    squares(g + 1)
                e3 = [nbuf(s, 2176, HID).rearrange("p (h d) -> p h d", d=DH) for s in range(2)]
                for s in range(2):
                    need(v, "P4", "q_exp", 2 * g + s + 1)
                    near(red(nbuf(s, 4124, HEADS), e3[s], AX.X, ALU.add))
                for s in range(2):
                    near(nc.vector.reciprocal(nbuf(s, 4124, HEADS), nbuf(s, 4124, HEADS)))
                for s in range(2):
                    near(ts(nbuf(s, 4124, HEADS), nbuf(s, 4124, HEADS), DH ** -0.5, None, ALU.mult))
                for s in range(2):
                    second(s)
                    tt(nbuf(s, 2560, HID).rearrange("p (h d) -> p h d", d=DH), e3[s],
                       nbuf(s, 4124, HEADS).unsqueeze(2).to_broadcast([P, HEADS, DH]),
                       ALU.mult).then_inc(sg["res_ok"], 1)
            front(0)
            tokens(0)
            squares(0)
            ch.groups(NG - 1, body)
            body(NG - 1, True)
            need(v, "P4", "hs_ok", NT)
            phase_end(v, 5)

            v.wait_ge(pe_one, 7)
            link(red(small[:, 2:3], psT[0][:, 0:P], AX.X, ALU.max))
            link(red(small[:, 5:6], col("mem_k", 0, MEM), AX.X, ALU.max))
            signal(tt(small[:, 2:3], small[:, 2:3], small[:, 5:6], ALU.max))
            signal(ts(small[:, 3:4], small[:, 2:3], -1.0, None, ALU.mult))
            v.wait_ge(pe_one, 8)
            link(nc.vector.tensor_copy(kneg[:, :], psT[0][:, P:2 * P]))
            v.wait_ge(pe_one, 9)
            signal(nc.vector.tensor_copy(nbuf(0, 1024, P)[0:MEM, :], psT[1][0:MEM, 0:P]))
            v.wait_ge(pe_one, 10)
            link(nc.vector.tensor_copy(ctxv[:, :], psT[1][:, P:P + HID + 1]))
            for s in range(2):
                link(nc.vector.memset(nbuf(s, 640 + HID, 1), 1.0))

            def body(g):
                for s in range(2):
                    t = 2 * g + s
                    landed(v, "P4b", s, g)
                    need(v, "P4b", "mm_a", t - 1)
                    nc.vector.tensor_copy(nbuf(s, 640, HID), nbuf(s, HID, HID))
                    need(v, "P4b", "q_exp", t - 1)
                    tt(nbuf(s, 256, P), nbuf(s, 0, P), kneg[:, :], ALU.subtract).then_inc(sg["q_max"], 1)
                for s in range(2):
                    t = 2 * g + s
                    need(v, "P4b", "mm_a", t + 1)
                    need(v, "P4b", "ev_a", t)
                    tt(ctxv[:, :], psA[s][:, 0:HID + 1], ctxv[:, :], ALU.add).then_inc(sg["ev_a"], 1)
            ch.groups(NG, body)
            need(v, "P4b", "ev_a", NT)
            signal(nc.vector.reciprocal(small[:, 6:7], ctxv[:, HID:HID + 1]))
            signal(ts(ctxn[:, 0, :], ctxv[:, 0:HID], small[:, 6:7], None, ALU.mult))
            signal(tt(ctxn[:, 0, :], ctxn[:, 0, :], headmask[:, :], ALU.mult))
            v.wait_ge(pe_one, 12)
            link(nc.vector.tensor_copy(w_m2[:, :], psA[0][:, 0:D]))
            phase_end(v, 6)

            link(nc.vector.memset(reg_g[:, 0:2 * B * D1], 0.0))
            nc.vector.memset(GR[:, :, D:D1], 1.0).then_inc(q_clear, 1)
            v.wait_ge(q_clear, 1)

            def scored_chunk(c, s, rnd):
                v.wait_ge(sum_ps, C + c + 1)
                v.wait_ge(g_sem[s], 16 * NB + 16 * (rnd + 1))
                wait(v, scored, c)
                stt(nbuf(0, 0, D1), psZ[s % 4][:, 0:D1], 1.0, GR[:, s, :], ALU.mult, ALU.mult,
                    accum_out=scol[:, s:s + 1]).then_inc(scored, 1)
                if s % H == H - 1:
                    v.wait_ge(scored, c + 1)
                    link(nc.vector.tensor_copy(score_c[:, bass.ds(c - (H - 1), H)], scol[:, s - (H - 1):s + 1]))

            def body(it, last_block=False):
                for s in range(B):
                    c = it * B + s
                    if s % H == 0:
                        h = s // H
                        nc.vector.tensor_copy(dcol[:, h, :], slot_c[:, bass.ds(c, H)]).then_inc(dcol_ok, 1)
                    if s % 4 == 0:
                        v.wait_ge(row_ps, c + 4)
                    wait(v, sum_ps, C + c - B + 1)
                    k = s % H
                    ts(SEL[:, s, :], psT[k // 4][:, (k % 4) * P:(k % 4 + 1) * P], piota[:, :], None,
                       ALU.is_equal).then_inc(sel_ok, 1)
                    if s >= LAG:
                        scored_chunk(c - LAG, s - LAG, it)
                    elif not (isinstance(it, int) and it == 0):
                        scored_chunk(c - LAG, s - LAG + B, it - 1)
                    next_indices(it, s, last_block)
            indices(0, 0)
            indices(0, 1)
            ch.groups(NB - 1, body, peel=2)
            body(NB - 1, True)
            for k in range(LAG):
                scored_chunk(C - LAG + k, B - LAG + k, NB - 1)
            v.sem_inc(scores_ok, 1)
            v.wait_ge(misc, 96 + 16 * CT)
            link(nc.vector.memset(reg_g[:, 0:CT * P].rearrange("p (i q) -> p i q", q=P)[:, :, 0:1], 0.0))
            link(tt(s_prev, s_b.bitcast(I32), s_a.bitcast(I32), ALU.is_equal))
            link(tt(s_next, s_b.bitcast(I32), s_next.bitcast(I32), ALU.is_equal))
            link(stt(s_a, s_c, col("we"), score, ALU.mult, ALU.add))
            link(ts(score, s_a, col("be"), None, ALU.add))

            def scan(dst, keep, x, op0, op1, neutral, back, i):
                def d(ap):
                    return ap[:, ::-1] if back else ap
                link(nc.vector.tensor_tensor_scan(d(dst), d(keep), d(x), neutral, op0, op1))
                link(nc.vector.tensor_copy(small[:, 16:17], dst[:, 0:1] if back else dst[:, CR - 1:CR]))
                red(small[:, 17:18], keep, AX.X, ALU.min).then_inc(scan_ok, 1)
                v.wait_ge(pe_one, 13 + 2 * i)
                link(nc.vector.tensor_copy(srow[0:1, 0, :], psA[0][0:1, 0:P]))
                link(nc.vector.tensor_copy(srow[0:1, 1, :], psA[0][0:1, P:2 * P]))
                r = (lambda k: srow[0:1, k, ::-1]) if back else (lambda k: srow[0:1, k, :])
                link(nc.vector.tensor_tensor_scan(r(2), r(1), r(0), neutral, op0, op1))
                link(nc.vector.memset(srow[0:1, 3, :], neutral))
                into, of = (slice(0, P - 1), slice(1, P)) if back else (slice(1, P), slice(0, P - 1))
                nc.vector.tensor_copy(srow[0:1, 3, into], srow[0:1, 2, of]).then_inc(scan_ok, 1)
                v.wait_ge(pe_one, 14 + 2 * i)
                link(nc.vector.tensor_copy(small[:, 18:19], psA[1][:, 0:1]))
                link(nc.vector.tensor_tensor_scan(d(dst), d(keep), d(x), small[:, 18:19], op0, op1))

            link(ts(s_a, s_prev, 1.0, BIG, ALU.subtract, ALU.mult))
            scan(s_b, s_a, score, ALU.add, ALU.max, -BIG, False, 0)
            link(ts(s_a, s_next, 1.0, BIG, ALU.subtract, ALU.mult))
            scan(s_c, s_a, s_b, ALU.add, ALU.max, -BIG, True, 1)
            tt(s_c, score, s_c, ALU.subtract).then_inc(shifted, 1)
            v.wait_ge(act_one, 4)
            scan(s_b, s_prev, s_c, ALU.mult, ALU.add, 0.0, False, 2)
            link(ts(s_a, s_next, -1.0, 1.0, ALU.mult, ALU.add))
            link(tt(s_b, s_b, s_a, ALU.mult))
            scan(s_a, s_next, s_b, ALU.mult, ALU.add, 0.0, True, 3)
            link(ts(s_a, s_a, 1e-12, None, ALU.max))
            link(nc.vector.reciprocal(s_a, s_a))
            tt(s_c, s_c, s_a, ALU.mult).then_inc(attention_ok, 1)
            phase_end(v, 7)
            nc.vector.memset(GR[:, :, D:D1], 1.0).then_inc(ones_ok, 1)
            sum_pass(2 * C, C)
            phase_end(v, 8)

            r, m, xn2, z, u, x3 = ([nbuf(s, off, D) for s in range(2)]
                                   for off in (2944, 1664, 256, 1920, 3200, 3584))

            def attention(g):
                for s in range(2):
                    t = 2 * g + s
                    landed(v, "P6", s, g)
                    sums_complete(v, "P6", t)
                    need(v, "P6", "mm_a", t + 1)
                    near(tt(r[s], psA[s][:, 0:D], row("bs"), ALU.add))
                    tt(m[s], psA[s][:, D:2 * D], row("b_out"), ALU.add).then_inc(sg["ev_a"], 1)
                for s in range(2):
                    near(stt(r[s], row("bv"), nbuf(s, 512 + D, 1), r[s], ALU.mult, ALU.add))
                for s in range(2):
                    near(tt(r[s], r[s], xn2[s], ALU.add))
                for s in range(2):
                    need(v, "P6", "ev_a", 2 * g + s + 1)
                    near(stt(square_junk[:, s, :], m[s], 1.0, m[s], ALU.mult, ALU.mult,
                             accum_out=nbuf(s, 4111, 1)), s == 1)
                for s in range(2):
                    second(s)
                    ts(nbuf(s, 4112, 1), nbuf(s, 4111, 1), 1e-24, None, ALU.max).then_inc(sg["sq_red"], 1)
                stats(2944, "P6")
                for s in range(2):
                    need(v, "P6", "rstd_ok", 2 * g + s + 1)
                    near(normal(s, 2944, 1920, None))
                for s in range(2):
                    near(tt(z[s], z[s], row("g1"), ALU.mult))
                for s in range(2):
                    second(s)
                    tt(z[s], z[s], row("b1"), ALU.add).then_inc(sg["xn_ok"], 1)
                for s in range(2):
                    need(v, "P6", "rstd_kv", 2 * g + s + 1)
                    near(ts(nbuf(s, 4115, 1), nbuf(s, 4114, 1), float(D) ** 0.5, None, ALU.mult))
                for s in range(2):
                    near(stt(m[s], m[s], nbuf(s, 4115, 1), row("g_out"), ALU.mult, ALU.mult))
                for s in range(2):
                    near(tt(m[s], m[s], xn2[s], ALU.add))

            def feed_forward(g):
                ch.settle()
                for s in range(2):
                    tt(ff_rest[:, s, :], m[s], nbuf(s, 0, D), ALU.add).then_inc(sg["hs_ok"], 1)
                for s in range(2):
                    need(v, "P6", "mm_b", 2 * g + s + 1)
                    need(v, "P6", "xn_ok", 2 * g + s + 1)
                    near(tt(u[s], psT[s][:, D:2 * D], row("b_ff2"), ALU.add))
                for s in range(2):
                    near(tt(u[s], u[s], z[s], ALU.add), True)
                stats(3200, "P6", "var2_ok", FF_COLS)

            def finish(g):
                for s in range(2):
                    need(v, "P6", "rstd2_ok", 2 * g + s + 1)
                    near(normal(s, 3200, 3200, None, FF_COLS))
                for s in range(2):
                    near(tt(u[s], u[s], row("g2"), ALU.mult))
                for s in range(2):
                    near(tt(u[s], u[s], row("b2"), ALU.add))
                for s in range(2):
                    need(v, "P6", "hs_ok", 2 * g + s + 1)
                    stored(v, "P6", "a", s, g)
                    second(s)
                    tt(x3[s], u[s], ff_rest[:, s, :], ALU.add).then_inc(sg["res_ok"], 1)
                need(v, "P6", "res_ok", 2 * g + 2)
                if not isinstance(g, int):
                    v.nop(nofuse=True)
                stats(3584, "P6", "v_ok", FF_COLS)
                for s in range(2):
                    need(v, "P6", "rstd3_ok", 2 * g + s + 1)
                    stored(v, "P6", "b", s, g)
                    normal(s, 3584, 3840, "dots_ok", FF_COLS)

            def body(g, first_pair=False):
                attention(g)
                if not first_pair:
                    finish(g - 1)
                feed_forward(g)
            body(0, True)
            ch.groups(NG, body, start=1)
            finish(NG - 1)
            phase_end(v, 9)

            def shift(g):
                for s in range(2):
                    need(v, "P7", "mm_a", 2 * g + s + 1)
                    lg = nbuf(s, 4150, EX)
                    link(tt(lg, psT[s][:, D:D + EX], col("moe_br", 0, EX), ALU.add))
                    link(red(nbuf(s, 4137, 1), lg, AX.X, ALU.max))
                    ts(lg, lg, nbuf(s, 4137, 1), None, ALU.subtract).then_inc(sg["q_max"], 1)

            def probabilities(g):
                for s in range(2):
                    wait(v, lo_ok, g * 2 * EX - 1 + s)
                    need(v, "P7", "q_exp", 2 * g + s + 1)
                    link(nc.vector.reciprocal(nbuf(s, 4141, 1), nbuf(s, 4140, 1)))
                    ts(nbuf(s, 4120, EX), nbuf(s, 4128, EX), nbuf(s, 4141, 1), None,
                       ALU.mult).then_inc(sg["sum_ok"], 1)

            def body(g, last_pair=False):
                for s in range(2):
                    t = 2 * g + s
                    landed(v, "P7", s, g)
                    need(v, "P7", "mm_b", t + 1)
                    tt(nbuf(s, 1536, D), psA[s][:, 0:D], nbuf(s, 0, D), ALU.add).then_inc(sg["ev_a"], 1)
                for e in range(EX):
                    if e == EX - 1 and not last_pair:
                        shift(g + 1)
                    for s in range(2):
                        n = g * 2 * EX + e * 2 + s
                        wait(v, lo_ps, n + 1)
                        if e == 0:
                            need(v, "P7", "ev_a", 2 * g + s + 1)
                        else:
                            v.wait_ge(lo_ok, n - 1)
                        dst = 1536
                        if e == EX - 1:
                            stored(v, "P7", "a", s, g)
                            dst = 1792
                        stt(nbuf(s, dst, D), psA[s][:, 0:D], nbuf(s, 4120 + e, 1), nbuf(s, 1536, D),
                            ALU.mult, ALU.add).then_inc(lo_ok, 1)
                if not last_pair:
                    probabilities(g + 1)
            shift(0)
            probabilities(0)
            ch.groups(NG - 1, body)
            body(NG - 1, True)


def kernel(**inputs):
    import concourse.bacc as bacc
    from concourse.bass_utils import run_bass_kernel_spmd

    x = {k: np.asarray(v) for k, v in inputs.items()}

    def fold_rows(w):
        k = w.shape[0] // P
        return w.reshape(k, P, w.shape[1]).transpose(1, 0, 2).reshape(P, k * w.shape[1])

    def columns(v):
        return v.reshape(-1, P).T

    def every(v):
        return np.broadcast_to(v.reshape(1, -1), (P, v.size))

    def experts(w):
        return w.reshape(EX, KD, P, D).transpose(2, 0, 1, 3).reshape(P, EX * KD * D)

    src = np.concatenate([x["src"], np.zeros(C * EC - E, np.int32)])
    dst = np.concatenate([x["dst"], np.full(CR * P - E, N, np.int32)])
    none = np.full(1, -1, np.int32)
    prev, nxt = np.concatenate([none, dst[:-1]]), np.concatenate([dst[1:], none])
    ew = np.concatenate([x["edge_weight"], np.zeros(CR * P - E, np.float32)])
    over = np.full((CT * P, P), N, np.int32)
    over[:C, 1:] = dst[:C * EC].reshape(C, EC)
    over[:C, 0] = prev[:C * EC:EC]
    f = "L1_ffn_"
    parts = {"ffn_b1": columns(x["L0_ffn_b1"]), "b_ff1": columns(x["L1_gnn_b_ff1"]),
             "g_pre": columns(x["L1_mix_g_pre"]), "bq": columns(x["L1_gnn_bq"]),
             "ffn_br": every(x["L0_ffn_br"]), "we": every(x["L1_gnn_we"]), "be": every(x["L1_gnn_be"]),
             "moe_br": every(x[f + "br"]), "mem_k": x["L1_mix_mem_kv"][0].reshape(HID, MEM)}
    for n in ("b1", "g1", "be1", "m1", "v1", "b2", "g2", "be2", "m2", "v2"):
        parts[n] = columns(x[f + n].reshape(-1))
    rowv = {"bout": "L0_mix_bout", "wr": "L0_ffn_wr", "ffn_b2": "L0_ffn_b2", "bs": "L1_gnn_bs", "bv": "L1_gnn_bv",
            "g1": "L1_gnn_g1", "b1": "L1_gnn_b1", "g2": "L1_gnn_g2", "b2": "L1_gnn_b2",
            "b_ff2": "L1_gnn_b_ff2", "b_out": "L1_mix_b_out", "g_out": "L1_mix_g_out"}
    arrays = {
        "x": np.concatenate([x["x"], np.zeros((NP - N, D), np.float32)]),
        "src_c": np.concatenate([np.zeros((1, C), np.int32), src.reshape(C, EC).T]),
        "dst_r": dst.reshape(P, CR), "dprev_r": prev.reshape(P, CR), "dnext_r": nxt.reshape(P, CR),
        "dst_ov": over.reshape(CT, P, P).transpose(1, 0, 2).reshape(P, CT * P), "first": every(over[:C, 1]),
        "ew_r": ew.reshape(P, CR),
        "rows": np.concatenate([every(x[rowv[n]]) for n in ROWS], 1),
        "cols": np.concatenate([parts[n] for n in COLS], 1),
        "W_neigh": fold_rows(x["L0_gnn_W_neigh"]), "W_self": fold_rows(x["L0_gnn_W_self"]),
        "Wkv": fold_rows(x["L0_mix_Wqkv"][INNER:].T), "Wq": fold_rows(x["L0_mix_Wqkv"][:INNER]),
        "WoutT": fold_rows(x["L0_mix_Wout"].T), "w1": fold_rows(x["L0_ffn_w1"]), "w2": fold_rows(x["L0_ffn_w2"]),
        "wqT": fold_rows(x["L1_gnn_wq"].T),
        "wkTb": fold_rows(np.concatenate([x["L1_gnn_wk"].T, x["L1_gnn_bk"].reshape(D, 1)], 1)),
        "w_qkv": fold_rows(x["L1_mix_w_qkv"]), "w_out": x["L1_mix_w_out"],
        "wv": fold_rows(x["L1_gnn_wv"]), "ws": fold_rows(x["L1_gnn_ws"]),
        "w_ff1": fold_rows(x["L1_gnn_w_ff1"]), "w_ff2": fold_rows(x["L1_gnn_w_ff2"]),
        "Wr": fold_rows(x[f + "Wr"]), "bo": x[f + "bo"],
        "mem_v": x["L1_mix_mem_kv"][1].reshape(HID, MEM).T,
        "W1": experts(x[f + "W1"]), "W2": experts(x[f + "W2"]), "Wo": experts(x[f + "Wo"]),
    }
    arrays = {"in_" + k: np.ascontiguousarray(v) for k, v in arrays.items()}
    nc = bacc.Bacc("TRN2", target_bir_lowering=False, num_devices=1)
    aps = {k[3:]: nc.dram_tensor(k, v.shape, mybir.dt.from_np(v.dtype), kind="ExternalInput").ap()
           for k, v in arrays.items()}
    out = nc.dram_tensor("out_0", (N, D), F32, kind="ExternalOutput").ap()
    build(nc, aps, out)
    r = run_bass_kernel_spmd(nc, [arrays], core_ids=[0])
    return r.results[0]["out_0"]
```
